# Optimizing a Trainium2 kernel written in Bass

```python
import numpy as np
import jax
import jax.numpy as jnp

def _softmax(x, axis=-1):
    return jax.nn.softmax(x, axis=axis)

def _gelu(x):
    return jax.nn.gelu(x, approximate=True)

def _silu(x):
    return jax.nn.silu(x)

def _sigmoid(x):
    return jax.nn.sigmoid(x)

def _layernorm(x, axis=-1, eps=1e-05):
    m = jnp.mean(x, axis=axis, keepdims=True)
    v = jnp.var(x, axis=axis, keepdims=True)
    return (x - m) / jnp.sqrt(v + eps)

def _scatter_add(tgt, idx, src, axis=0):
    return tgt.at[idx].add(src)

def _segment_sum(src, seg, n):
    return jax.ops.segment_sum(src, seg, n)
kernel_name = 'mk_gnn_resnorm_d4_gnn_r8_24d7ff'

def setup_inputs(seed: int=0):
    np.random.seed(seed)
    _w = jnp.asarray

    def _rec_inputs():
        import jax
        import jax.numpy as jnp
        _gk = jax.random.key(seed)
        x = -0.0005207 + 1.001 * jax.random.normal(jax.random.fold_in(_gk, 1), (512, 512), jnp.float32)
        src = jax.random.randint(jax.random.fold_in(_gk, 2), (16384,), 0, 512, jnp.int32)
        dst = jnp.minimum((512 * jax.random.uniform(jax.random.fold_in(_gk, 3), (16384,)) ** 2.0).astype(jnp.int32), 4095)
        _o = jnp.argsort(dst, stable=True)
        src = src[_o]
        dst = dst[_o]
        edge_attr_4 = 0.00171547 + 0.999346 * jax.random.normal(jax.random.fold_in(_gk, 11), (16384, 4), jnp.float32)
        edge_attr_8 = 0.000126197 + 0.999763 * jax.random.normal(jax.random.fold_in(_gk, 12), (16384, 8), jnp.float32)
        return (x, src, dst, edge_attr_4, edge_attr_8)
    x, src, dst, edge_attr_4, edge_attr_8 = _rec_inputs()

    def _L0_gnn_setup():
        import jax, jax.numpy as jnp
        import numpy as np
        N = 512
        E = 16384
        IN_F = 512
        OUT_F = 64
        H = 8
        SLOPE = 0.2
        key = jax.random.key(seed)
        k1, k2, k3, k4 = jax.random.split(key, 4)
        x = jax.random.normal(k1, (N, IN_F), dtype=jnp.float32)
        edge_index = jax.random.randint(k2, (2, E), 0, N, dtype=jnp.int64)
        W = jax.random.normal(k3, (H, OUT_F, IN_F), dtype=jnp.float32) * (1.0 / np.sqrt(IN_F))
        a = jax.random.normal(k4, (H, 2 * OUT_F), dtype=jnp.float32) * (1.0 / np.sqrt(2 * OUT_F))
        return {'x': x, 'edge_index': edge_index, 'W': W, 'a': a}
    _L0_gnn_all = _L0_gnn_setup()
    _L0_gnn_in = {k: v for k, v in _L0_gnn_all.items() if k in ('W', 'a')}
    del _L0_gnn_all

    def _L1_gnn_setup():
        import jax, jax.numpy as jnp
        import numpy as np
        N, IN_DIM, OUT_DIM, H = (1024, 512, 512, 4)
        E = 16384
        HC = H * OUT_DIM
        key = jax.random.key(seed)
        ks = jax.random.split(key, 12)
        s = 1.0 / np.sqrt(IN_DIM)
        return {'x': jax.random.normal(ks[0], (N, IN_DIM), dtype=jnp.float32), 'edge_index': jax.random.randint(ks[1], (2, E), 0, N, dtype=jnp.int64), 'Wq': jax.random.normal(ks[2], (IN_DIM, HC), dtype=jnp.float32) * s, 'bq': jnp.zeros((HC,), dtype=jnp.float32), 'Wk': jax.random.normal(ks[3], (IN_DIM, HC), dtype=jnp.float32) * s, 'bk': jnp.zeros((HC,), dtype=jnp.float32), 'Wv': jax.random.normal(ks[4], (IN_DIM, HC), dtype=jnp.float32) * s, 'bv': jnp.zeros((HC,), dtype=jnp.float32), 'Wskip': jax.random.normal(ks[5], (IN_DIM, HC), dtype=jnp.float32) * s, 'bskip': jnp.zeros((HC,), dtype=jnp.float32), 'Wlin': jax.random.normal(ks[6], (HC, OUT_DIM), dtype=jnp.float32) / np.sqrt(HC), 'blin': jnp.zeros((OUT_DIM,), dtype=jnp.float32), 'gamma': jnp.ones((OUT_DIM,), dtype=jnp.float32), 'beta': jnp.zeros((OUT_DIM,), dtype=jnp.float32)}
    _L1_gnn_all = _L1_gnn_setup()
    _L1_gnn_in = {k: v for k, v in _L1_gnn_all.items() if k in ('Wq', 'bq', 'Wk', 'bk', 'Wv', 'bv', 'Wskip', 'bskip', 'Wlin', 'blin', 'gamma', 'beta')}
    del _L1_gnn_all

    def _L2_gnn_setup():
        import jax, jax.numpy as jnp
        import numpy as np
        MUL = 128
        N_NODES = 1250
        N_EDGES = 20000
        R_BASIS = 8
        HIDDEN = 64
        W_NUMEL = 4 * MUL
        SQRT3 = 3.0 ** 0.5
        SILU_2MOM = 1.679177
        AVG_NUM_NEIGHBORS = 10.0

        def _lin_irreps(x0, x1, W0, W1):
            y0 = x0 @ W0 / jnp.sqrt(jnp.float32(W0.shape[0]))
            y1 = jnp.einsum('num,uv->nvm', x1, W1) / jnp.sqrt(jnp.float32(W1.shape[0]))
            return (y0, y1)

        def _forward(node_feats, edge_attrs, edge_feats, edge_index, W_up0, W_up1, W_mlp1, W_mlp2, W_mlp3, W_mlp4, W_out0, W_out1):
            num_nodes = node_feats.shape[0]
            sender, receiver = (edge_index[0], edge_index[1])
            x0 = node_feats[:, :MUL]
            x1 = node_feats[:, MUL:].reshape(num_nodes, MUL, 3)
            x0, x1 = _lin_irreps(x0, x1, W_up0, W_up1)
            h = edge_feats
            for W in (W_mlp1, W_mlp2, W_mlp3):
                h = SILU_2MOM * jax.nn.silu(h @ W / jnp.sqrt(jnp.float32(W.shape[0])))
            tpw = h @ W_mlp4 / jnp.sqrt(jnp.float32(W_mlp4.shape[0]))
            w1, w2, w3, w4 = jnp.split(tpw, 4, axis=-1)
            s0 = x0[sender]
            s1 = x1[sender]
            y0 = edge_attrs[:, 0:1]
            y1 = edge_attrs[:, 1:4]
            p1 = w1 * s0 * y0
            p2 = (w2 * s0)[:, :, None] * y1[:, None, :]
            p3 = w3[:, :, None] * s1 * y0[:, None, :]
            p4 = w4 * jnp.einsum('eum,em->eu', s1, y1) / SQRT3
            m0 = jnp.concatenate([p1, p4], axis=-1)
            m1 = jnp.concatenate([p2, p3], axis=1)
            msg0 = jax.ops.segment_sum(m0, receiver, num_segments=num_nodes)
            msg1 = jax.ops.segment_sum(m1, receiver, num_segments=num_nodes)
            o0, o1 = _lin_irreps(msg0, msg1, W_out0, W_out1)
            out = jnp.concatenate([o0, o1.reshape(num_nodes, 3 * MUL)], axis=-1)
            return out / AVG_NUM_NEIGHBORS
        key = jax.random.key(seed)
        ks = jax.random.split(key, 12)
        rn = lambda k, s: jax.random.normal(k, s, dtype=jnp.float32)
        return {'node_feats': rn(ks[0], (N_NODES, 4 * MUL)), 'edge_attrs': rn(ks[1], (N_EDGES, 4)), 'edge_feats': rn(ks[2], (N_EDGES, R_BASIS)), 'edge_index': jax.random.randint(ks[3], (2, N_EDGES), 0, N_NODES), 'W_up0': rn(ks[4], (MUL, MUL)), 'W_up1': rn(ks[5], (MUL, MUL)), 'W_mlp1': rn(ks[6], (R_BASIS, HIDDEN)), 'W_mlp2': rn(ks[7], (HIDDEN, HIDDEN)), 'W_mlp3': rn(ks[8], (HIDDEN, HIDDEN)), 'W_mlp4': rn(ks[9], (HIDDEN, W_NUMEL)), 'W_out0': rn(ks[10], (2 * MUL, MUL)), 'W_out1': rn(ks[11], (2 * MUL, MUL))}
    _L2_gnn_all = _L2_gnn_setup()
    _L2_gnn_in = {k: v for k, v in _L2_gnn_all.items() if k in ('W_up0', 'W_up1', 'W_mlp1', 'W_mlp2', 'W_mlp3', 'W_mlp4', 'W_out0', 'W_out1')}
    del _L2_gnn_all

    def _L3_gnn_setup():
        import jax, jax.numpy as jnp
        import numpy as np
        N_NODES = 1250
        N_EDGES = 20000
        IN_DIM = 512
        HID = 256
        HEADS = 4
        OUT_DIM = 512
        NEG_SLOPE = 0.2

        def _glorot(key, shape):
            fan_in, fan_out = (shape[0], shape[-1])
            lim = jnp.sqrt(6.0 / (fan_in + fan_out))
            return jax.random.uniform(key, shape, jnp.float32, -lim, lim)

        def gat_conv(x, src, dst, W, att_src, att_dst, bias):
            N = x.shape[0]
            h = (x @ W).reshape(N, HEADS, HID)
            a_src = jnp.sum(h * att_src, axis=-1)
            a_dst = jnp.sum(h * att_dst, axis=-1)
            e = jax.nn.leaky_relu(a_src[src] + a_dst[dst], NEG_SLOPE)
            m = jax.ops.segment_max(e, dst, num_segments=N)
            e = jnp.exp(e - m[dst])
            s = jax.ops.segment_sum(e, dst, num_segments=N)
            alpha = e / (s[dst] + 1e-16)
            msg = alpha[:, :, None] * h[src]
            out = jax.ops.segment_sum(msg, dst, num_segments=N)
            return out.reshape(N, HEADS * HID) + bias
        key = jax.random.key(seed)
        ks = jax.random.split(key, 16)
        x = jax.random.normal(ks[0], (N_NODES, IN_DIM), jnp.float32)
        edge_index = jax.random.randint(ks[1], (2, N_EDGES), 0, N_NODES, jnp.int64)
        W1 = _glorot(ks[2], (IN_DIM, HEADS * HID))
        att_src1 = _glorot(ks[3], (HEADS, HID))
        att_dst1 = _glorot(ks[4], (HEADS, HID))
        b1 = jnp.zeros((HEADS * HID,), jnp.float32)
        W2 = _glorot(ks[5], (HEADS * HID, HEADS * HID))
        att_src2 = _glorot(ks[6], (HEADS, HID))
        att_dst2 = _glorot(ks[7], (HEADS, HID))
        b2 = jnp.zeros((HEADS * HID,), jnp.float32)
        fcW = _glorot(ks[8], (HEADS * HID, OUT_DIM))
        fcb = jnp.zeros((OUT_DIM,), jnp.float32)
        return dict(x=x, edge_index=edge_index, W1=W1, att_src1=att_src1, att_dst1=att_dst1, b1=b1, W2=W2, att_src2=att_src2, att_dst2=att_dst2, b2=b2, fcW=fcW, fcb=fcb)
    _L3_gnn_all = _L3_gnn_setup()
    _L3_gnn_in = {k: v for k, v in _L3_gnn_all.items() if k in ('W1', 'att_src1', 'att_dst1', 'b1', 'W2', 'att_src2', 'att_dst2', 'b2', 'fcW', 'fcb')}
    del _L3_gnn_all
    return {'x': x, 'src': src, 'dst': dst, 'edge_attr_4': edge_attr_4, 'edge_attr_8': edge_attr_8, 'L0_gnn_W': _L0_gnn_in['W'], 'L0_gnn_a': _L0_gnn_in['a'], 'L1_gnn_Wq': _L1_gnn_in['Wq'], 'L1_gnn_bq': _L1_gnn_in['bq'], 'L1_gnn_Wk': _L1_gnn_in['Wk'], 'L1_gnn_bk': _L1_gnn_in['bk'], 'L1_gnn_Wv': _L1_gnn_in['Wv'], 'L1_gnn_bv': _L1_gnn_in['bv'], 'L1_gnn_Wskip': _L1_gnn_in['Wskip'], 'L1_gnn_bskip': _L1_gnn_in['bskip'], 'L1_gnn_Wlin': _L1_gnn_in['Wlin'], 'L1_gnn_blin': _L1_gnn_in['blin'], 'L1_gnn_gamma': _L1_gnn_in['gamma'], 'L1_gnn_beta': _L1_gnn_in['beta'], 'L2_gnn_W_up0': _L2_gnn_in['W_up0'], 'L2_gnn_W_up1': _L2_gnn_in['W_up1'], 'L2_gnn_W_mlp1': _L2_gnn_in['W_mlp1'], 'L2_gnn_W_mlp2': _L2_gnn_in['W_mlp2'], 'L2_gnn_W_mlp3': _L2_gnn_in['W_mlp3'], 'L2_gnn_W_mlp4': _L2_gnn_in['W_mlp4'], 'L2_gnn_W_out0': _L2_gnn_in['W_out0'], 'L2_gnn_W_out1': _L2_gnn_in['W_out1'], 'L3_gnn_W1': _L3_gnn_in['W1'], 'L3_gnn_att_src1': _L3_gnn_in['att_src1'], 'L3_gnn_att_dst1': _L3_gnn_in['att_dst1'], 'L3_gnn_b1': _L3_gnn_in['b1'], 'L3_gnn_W2': _L3_gnn_in['W2'], 'L3_gnn_att_src2': _L3_gnn_in['att_src2'], 'L3_gnn_att_dst2': _L3_gnn_in['att_dst2'], 'L3_gnn_b2': _L3_gnn_in['b2'], 'L3_gnn_fcW': _L3_gnn_in['fcW'], 'L3_gnn_fcb': _L3_gnn_in['fcb']}

def reference(x, src, dst, edge_attr_4, edge_attr_8, L0_gnn_W, L0_gnn_a, L1_gnn_Wq, L1_gnn_bq, L1_gnn_Wk, L1_gnn_bk, L1_gnn_Wv, L1_gnn_bv, L1_gnn_Wskip, L1_gnn_bskip, L1_gnn_Wlin, L1_gnn_blin, L1_gnn_gamma, L1_gnn_beta, L2_gnn_W_up0, L2_gnn_W_up1, L2_gnn_W_mlp1, L2_gnn_W_mlp2, L2_gnn_W_mlp3, L2_gnn_W_mlp4, L2_gnn_W_out0, L2_gnn_W_out1, L3_gnn_W1, L3_gnn_att_src1, L3_gnn_att_dst1, L3_gnn_b1, L3_gnn_W2, L3_gnn_att_src2, L3_gnn_att_dst2, L3_gnn_b2, L3_gnn_fcW, L3_gnn_fcb):
    import jax
    import jax.numpy as jnp

    def _L0_gnn_ref(x, edge_index, W, a):
        import jax, jax.numpy as jnp
        import numpy as np
        N = 512
        E = 16384
        IN_F = 512
        OUT_F = 64
        H = 8
        SLOPE = 0.2
        n = x.shape[0]
        src, dst = (edge_index[0], edge_index[1])
        mask = jnp.zeros((n, n), dtype=bool).at[src, dst].set(True)
        xh = jnp.einsum('hoi,ni->hno', W, x)
        a1 = a[:, :OUT_F]
        a2 = a[:, OUT_F:]
        s_j = jnp.einsum('hno,ho->hn', xh, a1)
        s_i = jnp.einsum('hno,ho->hn', xh, a2)
        e = jnp.where(mask[None, :, :], s_i[:, :, None] + s_j[:, None, :], 0.0)
        att = jax.nn.softmax(jnp.where(e >= 0, e, SLOPE * e), axis=2)
        out_h = jnp.einsum('hij,hjo->hio', att, xh)
        return out_h.transpose(1, 0, 2).reshape(n, H * OUT_F)

    def _L1_gnn_ref(x, edge_index, Wq, bq, Wk, bk, Wv, bv, Wskip, bskip, Wlin, blin, gamma, beta):
        import jax, jax.numpy as jnp
        import numpy as np
        N, IN_DIM, OUT_DIM, H = (1024, 512, 512, 4)
        E = 16384
        HC = H * OUT_DIM
        n = x.shape[0]
        src, dst = (edge_index[0], edge_index[1])
        q = (x @ Wq + bq).reshape(n, H, OUT_DIM)
        k = (x @ Wk + bk).reshape(n, H, OUT_DIM)
        v = (x @ Wv + bv).reshape(n, H, OUT_DIM)
        alpha = jnp.einsum('ehc,ehc->eh', q[dst], k[src]) / np.sqrt(OUT_DIM)
        amax = jax.ops.segment_max(alpha, dst, num_segments=n)
        ex = jnp.exp(alpha - amax[dst])
        denom = jax.ops.segment_sum(ex, dst, num_segments=n)
        attn = ex / denom[dst]
        msg = attn[:, :, None] * v[src]
        agg = jax.ops.segment_sum(msg, dst, num_segments=n).reshape(n, HC)
        x_attn = agg + x @ Wskip + bskip
        x_lin = x_attn @ Wlin + blin
        h = x_lin + x_attn[:, :OUT_DIM]
        mu = jnp.mean(h, axis=-1, keepdims=True)
        var = jnp.mean((h - mu) ** 2, axis=-1, keepdims=True)
        return gamma * (h - mu) / jnp.sqrt(var + 1e-05) + beta

    def _L2_gnn_ref(node_feats, edge_attrs, edge_feats, edge_index, W_up0, W_up1, W_mlp1, W_mlp2, W_mlp3, W_mlp4, W_out0, W_out1):
        import jax, jax.numpy as jnp
        import numpy as np
        MUL = 128
        N_NODES = 1250
        N_EDGES = 20000
        R_BASIS = 8
        HIDDEN = 64
        W_NUMEL = 4 * MUL
        SQRT3 = 3.0 ** 0.5
        SILU_2MOM = 1.679177
        AVG_NUM_NEIGHBORS = 10.0

        def _lin_irreps(x0, x1, W0, W1):
            y0 = x0 @ W0 / jnp.sqrt(jnp.float32(W0.shape[0]))
            y1 = jnp.einsum('num,uv->nvm', x1, W1) / jnp.sqrt(jnp.float32(W1.shape[0]))
            return (y0, y1)

        def _forward(node_feats, edge_attrs, edge_feats, edge_index, W_up0, W_up1, W_mlp1, W_mlp2, W_mlp3, W_mlp4, W_out0, W_out1):
            num_nodes = node_feats.shape[0]
            sender, receiver = (edge_index[0], edge_index[1])
            x0 = node_feats[:, :MUL]
            x1 = node_feats[:, MUL:].reshape(num_nodes, MUL, 3)
            x0, x1 = _lin_irreps(x0, x1, W_up0, W_up1)
            h = edge_feats
            for W in (W_mlp1, W_mlp2, W_mlp3):
                h = SILU_2MOM * jax.nn.silu(h @ W / jnp.sqrt(jnp.float32(W.shape[0])))
            tpw = h @ W_mlp4 / jnp.sqrt(jnp.float32(W_mlp4.shape[0]))
            w1, w2, w3, w4 = jnp.split(tpw, 4, axis=-1)
            s0 = x0[sender]
            s1 = x1[sender]
            y0 = edge_attrs[:, 0:1]
            y1 = edge_attrs[:, 1:4]
            p1 = w1 * s0 * y0
            p2 = (w2 * s0)[:, :, None] * y1[:, None, :]
            p3 = w3[:, :, None] * s1 * y0[:, None, :]
            p4 = w4 * jnp.einsum('eum,em->eu', s1, y1) / SQRT3
            m0 = jnp.concatenate([p1, p4], axis=-1)
            m1 = jnp.concatenate([p2, p3], axis=1)
            msg0 = jax.ops.segment_sum(m0, receiver, num_segments=num_nodes)
            msg1 = jax.ops.segment_sum(m1, receiver, num_segments=num_nodes)
            o0, o1 = _lin_irreps(msg0, msg1, W_out0, W_out1)
            out = jnp.concatenate([o0, o1.reshape(num_nodes, 3 * MUL)], axis=-1)
            return out / AVG_NUM_NEIGHBORS
        return _forward(node_feats, edge_attrs, edge_feats, edge_index, W_up0, W_up1, W_mlp1, W_mlp2, W_mlp3, W_mlp4, W_out0, W_out1)

    def _L3_gnn_ref(x, edge_index, W1, att_src1, att_dst1, b1, W2, att_src2, att_dst2, b2, fcW, fcb):
        import jax, jax.numpy as jnp
        import numpy as np
        N_NODES = 1250
        N_EDGES = 20000
        IN_DIM = 512
        HID = 256
        HEADS = 4
        OUT_DIM = 512
        NEG_SLOPE = 0.2

        def _glorot(key, shape):
            fan_in, fan_out = (shape[0], shape[-1])
            lim = jnp.sqrt(6.0 / (fan_in + fan_out))
            return jax.random.uniform(key, shape, jnp.float32, -lim, lim)

        def gat_conv(x, src, dst, W, att_src, att_dst, bias):
            N = x.shape[0]
            h = (x @ W).reshape(N, HEADS, HID)
            a_src = jnp.sum(h * att_src, axis=-1)
            a_dst = jnp.sum(h * att_dst, axis=-1)
            e = jax.nn.leaky_relu(a_src[src] + a_dst[dst], NEG_SLOPE)
            m = jax.ops.segment_max(e, dst, num_segments=N)
            e = jnp.exp(e - m[dst])
            s = jax.ops.segment_sum(e, dst, num_segments=N)
            alpha = e / (s[dst] + 1e-16)
            msg = alpha[:, :, None] * h[src]
            out = jax.ops.segment_sum(msg, dst, num_segments=N)
            return out.reshape(N, HEADS * HID) + bias
        N = x.shape[0]
        loops = jnp.arange(N, dtype=edge_index.dtype)
        src = jnp.concatenate([edge_index[0], loops])
        dst = jnp.concatenate([edge_index[1], loops])
        h = gat_conv(x, src, dst, W1, att_src1, att_dst1, b1)
        h = jax.nn.relu(h)
        h = gat_conv(h, src, dst, W2, att_src2, att_dst2, b2)
        h = jax.nn.relu(h)
        return h @ fcW + fcb
    edge_index = jnp.stack([src, dst])
    x = _layernorm(x + _L0_gnn_ref(x, edge_index, L0_gnn_W, L0_gnn_a), axis=-1)
    x = _layernorm(x + _L1_gnn_ref(x, edge_index, L1_gnn_Wq, L1_gnn_bq, L1_gnn_Wk, L1_gnn_bk, L1_gnn_Wv, L1_gnn_bv, L1_gnn_Wskip, L1_gnn_bskip, L1_gnn_Wlin, L1_gnn_blin, L1_gnn_gamma, L1_gnn_beta), axis=-1)
    x = _layernorm(x + _L2_gnn_ref(x, edge_attr_4, edge_attr_8, edge_index, L2_gnn_W_up0, L2_gnn_W_up1, L2_gnn_W_mlp1, L2_gnn_W_mlp2, L2_gnn_W_mlp3, L2_gnn_W_mlp4, L2_gnn_W_out0, L2_gnn_W_out1), axis=-1)
    x = _layernorm(x + _L3_gnn_ref(x, edge_index, L3_gnn_W1, L3_gnn_att_src1, L3_gnn_att_dst1, L3_gnn_b1, L3_gnn_W2, L3_gnn_att_src2, L3_gnn_att_dst2, L3_gnn_b2, L3_gnn_fcW, L3_gnn_fcb), axis=-1)
    return x

_drawn_inputs = setup_inputs


def setup_inputs(seed=0):
    import zlib

    import numpy as np

    out = dict(_drawn_inputs(seed))
    spreads = {'L1_gnn_bq': (0.0, 0.432),
     'L1_gnn_bk': (0.0, 2.0),
     'L1_gnn_bv': (0.0, 0.1),
     'L1_gnn_bskip': (0.0, 0.1),
     'L1_gnn_blin': (0.0, 0.1),
     'L1_gnn_gamma': (1.0, 0.2),
     'L1_gnn_beta': (0.0, 0.1),
     'L3_gnn_b1': (0.0, 0.1),
     'L3_gnn_b2': (0.0, 0.1),
     'L3_gnn_fcb': (0.0, 0.1)}
    factors = {'L0_gnn_a': 2.739,
     'L3_gnn_att_dst1': 8.0,
     'L3_gnn_att_src2': 8.0,
     'L3_gnn_att_dst2': 91.262}
    for name, (base, spread) in spreads.items():
        noise = np.random.default_rng([zlib.crc32(name.encode()), seed]).standard_normal(out[name].shape)
        drawn = base * np.exp(spread * noise) if base else spread * noise
        out[name] = jnp.asarray(drawn.astype(out[name].dtype))
    for name, factor in factors.items():
        out[name] = (out[name] * factor).astype(out[name].dtype)
    return out
```

```python
from contextlib import ExitStack

import concourse.bass as bass
from concourse import mybir

F32 = mybir.dt.float32
BF16 = mybir.dt.bfloat16
F16 = mybir.dt.float16
I32 = mybir.dt.int32
U32 = mybir.dt.uint32
ALU = mybir.AluOpType
ACT = mybir.ActivationFunctionType
AX = mybir.AxisListType

P = 128
N = 512
D = 512
E = 16384
NB = N // P
KB = D // P
ET = E // P
UNIT = 4 * P
NU = E // UNIT + NB - 1
REC = 16
NEG = -1.0e30
EPS = 1e-5
H0, F0 = 8, 64
H1 = 4
H3, F3 = 4, 256
W3 = H3 * F3
MUL = 128
HID = 64
SILU_2MOM = 1.679177


class Steps:

    def __init__(self, eng, sem, turn=0, per_turn=0):
        self.eng, self.sem, self.base, self.n, self.per_turn = eng, sem, turn * per_turn, 0, per_turn

    def link(self, instruction):
        self.mark(instruction)
        self.wait()

    def mark(self, instruction):
        instruction.then_inc(self.sem, 1)
        self.n += 1

    def wait(self):
        self.eng.wait_ge(self.sem, self.base + self.n)

    def done(self):
        assert self.n == self.per_turn, self.n


def graph_kernel(nc, x, src, dst, ea, ef, w0, a0, wq, bq, wk, bk, wv, bv, wskip, bskip, wlin, blin, gamma, beta,
                 wup0, wup1, wm1, wm2, wm3, wm4, wout0, wout1, w31, asrc1, adst1, b31, w32, asrc2, adst2, b32,
                 fcw, fcb, out):
    ctx = ExitStack()
    with ctx:
        def sem(name):
            return ctx.enter_context(nc.semaphore(name))

        def sb(name, shape, dt=F32, where=ctx):
            return where.enter_context(nc.sbuf_tensor(name, shape, dt))

        ps = [ctx.enter_context(nc.psum_tensor(f"bank{b}", [P, 512], F32)) for b in range(8)]
        records = nc.dram_tensor("records", [(NU + 1) * UNIT, REC], F32)
        xup_dram = nc.dram_tensor("xup_dram", [N, 4 * MUL], F32)

        ident = sb("ident", [P, P])
        ones = sb("ones", [P, P])
        iota = sb("iota", [P, N])
        xs = sb("xs", [P, NB, D])
        xT = sb("xT", [P, KB, N])
        count = sb("count", [P, NB, N])
        nomask = sb("nomask", [P, NB, N])
        ln_stat = sb("ln_stat", [P, NB, 6])
        ln_mv = sb("ln_mv", [P, NB, 2])
        ln_std = sb("ln_std", [P, NB])
        ln_r = sb("ln_r", [P, NB])
        ubase = sb("ubase", [P, NU + 1], I32)
        s_w1 = {n: sem(f"s_load_{n}") for n in ("wq", "wk", "wv", "ws", "wl")}
        s_b1 = sem("s_load_bias1")
        s_gate_dve, s_gate_pool, s_gate_sp = sem("s_gate_dve"), sem("s_gate_pool"), sem("s_gate_sp")

        def psum4(b):
            return ps[b][:, :].rearrange("p (c n) -> p c n", c=4)

        def layernorm(dve, s, s_var, s_std, src_t, dst_t):
            for c in range(NB):
                s.mark(dve.bn_stats(ln_stat[:, c, :], src_t[:, c, :]))
            s.wait()
            for c in range(NB):
                s.mark(dve.bn_aggr(ln_mv[:, c, :], ln_stat[:, c, :]))
            s.wait()
            dve.tensor_scalar(ln_std[:, :], ln_mv[:, :, 1], EPS, None, ALU.add).then_inc(s_var, 1)
            dve.wait_ge(s_std, 1)
            s.link(dve.reciprocal(ln_r[:, :], ln_std[:, :]))
            for c in range(NB):
                s.mark(dve.tensor_scalar(dst_t[:, c, :], src_t[:, c, :], ln_mv[:, c, 0:1], ln_r[:, c:c + 1],
                                         ALU.subtract, ALU.mult))
            s.wait()

        def root(act, s_var, s_std):
            act.wait_ge(s_var, 1)
            act.activation(ln_std[:, :], ln_std[:, :], ACT.Sqrt).then_inc(s_std, 1)

        lay1 = ExitStack()
        wq_sb, wk_sb, wv_sb, ws_sb, wl_sb = (sb(n, [P, KB, D], F32, lay1) for n in ("wq_sb", "wk_sb", "wv_sb", "ws_sb", "wl_sb"))
        brow = sb("brow", [16, 3, P], F32, lay1)
        blin_row = sb("blin_row", [1, D], F32, lay1)
        gamma_b = sb("gamma_b", [P, D], F32, lay1)
        beta_b = sb("beta_b", [P, D], F32, lay1)

        def head_loads(q, h, which):
            for n, dram, t in (("wq", wq, wq_sb), ("wk", wk, wk_sb), ("wv", wv, wv_sb), ("ws", wskip, ws_sb)):
                if n in which:
                    q.dma_start(t[:, :, :], dram.rearrange("(k p) c -> p k c", p=P)[:, :, bass.ds(h * D, D)])\
                        .then_inc(s_w1[n], 16)
            if "wl" in which:
                q.dma_start(wl_sb[:, :, :], wlin[bass.ds(h * D, D), :].rearrange("(k p) c -> p k c", p=P))\
                    .then_inc(s_w1["wl"], 16)

        with ExitStack() as c0:
            def t0(name, shape, dt=F32):
                return sb(name, shape, dt, c0)

            iota_i = t0("iota_i", [P, N], I32)
            iota_h = t0("iota_h", [P, N], F16)
            tri = t0("tri", [P, P])
            fill = t0("fill", [P, (NU + 1) * UNIT // P, REC])
            dst_i, src_i, tmp_i = (t0(n, [P, ET], I32) for n in ("dst_i", "src_i", "tmp_i"))
            dst_f, src_f, blk_f, loc_f, pos_f = (t0(n, [P, ET]) for n in ("dst_f", "src_f", "blk_f", "loc_f", "pos_f"))
            pos_i = t0("pos_i", [P, ET], I32)
            mask_g = t0("mask_g", [P, NB, ET])
            scan_g = t0("scan_g", [P, NB, ET])
            tot = t0("tot", [P, NB])
            sc = t0("sc", [P, 6, NB])
            sc_i = t0("sc_i", [P, 2, NB], I32)
            ub_f = t0("ub_f", [P, NU + 1])
            ef_sb = t0("ef_sb", [P, ET, 8])
            ea_sb = t0("ea_sb", [P, ET, 4])
            rec = t0("rec", [P, ET, REC])
            rbuf = t0("rbuf", [P, 2, 4, REC])
            ibuf = t0("ibuf", [P, 2, 4], I32)
            zero_b = t0("zero_b", [P, N], BF16)
            ohd = t0("ohd", [P, 4, N], BF16)
            ohs = t0("ohs", [P, 4, N], BF16)
            w0_sb = t0("w0_sb", [P, KB, D])
            w0T = t0("w0T", [P, KB, D])
            xh = t0("xh", [P, NB, H0 * F0])
            a_b = t0("a_b", [P, 2, H0, F0])
            prod = t0("prod", [P, 2, H0 * F0])
            sij = t0("sij", [P, 2, NB, H0])
            maskT = t0("maskT", [P, NB, N])
            diag = t0("diag", [P, NB, P])
            tsum = t0("tsum", [P, 2, N])
            esc = t0("esc", [P, 2, N])
            lsc = t0("lsc", [P, 2, N])
            emx = t0("emx", [P, 2])
            nmx = t0("nmx", [P, 4])
            ex = t0("ex", [P, 2, N])
            rsum = t0("rsum", [P, 4])
            rinv = t0("rinv", [P, 4])
            exT = t0("exT", [P, 2, NB, P])
            y0 = t0("y0", [P, NB, D])

            s_idx, s_att, s_x, s_w0, s_a0, s_fill = (sem(n) for n in ("s_idx", "s_att", "s_x", "s_w0", "s_a0", "s_fill"))
            s_const, s_ident, s_iota, s_tot, s_off = (sem(n) for n in ("s_const", "s_ident", "s_iota", "s_tot", "s_off"))
            s_loc, s_pos, s_rec, s_cp = (sem(n) for n in ("s_loc", "s_pos", "s_rec", "s_cp"))
            s_sent = [sem(f"s_sent{b}") for b in range(2)]
            s_fillset, s_oh, s_ohfree, s_cnt, s_cs = (sem(n) for n in ("s_fillset", "s_oh", "s_ohfree", "s_cnt", "s_cs"))
            s_t0, s_t0c, s_xh, s_xhc, s_zero = (sem(n) for n in ("s_t0", "s_t0c", "s_xh", "s_xhc", "s_zero"))
            s_mT, s_mTc = sem("s_mT"), sem("s_mTc")
            s_v0, s_diag, s_sjb, s_ts, s_em, s_ex = (sem(n) for n in ("s_v0", "s_diag", "s_sjb", "s_ts", "s_em", "s_ex"))
            s_nm, s_xT, s_xTc, s_o, s_y, s_vl0 = (sem(n) for n in ("s_nm", "s_xT", "s_xTc", "s_o", "s_y", "s_vl0"))
            s_ln0, s_ln0r, s_lnx0, s_xT0, s_xT0c = (sem(n) for n in ("s_ln0", "s_ln0r", "s_lnx0", "s_xT0", "s_xT0c"))

            with nc.Block() as block:
                @block.sync
                def _(sp):
                    sp.dma_start(dst_i[:, :], dst.rearrange("(p t) -> p t", p=P)).then_inc(s_idx, 16)
                    sp.dma_start(src_i[:, :], src.rearrange("(p t) -> p t", p=P)).then_inc(s_idx, 16)
                    sp.dma_start(xs[:, :, :], x.rearrange("(c p) d -> p c d", p=P)).then_inc(s_x, 16)
                    sp.dma_start(w0_sb[:, :, :], w0.rearrange("h o i -> (h o) i").rearrange("(c p) i -> p c i", p=P))\
                        .then_inc(s_w0, 16)
                    for j in range(2):
                        sp.dma_start(a_b[:, j, :, :], a0[:, j * F0:(j + 1) * F0].partition_broadcast(P))\
                            .then_inc(s_a0, 16)
                    sp.dma_start(ef_sb[:, :, :], ef.rearrange("(p t) k -> p t k", p=P)).then_inc(s_att, 16)
                    sp.dma_start(ea_sb[:, :, :], ea.rearrange("(p t) k -> p t k", p=P)).then_inc(s_att, 16)
                    sp.wait_ge(s_fillset, 2)
                    sp.dma_start(records.ap().rearrange("(p r) k -> p r k", p=P), fill[:, :, :]).then_inc(s_fill, 16)
                    head_loads(sp, H1 - 1, ("wq", "wk", "wv", "ws", "wl"))
                    for j, b in enumerate((bq, bk, bskip)):
                        sp.dma_start(brow[:, j, :], b.rearrange("(c p) -> c p", p=P)).then_inc(s_b1, 16)
                    sp.dma_start(blin_row[:, :], blin.rearrange("(a c) -> a c", a=1)).then_inc(s_b1, 16)
                    sp.dma_start(gamma_b[:, :], gamma.partition_broadcast(P)).then_inc(s_b1, 16)
                    sp.dma_start(beta_b[:, :], beta.partition_broadcast(P)).then_inc(s_b1, 16)

                @block.gpsimd
                def _(pool):
                    pool.iota(iota_i[:, :], pattern=[[1, N]], base=0, channel_multiplier=0).then_inc(s_iota, 1)
                    pool.memset(ones[:, :], 1.0).then_inc(s_const, 1)
                    pool.memset(ident[:, :], 0.0).then_inc(s_const, 1)
                    pool.wait_ge(s_const, 2)
                    pool.affine_select(out=ident[:, :], in_=ident[:, :], compare_op=ALU.not_equal, fill=1.0, base=0,
                                       pattern=[[-1, P]], channel_multiplier=1).then_inc(s_ident, 1)
                    pool.affine_select(out=tri[:, :], in_=ones[:, :], compare_op=ALU.is_gt, fill=0.0, base=0,
                                       pattern=[[1, P]], channel_multiplier=-1).then_inc(s_ident, 1)
                    pool.memset(fill[:, :, :], 0.0).then_inc(s_fillset, 1)
                    pool.wait_ge(s_fillset, 1)
                    pool.memset(fill[:, :, 13:14], -1.0).then_inc(s_fillset, 1)
                    pool.memset(rec[:, :, 14:16], 0.0).then_inc(s_rec, 1)
                    pool.wait_ge(s_idx, 32)
                    pool.tensor_copy(rec[:, :, 12].bitcast(I32), src_i[:, :]).then_inc(s_rec, 1)
                    pool.wait_ge(s_att, 32)
                    pool.tensor_copy(rec[:, :, 0:8], ef_sb[:, :, :]).then_inc(s_rec, 1)
                    pool.tensor_copy(rec[:, :, 8:12], ea_sb[:, :, :]).then_inc(s_rec, 1)
                    pool.wait_ge(s_loc, 1)
                    pool.tensor_copy(rec[:, :, 13], loc_f[:, :]).then_inc(s_rec, 1)
                    pool.wait_ge(s_rec, 5)
                    pool.wait_ge(s_pos, 1)
                    pool.wait_ge(s_fill, 16)

                    def send(i, first):
                        for b in range(2):
                            if not first:
                                pool.wait_ge(s_sent[b], i * 64)
                            pool.tensor_copy(rbuf[:, b, :, :], rec[:, bass.ds(i * 8 + b * 4, 4), :]).then_inc(s_cp, 1)
                            pool.tensor_copy(ibuf[:, b, :], pos_i[:, bass.ds(i * 8 + b * 4, 4)]).then_inc(s_cp, 1)
                            pool.wait_ge(s_cp, i * 4 + b * 2 + 2)
                            pool.sem_inc(s_gate_pool, 1)
                            for k in range(4):
                                pool.indirect_dma_start(
                                    records.ap()[:, :],
                                    bass.IndirectOffsetOnAxis(ap=ibuf[:, b, k:k + 1], axis=0),
                                    rbuf[:, b, k, :], None).then_inc(s_sent[b], 16)

                    send(0, True)
                    with pool.Fori(1, ET // 8) as i:
                        send(i, False)
                    for b in range(2):
                        pool.wait_ge(s_sent[b], 64 * (ET // 8))

                def l0_out(pe, h, c):
                    pe.wait_ge(s_xTc, h * 4 + c + 3)
                    pe.wait_ge(s_y, h * 4 + c + 1)
                    for g in range(NB):
                        mm = pe.matmul(ps[4 + c % 2][:, 0:F0], exT[:, c % 2, g, :], xh[:, g, bass.ds(h * F0, F0)],
                                       start=(g == 0), stop=(g == NB - 1))
                    mm.then_inc(s_o, 1)

                @block.tensor
                def _(pe):
                    pe.wait_ge(s_ident, 1)
                    pe.wait_ge(s_x, 16)
                    pe.wait_ge(s_w0, 16)
                    n = 0
                    for t in (xs, w0_sb):
                        for k in range(KB):
                            if n >= 2:
                                pe.wait_ge(s_t0c, n - 1)
                            for c in range(NB):
                                mm = pe.transpose(ps[n % 2][:, c * P:(c + 1) * P], t[:, c, k * P:(k + 1) * P], ident[:, :])
                            mm.then_inc(s_t0, 1)
                            n += 1
                    pe.wait_ge(s_t0c, n)
                    for c in range(NB):
                        if c >= 2:
                            pe.wait_ge(s_xhc, c - 1)
                        for k in range(KB):
                            mm = pe.matmul(ps[c % 2][:, :], xT[:, k, c * P:(c + 1) * P], w0T[:, k, :],
                                           start=(k == 0), stop=(k == KB - 1))
                        mm.then_inc(s_xh, 1)
                    pe.wait_ge(s_ident, 2)
                    pe.wait_ge(s_tot, 1)
                    pe.matmul(ps[2][:, 0:NB], tri[:, :], tot[:, :], start=True, stop=True)
                    pe.matmul(ps[2][:, NB:2 * NB], ones[:, :], tot[:, :], start=True, stop=True).then_inc(s_off, 1)
                    pe.wait_ge(s_zero, 1)
                    for c in range(NB):
                        pe.matmul(ps[4 + c][:, :], zero_b[:, 0:P], zero_b[:, :], start=True, stop=False,
                                  skip_group_check=True)
                    pe.sem_inc(s_ohfree, 4)
                    pe.sem_inc(s_o, 2)
                    with pe.Fori(0, ET // 4) as i:
                        for k in range(4):
                            pe.wait_ge(s_oh, i * 4 + k + 1)
                            for c in range(NB):
                                mm = pe.matmul(ps[4 + c][:, :], ohd[:, k, c * P:(c + 1) * P], ohs[:, k, :],
                                               start=False, stop=False, skip_group_check=True)
                            mm.then_inc(s_ohfree, 1)
                    for c in range(NB):
                        mm = pe.matmul(ps[4 + c][:, :], zero_b[:, 0:P], zero_b[:, :], start=False, stop=True,
                                       skip_group_check=True)
                    mm.then_inc(s_cnt, 1)
                    pe.wait_ge(s_cs, 1)
                    for c in range(NB):
                        if c >= 2:
                            pe.wait_ge(s_mTc, c - 1)
                        for g in range(NB):
                            mm = pe.transpose(ps[c % 2][:, g * P:(g + 1) * P], count[:, g, c * P:(c + 1) * P], ident[:, :])
                        mm.then_inc(s_mT, 1)
                    with pe.Fori(0, H0) as h:
                        pe.wait_ge(s_diag, h + 1)
                        pe.wait_ge(s_ts, h * 4 + 4)
                        pe.matmul(ps[0][:, :], ones[:, :], diag[:, :, :].rearrange("p c n -> p (c n)"),
                                  start=True, stop=True).then_inc(s_sjb, 1)
                        for c in range(NB):
                            pe.wait_ge(s_ex, h * 4 + c + 3)
                            pe.wait_ge(s_xTc, h * 4 + c + 1)
                            for g in range(NB):
                                mm = pe.transpose(ps[2 + c % 2][:, g * P:(g + 1) * P], ex[:, c % 2, g * P:(g + 1) * P],
                                                  ident[:, :])
                            mm.then_inc(s_xT, 1)
                            if c >= 1:
                                l0_out(pe, h, c - 1)
                        l0_out(pe, h, NB - 1)
                    pe.wait_ge(s_lnx0, 1)
                    for k in range(KB):
                        if k >= 2:
                            pe.wait_ge(s_xT0c, k - 1)
                        for c in range(NB):
                            mm = pe.transpose(ps[k % 2][:, c * P:(c + 1) * P], xs[:, c, k * P:(k + 1) * P], ident[:, :])
                        mm.then_inc(s_xT0, 1)

                @block.scalar
                def _(act):
                    act.sem_inc(s_ts, 4)
                    act.sem_inc(s_xTc, 2)
                    act.sem_inc(s_ex, 2)
                    for n in range(2 * KB):
                        act.wait_ge(s_t0, n + 1)
                        t = xT if n < KB else w0T
                        act.activation(t[:, n % KB, :], ps[n % 2][:, :], ACT.Copy).then_inc(s_t0c, 1)
                    for c in range(NB):
                        act.wait_ge(s_xh, c + 1)
                        act.activation(xh[:, c, :], ps[c % 2][:, :], ACT.Copy).then_inc(s_xhc, 1)
                    with act.Fori(0, H0) as h:
                        act.wait_ge(s_sjb, h + 1)

                        def tsum_step(c):
                            act.wait_ge(s_em, h * 4 + c + 1)
                            act.activation(tsum[:, c % 2, :], ps[0][:, :], ACT.Identity,
                                           bias=sij[:, 1, c, bass.ds(h, 1)]).then_inc(s_ts, 1)

                        def exp_step(c):
                            act.wait_ge(s_nm, h * 4 + c + 1)
                            act.activation(ex[:, c % 2, :], lsc[:, c % 2, :], ACT.Exp, bias=nmx[:, c:c + 1],
                                           accum_out=rsum[:, c:c + 1]).then_inc(s_ex, 1)

                        def evac_step(c):
                            act.wait_ge(s_xT, h * 4 + c + 1)
                            act.wait_ge(s_o, h * 4 + c + 1)
                            act.activation(exT[:, c % 2, :, :].rearrange("p g n -> p (g n)"), ps[2 + c % 2][:, :],
                                           ACT.Copy).then_inc(s_xTc, 1)

                        tsum_step(0)
                        tsum_step(1)
                        exp_step(0)
                        tsum_step(2)
                        exp_step(1)
                        evac_step(0)
                        tsum_step(3)
                        evac_step(1)
                        exp_step(2)
                        exp_step(3)
                        evac_step(2)
                        evac_step(3)
                    root(act, s_ln0, s_ln0r)
                    for k in range(KB):
                        act.wait_ge(s_xT0, k + 1)
                        act.activation(xT[:, k, :], ps[k % 2][:, :], ACT.Copy).then_inc(s_xT0c, 1)

                @block.vector
                def _(dve):
                    s = Steps(dve, s_v0)
                    dve.memset(zero_b[:, :], 0.0).then_inc(s_zero, 1)
                    dve.wait_ge(s_iota, 1)
                    s.mark(dve.tensor_copy(iota[:, :], iota_i[:, :]))
                    s.mark(dve.tensor_copy(iota_h[:, :], iota_i[:, :]))
                    dve.wait_ge(s_idx, 32)
                    s.mark(dve.tensor_copy(dst_f[:, :], dst_i[:, :]))
                    s.mark(dve.tensor_copy(src_f[:, :], src_i[:, :]))
                    s.link(dve.tensor_scalar(tmp_i[:, :], dst_i[:, :], P - 1, None, ALU.bitwise_and))
                    dve.tensor_copy(loc_f[:, :], tmp_i[:, :]).then_inc(s_loc, 1)
                    dve.wait_ge(s_loc, 1)
                    s.link(dve.tensor_scalar(tmp_i[:, :], dst_i[:, :], 7, None, ALU.logical_shift_right))
                    s.link(dve.tensor_copy(blk_f[:, :], tmp_i[:, :]))
                    dve.wait_ge(s_const, 2)
                    for g in range(NB):
                        s.mark(dve.tensor_scalar(mask_g[:, g, :], blk_f[:, :], float(g), None, ALU.is_equal))
                    s.wait()
                    for g in range(NB):
                        s.mark(dve.tensor_tensor_scan(scan_g[:, g, :], ones[:, :], mask_g[:, g, :], 0.0,
                                                      ALU.mult, ALU.add))
                    s.wait()
                    dve.tensor_copy(tot[:, :], scan_g[:, :, ET - 1]).then_inc(s_tot, 1)
                    dve.wait_ge(s_off, 1)
                    s.link(dve.tensor_scalar(sc_i[:, 0, :], ps[2][:, NB:2 * NB], float(UNIT - 1), None, ALU.add))
                    s.link(dve.tensor_scalar(sc_i[:, 1, :], sc_i[:, 0, :], 9, None, ALU.logical_shift_right))
                    s.link(dve.tensor_copy(sc[:, 0, :], sc_i[:, 1, :]))
                    s.link(dve.tensor_tensor_scan(sc[:, 1, :], ones[:, 0:NB], sc[:, 0, :], 0.0, ALU.mult, ALU.add))
                    s.link(dve.tensor_tensor(sc[:, 2, :], sc[:, 1, :], sc[:, 0, :], ALU.subtract))
                    s.link(dve.tensor_scalar(sc[:, 3, :], sc[:, 2, :], float(UNIT), -1.0, ALU.mult, ALU.add))
                    s.link(dve.tensor_tensor(sc[:, 4, :], ps[2][:, 0:NB], sc[:, 3, :], ALU.add))
                    for g in range(NB):
                        s.mark(dve.scalar_tensor_tensor(scan_g[:, g, :], scan_g[:, g, :], sc[:, 4, g:g + 1],
                                                        mask_g[:, g, :], ALU.add, ALU.mult))
                    s.wait()
                    s.link(dve.tensor_tensor(pos_f[:, :], scan_g[:, 0, :], scan_g[:, 1, :], ALU.add))
                    s.link(dve.tensor_tensor(pos_f[:, :], pos_f[:, :], scan_g[:, 2, :], ALU.add))
                    s.link(dve.tensor_tensor(pos_f[:, :], pos_f[:, :], scan_g[:, 3, :], ALU.add))
                    dve.tensor_copy(pos_i[:, :], pos_f[:, :]).then_inc(s_pos, 1)
                    s.link(dve.tensor_scalar(ub_f[:, :], iota[:, 0:NU + 1], sc[:, 2, 1:2], None, ALU.is_ge))
                    for g in (2, 3):
                        s.link(dve.scalar_tensor_tensor(ub_f[:, :], iota[:, 0:NU + 1], sc[:, 2, g:g + 1], ub_f[:, :],
                                                        ALU.is_ge, ALU.add))
                    s.link(dve.tensor_scalar(ubase[:, :], ub_f[:, :], 1024.0, None, ALU.mult))

                    with dve.Fori(0, ET // 4) as i:
                        for k in range(4):
                            dve.wait_ge(s_ohfree, i * 4 + k + 1)
                            dve.tensor_scalar(ohd[:, k, :], iota_h[:, :], dst_f[:, bass.ds(i * 4 + k, 1)], None,
                                              ALU.is_equal)
                            dve.tensor_scalar(ohs[:, k, :], iota_h[:, :], src_f[:, bass.ds(i * 4 + k, 1)], None,
                                              ALU.is_equal).then_inc(s_oh, 1)
                    dve.wait_ge(s_xhc, NB)
                    dve.wait_ge(s_a0, 32)
                    for c in range(NB):
                        for j in range(2):
                            s.mark(dve.tensor_tensor(prod[:, j, :], xh[:, c, :], a_b[:, j, :, :].rearrange("p h f -> p (h f)"), ALU.mult))
                        s.wait()
                        for j in range(2):
                            s.mark(dve.tensor_reduce(sij[:, j, c, :], prod[:, j, :].rearrange("p (h f) -> p h f", h=H0),
                                                     AX.X, ALU.add))
                        s.wait()
                    dve.wait_ge(s_cnt, 1)
                    for c in range(NB):
                        s.mark(dve.tensor_copy(count[:, c, :], ps[4 + c][:, :]))
                    s.wait()
                    for c in range(NB):
                        ins = dve.tensor_scalar(nomask[:, c, :], count[:, c, :], 0.0, NEG, ALU.is_equal, ALU.mult)
                    ins.then_inc(s_cs, 1)
                    for c in range(NB):
                        dve.wait_ge(s_mT, c + 1)
                        dve.tensor_scalar(maskT[:, c, :], ps[c % 2][:, :], 1.0, None, ALU.min).then_inc(s_mTc, 1)
                    dve.wait_ge(s_mTc, NB)
                    dve.sem_inc(s_em, 2)
                    dve.sem_inc(s_y, 2)
                    with dve.Fori(0, H0) as h:
                        v = Steps(dve, s_vl0, h, 12)
                        dve.wait_ge(s_ts, h * 4 + 4)
                        dve.tensor_tensor(diag[:, :, :], ident[:, None, :].to_broadcast([P, NB, P]),
                                          sij[:, 0, :, bass.ds(h, 1)].to_broadcast([P, NB, P]), ALU.mult).then_inc(s_diag, 1)

                        def score(c):
                            dve.wait_ge(s_ts, h * 4 + c + 5)
                            dve.sem_inc(s_gate_dve, 1)
                            dve.tensor_tensor_reduce(esc[:, c % 2, :], tsum[:, c % 2, :], maskT[:, c, :], 1.0, -3.0e38,
                                                     ALU.mult, ALU.max, emx[:, c % 2:c % 2 + 1]).then_inc(s_em, 1)
                            dve.wait_ge(s_em, h * 4 + c + 3)
                            dve.wait_ge(s_ex, h * 4 + c + 1)
                            v.mark(dve.scalar_tensor_tensor(lsc[:, c % 2, :], esc[:, c % 2, :], 0.2, esc[:, c % 2, :],
                                                            ALU.mult, ALU.max))
                            v.link(dve.scalar_tensor_tensor(nmx[:, c:c + 1], emx[:, c % 2:c % 2 + 1], 0.2,
                                                            emx[:, c % 2:c % 2 + 1], ALU.mult, ALU.max))
                            dve.tensor_scalar(nmx[:, c:c + 1], nmx[:, c:c + 1], -1.0, None, ALU.mult).then_inc(s_nm, 1)

                        def result(c):
                            dve.wait_ge(s_ex, h * 4 + c + 3)
                            v.link(dve.reciprocal(rinv[:, c:c + 1], rsum[:, c:c + 1]))
                            dve.wait_ge(s_o, h * 4 + c + 3)
                            dve.scalar_tensor_tensor(y0[:, c, bass.ds(h * F0, F0)], ps[4 + c % 2][:, 0:F0],
                                                     rinv[:, c:c + 1], xs[:, c, bass.ds(h * F0, F0)],
                                                     ALU.mult, ALU.add).then_inc(s_y, 1)

                        score(0)
                        score(1)
                        score(2)
                        result(0)
                        score(3)
                        result(1)
                        result(2)
                        result(3)
                        v.done()
                    dve.wait_ge(s_y, 4 * H0 + 2)
                    layernorm(dve, s, s_ln0, s_ln0r, y0, xs)
                    dve.sem_inc(s_lnx0, 1)
        with ExitStack() as c1:
            def t1(name, shape, dt=F32):
                return sb(name, shape, dt, c1)

            SCALE1 = float(D) ** -0.5
            bvb = t1("bvb", [P, H1, D])
            bT = t1("bT", [P, 3, H1 * KB])
            qT, kT, xaT = (t1(n, [P, KB, N]) for n in ("qT", "kT", "xaT"))
            v1 = t1("v1", [P, NB, D])
            sm1 = t1("sm1", [P, 2, N])
            pr1 = t1("pr1", [P, 2, N])
            pc1 = t1("pc1", [P, 2, N])
            pn1 = t1("pn1", [P, NB, N])
            pT1 = t1("pT1", [P, NB, N])
            mx1 = t1("mx1", [P, 4])
            nm1 = t1("nm1", [P, 4])
            dn1 = t1("dn1", [P, 4])
            ri1 = t1("ri1", [P, 4])
            h1 = t1("h1", [P, NB, D])

            s_bv, s_bTp, s_bT, s_xl0 = (sem(n) for n in ("s_bv", "s_bTp", "s_bT", "s_xl0"))
            s_q, s_qc, s_k, s_s, s_sm, s_nm1, s_e1 = (sem(n) for n in ("s_q", "s_qc", "s_k", "s_s", "s_sm", "s_nm1", "s_e1"))
            s_c1, s_n1, s_p1, s_p1c, s_v, s_vc, s_g, s_gc, s_xl = (sem(n) for n in ("s_c1", "s_n1", "s_p1", "s_p1c", "s_v", "s_vc", "s_g", "s_gc", "s_xl"))
            s_d1, s_h1v, s_h1d, s_xlast = (sem(n) for n in ("s_d1", "s_h1v", "s_h1d", "s_xlast"))
            s_ln1a, s_ln1ar, s_ln1b, s_ln1br, s_lnx1, s_xT1, s_xT1c = (sem(n) for n in ("s_ln1a", "s_ln1ar", "s_ln1b", "s_ln1br", "s_lnx1", "s_xT1", "s_xT1c"))

            with nc.Block() as block:
                @block.sync
                def _(sp):
                    sp.dma_start(bvb[:, :, :], bv.rearrange("(h c) -> h c", h=H1).partition_broadcast(P)).then_inc(s_bv, 16)
                    with sp.Fori(0, H1 - 1) as i:
                        h = (H1 - 2) - i
                        sp.wait_ge(s_q, i * 8 + 4)
                        sp.sem_inc(s_gate_sp, 1)
                        head_loads(sp, h, ("wq",))
                        sp.wait_ge(s_q, i * 8 + 8)
                        sp.sem_inc(s_gate_sp, 1)
                        head_loads(sp, h, ("wk",))
                        sp.wait_ge(s_v, i * 4 + 4)
                        sp.sem_inc(s_gate_sp, 1)
                        head_loads(sp, h, ("wv",))
                        sp.wait_ge(s_g, i * 4 + 4)
                        sp.sem_inc(s_gate_sp, 1)
                        head_loads(sp, h, ("ws",))
                        sp.wait_ge(s_xl, i + 1)
                        sp.sem_inc(s_gate_sp, 1)
                        head_loads(sp, h, ("wl",))

                @block.tensor
                def _(pe):
                    pe.wait_ge(s_b1, 96)
                    for j in range(3):
                        mm = pe.transpose(ps[4][:, j * 16:(j + 1) * 16], brow[:, j, :], ident[0:16, 0:16])
                    mm.then_inc(s_bTp, 1)
                    for c in range(NB):
                        pe.matmul(ps[c][:, :], ones[0:1, :], blin_row[:, :], start=True, stop=False, skip_group_check=True)
                    pe.wait_ge(s_bT, 1)
                    with pe.Fori(0, H1) as i:
                        for j, (w, n) in enumerate(((wq_sb, "wq"), (wk_sb, "wk"))):
                            pe.wait_ge(s_w1[n], i * 16 + 16)
                            for c in range(KB):
                                pe.wait_ge(s_qc, i * 12 + j * 4 + c + 1)
                                for k in range(KB):
                                    mm = pe.matmul(ps[4 + c % 2][:, :], w[:, k, c * P:(c + 1) * P], xT[:, k, :],
                                                   start=(k == 0), stop=(k == KB - 1))
                                mm.then_inc(s_q, 1)
                        pe.wait_ge(s_qc, i * 12 + 8 + 2)
                        for c in range(NB):
                            pe.wait_ge(s_vc, i * 12 + c + 1)
                            for k in range(KB):
                                mm = pe.matmul(ps[6 + c % 2][:, :], qT[:, k, c * P:(c + 1) * P], kT[:, k, :],
                                               start=(k == 0), stop=(k == KB - 1))
                            mm.then_inc(s_s, 1)
                        pe.wait_ge(s_w1["wv"], i * 16 + 16)
                        for c in range(NB):
                            pe.wait_ge(s_vc, i * 12 + 4 + c + 1)
                            for k in range(KB):
                                mm = pe.matmul(ps[6 + c % 2][:, :], xT[:, k, c * P:(c + 1) * P], wv_sb[:, k, :],
                                               start=(k == 0), stop=(k == KB - 1))
                            mm.then_inc(s_v, 1)
                        for c in range(NB):
                            pe.wait_ge(s_n1, i * 4 + c + 3)
                            pe.wait_ge(s_qc, i * 12 + 8 + c + 1)
                            for g in range(NB):
                                mm = pe.transpose(ps[4 + c % 2][:, g * P:(g + 1) * P], pn1[:, c, g * P:(g + 1) * P],
                                                  ident[:, :])
                            mm.then_inc(s_p1, 1)
                        pe.wait_ge(s_w1["ws"], i * 16 + 16)
                        for c in range(KB):
                            pe.wait_ge(s_vc, i * 12 + 8 + c + 1)
                            for k in range(KB):
                                pe.matmul(ps[6 + c % 2][:, :], ws_sb[:, k, c * P:(c + 1) * P], xT[:, k, :],
                                          start=(k == 0), stop=False)
                            if c == 0:
                                pe.wait_ge(s_qc, i * 12 + 12 + 2)
                                pe.wait_ge(s_vc, i * 12 + 8 + 2)
                            for g in range(NB):
                                mm = pe.matmul(ps[6 + c % 2][:, :], v1[:, g, c * P:(c + 1) * P], pT1[:, g, :],
                                               start=False, stop=(g == NB - 1))
                            mm.then_inc(s_g, 1)
                        pe.wait_ge(s_w1["wl"], i * 16 + 16)
                        pe.wait_ge(s_vc, i * 12 + 12 + 2)
                        for c in range(NB):
                            for k in range(KB):
                                mm = pe.matmul(ps[c][:, :], xaT[:, k, c * P:(c + 1) * P], wl_sb[:, k, :],
                                               start=False, stop=False, skip_group_check=True)
                        mm.then_inc(s_xl, 1)
                    for c in range(NB):
                        for k in range(KB):
                            mm = pe.matmul(ps[c][:, k * P:(k + 1) * P], xaT[:, k, c * P:(c + 1) * P], ident[:, :],
                                           start=False, stop=(k == KB - 1), skip_group_check=True)
                    mm.then_inc(s_xlast, 1)

                @block.scalar
                def _(act):
                    act.sem_inc(s_qc, 2)
                    act.wait_ge(s_bTp, 1)
                    act.activation(bT[:, :, :].rearrange("p a b -> p (a b)"), ps[4][:, 0:48], ACT.Copy).then_inc(s_bT, 1)
                    act.wait_ge(s_bT, 1)
                    with act.Fori(0, H1) as i:
                        h = (H1 - 1) - i
                        for j, t in enumerate((qT, kT)):
                            for c in range(KB):
                                act.wait_ge(s_q, i * 8 + j * 4 + c + 1)
                                act.activation(t[:, c, :], ps[4 + c % 2][:, :], ACT.Identity,
                                               bias=bT[:, j, bass.ds(h * KB + c, 1)]).then_inc(s_qc, 1)

                        def scaled(c):
                            act.wait_ge(s_c1, i * 4 + c + 3)
                            act.activation(pn1[:, c, :], pc1[:, c % 2, :], ACT.Copy, scale=ri1[:, c:c + 1])\
                               .then_inc(s_n1, 1)

                        def transposed(c):
                            act.wait_ge(s_p1, i * 4 + c + 1)
                            act.activation(pT1[:, :, c * P:(c + 1) * P], psum4(4 + c % 2), ACT.Copy).then_inc(s_qc, 1)

                        for c in range(NB):
                            act.wait_ge(s_nm1, i * 4 + c + 1)
                            act.wait_ge(s_c1, i * 4 + c + 1)
                            act.activation(pr1[:, c % 2, :], sm1[:, c % 2, :], ACT.Exp, bias=nm1[:, c:c + 1],
                                           scale=SCALE1).then_inc(s_e1, 1)
                            if c >= 1:
                                scaled(c - 1)
                        scaled(NB - 1)
                        for c in range(NB):
                            transposed(c)
                    root(act, s_ln1a, s_ln1ar)
                    root(act, s_ln1b, s_ln1br)

                @block.vector
                def _(dve):
                    dve.sem_inc(s_vc, 2)
                    dve.sem_inc(s_c1, 2)
                    dve.sem_inc(s_e1, 2)
                    dve.sem_inc(s_n1, 2)
                    with dve.Fori(0, H1) as i:
                        h = (H1 - 1) - i
                        v = Steps(dve, s_d1, i, 12)

                        def score(c):
                            dve.wait_ge(s_s, i * 4 + c + 1)
                            dve.wait_ge(s_e1, i * 4 + c + 1)
                            dve.sem_inc(s_gate_dve, 1)
                            dve.tensor_tensor_reduce(sm1[:, c % 2, :], ps[6 + c % 2][:, :], nomask[:, c, :], 1.0, -3.0e38,
                                                     ALU.add, ALU.max, mx1[:, c:c + 1]).then_inc(s_vc, 1)
                            dve.wait_ge(s_vc, i * 12 + c + 3)
                            dve.tensor_scalar(nm1[:, c:c + 1], mx1[:, c:c + 1], -SCALE1, None, ALU.mult).then_inc(s_nm1, 1)

                        def weigh(c):
                            dve.wait_ge(s_e1, i * 4 + c + 3)
                            dve.wait_ge(s_n1, i * 4 + c + 1)
                            dve.sem_inc(s_gate_dve, 1)
                            v.link(dve.tensor_tensor_reduce(pc1[:, c % 2, :], pr1[:, c % 2, :], count[:, c, :], 1.0, 0.0,
                                                            ALU.mult, ALU.add, dn1[:, c:c + 1]))
                            v.link(dve.tensor_scalar(dn1[:, c:c + 1], dn1[:, c:c + 1], 1.0e-30, None, ALU.max))
                            v.link(dve.reciprocal(ri1[:, c:c + 1], dn1[:, c:c + 1]))
                            dve.sem_inc(s_c1, 1)

                        score(0)
                        score(1)
                        weigh(0)
                        score(2)
                        weigh(1)
                        score(3)
                        weigh(2)
                        weigh(3)
                        v.done()
                        dve.wait_ge(s_bv, 16)
                        for c in range(NB):
                            dve.wait_ge(s_v, i * 4 + c + 1)
                            dve.tensor_tensor(v1[:, c, :], ps[6 + c % 2][:, :], bvb[:, bass.ds(h, 1), :].rearrange("p a c -> p (a c)"),
                                              ALU.add).then_inc(s_vc, 1)
                        for c in range(KB):
                            dve.wait_ge(s_g, i * 4 + c + 1)
                            dve.tensor_scalar(xaT[:, c, :], ps[6 + c % 2][:, :], bT[:, 2, bass.ds(h * KB + c, 1)], None,
                                              ALU.add).then_inc(s_vc, 1)
                    s = Steps(dve, s_h1v)
                    dve.wait_ge(s_xlast, 1)
                    for c in range(NB):
                        s.mark(dve.tensor_copy(h1[:, c, :], ps[c][:, :]))
                    s.wait()
                    layernorm(dve, s, s_ln1a, s_ln1ar, h1, h1)
                    for c in range(NB):
                        s.mark(dve.tensor_tensor(h1[:, c, :], h1[:, c, :], gamma_b[:, :], ALU.mult))
                    s.wait()
                    for c in range(NB):
                        s.mark(dve.tensor_tensor(h1[:, c, :], h1[:, c, :], beta_b[:, :], ALU.add))
                    s.wait()
                    for c in range(NB):
                        s.mark(dve.tensor_tensor(h1[:, c, :], h1[:, c, :], xs[:, c, :], ALU.add))
                    s.wait()
                    layernorm(dve, s, s_ln1b, s_ln1br, h1, xs)
        lay1.close()

        lay3 = ExitStack()
        w31_sb = sb("w31_sb", [P, KB, W3], F32, lay3)
        w32_sb = sb("w32_sb", [P, W3 // P, W3], F32, lay3)
        fcw_sb = sb("fcw_sb", [P, W3 // P, D], F32, lay3)
        fcb_b = sb("fcb_b", [P, D], F32, lay3)
        b3row = sb("b3row", [W3 // P, 2, P], F32, lay3)
        s_w3 = [sem(f"s_w3_{n}") for n in range(3)]
        s_b3 = sem("s_b3")

        with ExitStack() as c2:
            def t2(name, shape, dt=F32):
                return sb(name, shape, dt, c2)

            wup = t2("wup", [P, 2, MUL])
            wmA = t2("wmA", [8, HID])
            wmB = t2("wmB", [HID, HID])
            wmC = t2("wmC", [HID, HID])
            wm4_sb = t2("wm4_sb", [HID, 4 * MUL])
            wout = t2("wout", [P, 2, 2, MUL])
            uT = t2("uT", [P, 4, N])
            xup = t2("xup", [P, NB, 4 * MUL])
            rb = t2("rb", [P, 2, 4, REC])
            sg = t2("sg", [P, 2, 4, 4 * MUL])
            efT = t2("efT", [8, UNIT])
            hA = t2("hA", [HID, UNIT])
            hB = t2("hB", [HID, UNIT])
            h3 = t2("h3", [HID, 2, UNIT])
            oh = t2("oh", [P, 2, P])
            msg = t2("msg", [P, 2, 8, MUL])
            dot = t2("dot", [P, 2, 3, MUL])
            acc = t2("acc", [P, NB * 8 * MUL])
            mT = t2("mT", [P, 8, N])
            y2 = t2("y2", [P, NB, D])

            s_w2, s_uT, s_uTc, s_up, s_upc, s_xup = (sem(n) for n in ("s_w2", "s_uT", "s_uTc", "s_up", "s_upc", "s_xup"))
            s_rl = [sem(f"s_rl{b}") for b in range(2)]
            s_sg = [sem(f"s_sg{b}") for b in range(2)]
            s_m, s_mc, s_w, s_msg, s_sc, s_fl, s_d2, s_d2v = (sem(n) for n in ("s_m", "s_mc", "s_w", "s_msg", "s_sc", "s_fl", "s_d2", "s_d2v"))
            s_mT2, s_mT2c, s_o2, s_o2c = (sem(n) for n in ("s_mT2", "s_mT2c", "s_o2", "s_o2c"))
            s_ln2, s_ln2r, s_w4, s_gate_pe = (sem(n) for n in ("s_ln2", "s_ln2r", "s_w4", "s_gate_pe"))
            LOOPS = (NU - 1) // 2
            assert NU == 2 * LOOPS + 1

            with nc.Block() as block:
                @block.sync
                def _(sp):
                    sp.dma_start(wup[:, 0, :], wup0).then_inc(s_w2, 16)
                    sp.dma_start(wup[:, 1, :], wup1).then_inc(s_w2, 16)
                    sp.dma_start(wmA[:, :], wm1).then_inc(s_w2, 16)
                    sp.dma_start(wmB[:, :], wm2).then_inc(s_w2, 16)
                    sp.dma_start(wmC[:, :], wm3).then_inc(s_w2, 16)
                    sp.dma_start(wm4_sb[:, :], wm4).then_inc(s_w2, 16)
                    for j, w in enumerate((wout0, wout1)):
                        sp.dma_start(wout[:, j, :, :], w.rearrange("(k p) v -> p k v", p=P)).then_inc(s_w2, 16)

                    def load(u, b):
                        sp.wait_ge(s_msg, u * 4 + 4)
                        sp.sem_inc(s_gate_sp, 1)
                        sp.dma_start(rb[:, b, :, :], records.ap()[bass.ds(u * UNIT, UNIT), :].rearrange("(p t) k -> p t k", p=P))\
                            .then_inc(s_rl[b], 16)

                    load(0, 0)
                    load(1, 1)
                    sp.wait_ge(s_upc, NB)
                    sp.dma_start(xup_dram.ap().rearrange("(c p) d -> p c d", p=P), xup[:, :, :]).then_inc(s_xup, 16)
                    sp.dma_start(w31_sb[:, :, :], w31.rearrange("(k p) c -> p k c", p=P)).then_inc(s_w3[0], 16)
                    sp.dma_start(w32_sb[:, :, :], w32.rearrange("(k p) c -> p k c", p=P)).then_inc(s_w3[1], 16)
                    sp.dma_start(fcw_sb[:, :, :], fcw.rearrange("(k p) c -> p k c", p=P)).then_inc(s_w3[2], 16)
                    sp.dma_start(fcb_b[:, :], fcb.partition_broadcast(P)).then_inc(s_b3, 16)
                    sp.dma_start(b3row[:, 0, :], b31.rearrange("(c p) -> c p", p=P)).then_inc(s_b3, 16)
                    sp.dma_start(b3row[:, 1, :], b32.rearrange("(c p) -> c p", p=P)).then_inc(s_b3, 16)
                    with sp.Fori(0, LOOPS) as j:
                        load(j * 2 + 2, 0)
                        load(j * 2 + 3, 1)

                @block.gpsimd
                def _(pool):
                    def gather(u, turn, b):
                        pool.wait_ge(s_rl[b], turn * 16 + 16)
                        pool.sem_inc(s_gate_pool, 1)
                        for k in range(4):
                            pool.indirect_dma_start(sg[:, b, k, :], None, xup_dram.ap()[:, :],
                                                    bass.IndirectOffsetOnAxis(ap=rb[:, b, k, 12:13].bitcast(I32), axis=0))\
                                .then_inc(s_sg[b], 16)

                    pool.wait_ge(s_xup, 16)
                    gather(0, 0, 0)
                    with pool.Fori(0, LOOPS) as j:
                        gather(j * 2 + 1, j, 1)
                        gather(j * 2 + 2, j + 1, 0)
                    pool.wait_ge(s_sg[0], 64 * (LOOPS + 1))
                    pool.wait_ge(s_sg[1], 64 * LOOPS)

                @block.tensor
                def _(pe):
                    pe.wait_ge(s_w2, 16 * 8)
                    for m in range(4):
                        if m >= 2:
                            pe.wait_ge(s_uTc, m - 1)
                        for c in range(NB):
                            part = xs[:, c, 0:MUL] if m == 0 else xs[:, c, MUL + m - 1:D:3]
                            mm = pe.transpose(ps[m % 2][:, c * P:(c + 1) * P], part, ident[:, :])
                        mm.then_inc(s_uT, 1)
                    pe.wait_ge(s_uTc, 4)
                    for c in range(NB):
                        if c >= 2:
                            pe.wait_ge(s_upc, c - 1)
                        for m in range(4):
                            mm = pe.matmul(ps[2 + c % 2][:, m * MUL:(m + 1) * MUL], uT[:, m, c * P:(c + 1) * P],
                                           wup[:, min(m, 1), :], start=True, stop=True)
                        mm.then_inc(s_up, 1)
                    pe.wait_ge(s_upc, NB)

                    def edge_mlp(u, turn, b, step):
                        if step == 0:
                            pe.wait_ge(s_rl[b], turn * 16 + 16)
                            for k in range(4):
                                mm = pe.transpose(ps[6][0:8, k * P:(k + 1) * P], rb[:, b, k, 0:8], ident[:, :])
                        else:
                            pe.wait_ge(s_mc, u * 4 + step)
                            pe.sem_inc(s_gate_pe, 1)
                            w, t = ((wmA, efT), (wmB, hA), (wmC, hB))[step - 1]
                            mm = pe.matmul(ps[6 + step % 2][0:HID, :], w[:, :], t[:, :], start=True, stop=True)
                        mm.then_inc(s_m, 1)

                    def weights(u, b, k):
                        if k == 0:
                            pe.wait_ge(s_mc, u * 4 + 4)
                        pe.wait_ge(s_msg, u * 4 + k + 7)
                        pe.matmul(ps[4 + k % 2][:, :], h3[:, b, k * P:(k + 1) * P], wm4_sb[:, :],
                                  start=True, stop=True).then_inc(s_w, 1)

                    def scatter(u, b, k):
                        if k == 0:
                            pe.wait_ge(s_fl, u + 1)
                        pe.wait_ge(s_msg, u * 4 + k + 9)
                        for half in range(2):
                            mm = pe.matmul(ps[2 * b + half][:, :], oh[:, k % 2, :],
                                           msg[:, k % 2, 4 * half:4 * half + 4, :].rearrange("p a v -> p (a v)"),
                                           start=(k == 0), stop=(k == 3))
                        mm.then_inc(s_sc, 1)

                    def unit(u, next_turn, b):
                        edge_mlp(u + 1, next_turn, 1 - b, 0)
                        weights(u, b, 1)
                        scatter(u, b, 0)
                        edge_mlp(u + 1, next_turn, 1 - b, 1)
                        weights(u, b, 2)
                        edge_mlp(u + 1, next_turn, 1 - b, 2)
                        scatter(u, b, 1)
                        edge_mlp(u + 1, next_turn, 1 - b, 3)
                        weights(u, b, 3)
                        scatter(u, b, 2)

                    pe.wait_ge(s_w4, 1)
                    for step in range(4):
                        edge_mlp(0, 0, 0, step)
                    weights(0, 0, 0)
                    unit(0, 0, 0)
                    with pe.Fori(0, LOOPS) as j:
                        weights(j * 2 + 1, 1, 0)
                        scatter(j * 2, 0, 3)
                        unit(j * 2 + 1, j + 1, 1)
                        weights(j * 2 + 2, 0, 0)
                        scatter(j * 2 + 1, 1, 3)
                        unit(j * 2 + 2, j + 1, 0)
                    scatter(NU - 1, 0, 3)
                    pe.wait_ge(s_fl, NU + 2)
                    for m in range(8):
                        if m >= 2:
                            pe.wait_ge(s_mT2c, m - 1)
                        for g in range(NB):
                            col = (g * 8 + m) * MUL
                            mm = pe.transpose(ps[4 + m % 2][:, g * P:(g + 1) * P], acc[:, col:col + MUL], ident[:, :])
                        mm.then_inc(s_mT2, 1)
                    pe.wait_ge(s_mT2c, 8)
                    for c in range(NB):
                        if c >= 2:
                            pe.wait_ge(s_o2c, c - 1)
                        for m in range(4):
                            a, b = (0, 1) if m == 0 else (1 + m, 4 + m)
                            for half, blk in enumerate((a, b)):
                                mm = pe.matmul(ps[c % 2][:, m * MUL:(m + 1) * MUL], mT[:, blk, c * P:(c + 1) * P],
                                               wout[:, min(m, 1), half, :], start=(half == 0), stop=(half == 1))
                        mm.then_inc(s_o2, 1)

                @block.scalar
                def _(act):
                    act.sem_inc(s_msg, 8)
                    act.sem_inc(s_sc, 2)
                    act.sem_inc(s_fl, 2)
                    for m in range(4):
                        act.wait_ge(s_uT, m + 1)
                        act.activation(uT[:, m, :], ps[m % 2][:, :], ACT.Copy).then_inc(s_uTc, 1)
                    for c in range(NB):
                        act.wait_ge(s_up, c + 1)
                        act.activation(xup[:, c, :], ps[2 + c % 2][:, :], ACT.Copy, scale=MUL ** -0.5).then_inc(s_upc, 1)

                    def edge_mlp(u, b):
                        act.wait_ge(s_m, u * 4 + 1)
                        act.activation(efT[:, :], ps[6][0:8, :], ACT.Copy).then_inc(s_mc, 1)
                        for step, t, scale in ((1, hA[:, :], 8 ** -0.5), (2, hB[:, :], SILU_2MOM * HID ** -0.5),
                                               (3, h3[:, b, :], SILU_2MOM * HID ** -0.5)):
                            act.wait_ge(s_m, u * 4 + step + 1)
                            act.activation(t, ps[6 + step % 2][0:HID, :], ACT.Silu, scale=scale).then_inc(s_mc, 1)

                    edge_mlp(0, 0)
                    edge_mlp(1, 1)
                    with act.Fori(0, LOOPS) as j:
                        edge_mlp(j * 2 + 2, 0)
                        edge_mlp(j * 2 + 3, 1)
                    for m in range(8):
                        act.wait_ge(s_mT2, m + 1)
                        act.activation(mT[:, m, :], ps[4 + m % 2][:, :], ACT.Copy).then_inc(s_mT2c, 1)
                    root(act, s_ln2, s_ln2r)

                @block.vector
                def _(dve):
                    s = Steps(dve, s_d2)
                    dve.wait_ge(s_w2, 16 * 8)
                    c4 = SILU_2MOM * HID ** -0.5
                    dve.tensor_scalar(wm4_sb[:, 0:3 * MUL], wm4_sb[:, 0:3 * MUL], c4, None, ALU.mult)
                    dve.tensor_scalar(wm4_sb[:, 3 * MUL:], wm4_sb[:, 3 * MUL:], c4 * 3.0 ** -0.5, None, ALU.mult).then_inc(s_w4, 1)
                    s.link(dve.memset(acc[:, :], 0.0))

                    def messages(v, u, turn, b, k):
                        y = [rb[:, b, k, 8 + m:9 + m] for m in range(4)]
                        feat, w, out_ = sg[:, b, k, :], ps[4 + k % 2], msg[:, k % 2, :, :]
                        if k == 0:
                            dve.wait_ge(s_rl[b], turn * 16 + 16)
                            dve.wait_ge(s_sg[b], turn * 64 + 64)
                        d = dot[:, k % 2, :, :]
                        dve.wait_ge(s_msg, u * 4 + k + 7)
                        v.link(dve.tensor_scalar(d[:, 0, :], feat[:, MUL:2 * MUL], y[1], None, ALU.mult))
                        v.link(dve.scalar_tensor_tensor(d[:, 1, :], feat[:, 2 * MUL:3 * MUL], y[2], d[:, 0, :], ALU.mult, ALU.add))
                        v.mark(dve.scalar_tensor_tensor(d[:, 2, :], feat[:, 3 * MUL:4 * MUL], y[3], d[:, 1, :], ALU.mult, ALU.add))
                        dve.wait_ge(s_sc, u * 4 + k + 1)
                        dve.tensor_scalar(oh[:, k % 2, :], iota[:, 0:P], rb[:, b, k, 13:14], None, ALU.is_equal)
                        dve.wait_ge(s_w, u * 4 + k + 1)
                        dve.scalar_tensor_tensor(out_[:, 0, :], w[:, 0:MUL], y[0], feat[:, 0:MUL], ALU.mult, ALU.mult)
                        for m in range(3):
                            dve.scalar_tensor_tensor(out_[:, 2 + m, :], w[:, MUL:2 * MUL], y[1 + m], feat[:, 0:MUL],
                                                     ALU.mult, ALU.mult)
                        dve.scalar_tensor_tensor(out_[:, 5:8, :], w[:, None, 2 * MUL:3 * MUL].to_broadcast([P, 3, MUL]), y[0],
                                                 feat[:, MUL:].rearrange("p (m v) -> p m v", m=3), ALU.mult, ALU.mult)
                        v.wait()
                        dve.tensor_tensor(out_[:, 1, :], w[:, 3 * MUL:4 * MUL], d[:, 2, :], ALU.mult).then_inc(s_msg, 1)

                    def flush(u, b):
                        base = dve.value_load(ubase[0:1, bass.ds(u, 1)], min_val=0, max_val=(NB - 1) * 8 * MUL)
                        dve.wait_ge(s_sc, u * 4 + 4 + 2)
                        for half in range(2):
                            t = acc[:, bass.ds(base + half * 512, 512)]
                            ins = dve.tensor_tensor(t, ps[2 * b + half][:, :], t, ALU.add)
                        ins.then_inc(s_fl, 1)

                    v = Steps(dve, s_d2v)
                    for k in range(4):
                        messages(v, 0, 0, 0, k)
                    with dve.Fori(0, LOOPS) as j:
                        v = Steps(dve, s_d2v, j + 1 - 1, 24)
                        v.base = v.base + 12
                        for b, u, turn in ((1, j * 2 + 1, j), (0, j * 2 + 2, j + 1)):
                            for k in range(4):
                                messages(v, u, turn, b, k)
                                if k == 0:
                                    flush(u - 1, 1 - b)
                        v.done()
                    flush(NU - 1, 0)
                    for c in range(NB):
                        dve.wait_ge(s_o2, c + 1)
                        sc2 = 1.0 / (16.0 * 10.0)
                        s.mark(dve.scalar_tensor_tensor(y2[:, c, 0:MUL], ps[c % 2][:, 0:MUL], sc2, xs[:, c, 0:MUL], ALU.mult, ALU.add))
                        dve.scalar_tensor_tensor(y2[:, c, MUL:].rearrange("p (v m) -> p m v", m=3),
                                                 ps[c % 2][:, MUL:].rearrange("p (m v) -> p m v", m=3), sc2,
                                                 xs[:, c, MUL:].rearrange("p (v m) -> p m v", m=3),
                                                 ALU.mult, ALU.add).then_inc(s_o2c, 1)
                    s.wait()
                    dve.wait_ge(s_o2c, NB)
                    layernorm(dve, s, s_ln2, s_ln2r, y2, xs)

        with ExitStack() as c3:
            def t3_(name, shape, dt=F32):
                return sb(name, shape, dt, c3)

            K3 = W3 // P
            FB = F3 // P
            att_b = t3_("att_b", [P, 2, 2, H3, F3])
            b3T = t3_("b3T", [P, 2, K3])
            hs3 = t3_("hs3", [P, NB, W3])
            o3T = [t3_("o3T0", [P, K3, N]), w31_sb[:, :, :].rearrange("p k (a n) -> p (k a) n", n=N)]
            sd3 = t3_("sd3", [P, 2, NB, H3])
            diag3 = t3_("diag3", [P, NB, P])
            ts3, l3, lm3, e3, pc3 = (t3_(n, [P, 2, N]) for n in ("ts3", "l3", "lm3", "e3", "pc3"))
            pn3 = t3_("pn3", [P, NB, N])
            junk3 = pn3[:, :, :].rearrange("p c (a f) -> p (c a) f", f=F3)
            pT3 = t3_("pT3", [P, NB, N])
            mx3, nm3, dn3, ri3 = (t3_(n, [P, 4]) for n in ("mx3", "nm3", "dn3", "ri3"))
            hcur = t3_("hcur", [P, NB, F3])
            y3 = hs3[:, :, 0:D]
            s_att3, s_b3p, s_b3T, s_loops, s_y3, s_out = (sem(n) for n in ("s_att3", "s_b3p", "s_b3T", "s_loops", "s_y3", "s_out"))
            s_ln3, s_ln3r, s_x3, s_x3c, s_v3 = (sem(n) for n in ("s_ln3", "s_ln3r", "s_x3", "s_x3c", "s_v3"))
            q = {n: sem(f"s3_{n}") for n in ("hp", "hc", "dg", "bc", "t", "l", "e", "nm", "c", "n", "p", "pc", "g", "oc",
                                             "cur", "v", "vl")}
            NH = 2 * NB

            def conv_tensor(pe, j, w_sb, kc, in_T):
                for c in range(NB):
                    for half in range(2):
                        n = 2 * c + half
                        if n >= 2 or j:
                            pe.wait_ge(q["hc"], j * NH + n - 1)
                        for k in range(kc):
                            mm = pe.matmul(ps[n % 2][:, :], in_T[:, k, c * P:(c + 1) * P],
                                           w_sb[:, k, half * 512:(half + 1) * 512], start=(k == 0), stop=(k == kc - 1))
                        mm.then_inc(q["hp"], 1)
                with pe.Fori(j * H3, (j + 1) * H3) as t:
                    h = t - j * H3
                    pe.wait_ge(q["t"], t * 4 + 4)
                    pe.wait_ge(q["dg"], t + 1)
                    pe.matmul(ps[2][:, :], ones[:, :], diag3[:, :, :].rearrange("p c n -> p (c n)"),
                              start=True, stop=True).then_inc(q["bc"], 1)
                    for c in range(NB):
                        pe.wait_ge(q["n"], t * 4 + c + 3)
                        pe.wait_ge(q["pc"], t * 4 + c + 1)
                        for g in range(NB):
                            mm = pe.transpose(ps[4 + c % 2][:, g * P:(g + 1) * P], pn3[:, c, g * P:(g + 1) * P], ident[:, :])
                        mm.then_inc(q["p"], 1)
                    pe.wait_ge(q["cur"], t + 1)
                    pe.wait_ge(q["pc"], t * 4 + 4 + 2)
                    for f in range(FB):
                        pe.wait_ge(q["oc"], t * 2 + f + 1)
                        for g in range(NB):
                            mm = pe.matmul(ps[6 + f][:, :], hcur[:, g, f * P:(f + 1) * P], pT3[:, g, :],
                                           start=(g == 0), stop=(g == NB - 1))
                        mm.then_inc(q["g"], 1)

            def conv_scalar(act, j, out_T):
                for n in range(2 * NB):
                    act.wait_ge(q["hp"], j * NH + n + 1)
                    act.activation(hs3[:, n // 2, (n % 2) * 512:(n % 2 + 1) * 512], ps[n % 2][:, :], ACT.Copy)\
                        .then_inc(q["hc"], 1)
                with act.Fori(j * H3, (j + 1) * H3) as t:
                    h = t - j * H3
                    act.wait_ge(q["bc"], t + 1)

                    def plus(c):
                        act.wait_ge(q["l"], t * 4 + c + 1)
                        act.activation(ts3[:, c % 2, :], ps[2][:, :], ACT.Identity, bias=sd3[:, 1, c, bass.ds(h, 1)])\
                            .then_inc(q["t"], 1)

                    def exp(c):
                        act.wait_ge(q["nm"], t * 4 + c + 1)
                        act.wait_ge(q["c"], t * 4 + c + 1)
                        act.activation(e3[:, c % 2, :], lm3[:, c % 2, :], ACT.Exp, bias=nm3[:, c:c + 1]).then_inc(q["e"], 1)

                    def transposed(c):
                        act.wait_ge(q["p"], t * 4 + c + 5)
                        act.wait_ge(q["g"], t * 2 + 2)
                        act.activation(pT3[:, :, c * P:(c + 1) * P], psum4(4 + c % 2), ACT.Copy).then_inc(q["pc"], 1)

                    plus(0)
                    plus(1)
                    exp(0)
                    plus(2)
                    exp(1)
                    plus(3)
                    exp(2)
                    transposed(0)
                    exp(3)
                    transposed(1)
                    transposed(2)
                    transposed(3)
                    for f in range(FB):
                        act.wait_ge(q["g"], t * 2 + f + 3)
                        act.activation(out_T[:, bass.ds(h * FB + f, 1), :].rearrange("p a n -> p (a n)"), ps[6 + f][:, :],
                                       ACT.Relu, bias=b3T[:, j, bass.ds(h * FB + f, 1)]).then_inc(q["oc"], 1)

            def conv_pool(pool, j):
                pool.wait_ge(q["hc"], (j + 1) * NH)
                with pool.Fori(j * H3, (j + 1) * H3) as t:
                    h = t - j * H3
                    pool.wait_ge(q["g"], t * 2 + 2)
                    pool.sem_inc(s_gate_pool, 1)
                    pool.tensor_copy(hcur[:, :, :], hs3[:, :, bass.ds(h * F3, F3)]).then_inc(q["cur"], 1)
                    for c in range(NB):
                        pool.wait_ge(q["c"], t * 4 + c + 3)
                        pool.wait_ge(q["p"], t * 4 + c + 1)
                        pool.sem_inc(s_gate_pool, 1)
                        pool.tensor_scalar(pn3[:, c, :], pc3[:, c % 2, :], ri3[:, c:c + 1], 1.0, ALU.mult, ALU.mult)\
                            .then_inc(q["n"], 1)

            def conv_vector(dve, j):
                s = Steps(dve, q["v"], j, NB * 2 * H3)
                for c in range(NB):
                    dve.wait_ge(q["hc"], j * NH + 2 * c + 2)
                    for h in range(H3):
                        for e in range(2):
                            s.mark(dve.tensor_tensor_reduce(junk3[:, 2 * h + e, :], hs3[:, c, h * F3:(h + 1) * F3],
                                                            att_b[:, j, e, h, :], 1.0, 0.0, ALU.mult, ALU.add,
                                                            sd3[:, e, c, h:h + 1]))
                    s.wait()
                with dve.Fori(j * H3, (j + 1) * H3) as t:
                    h = t - j * H3
                    v = Steps(dve, q["vl"], t, 16)
                    dve.wait_ge(q["t"], t * 4 + 4)
                    dve.tensor_tensor(diag3[:, :, :], ident[:, None, :].to_broadcast([P, NB, P]),
                                      sd3[:, 0, :, bass.ds(h, 1)].to_broadcast([P, NB, P]), ALU.mult).then_inc(q["dg"], 1)

                    def score(c):
                        dve.wait_ge(q["t"], t * 4 + c + 5)
                        dve.scalar_tensor_tensor(l3[:, c % 2, :], ts3[:, c % 2, :], 0.2, ts3[:, c % 2, :],
                                                 ALU.mult, ALU.max).then_inc(q["l"], 1)
                        dve.wait_ge(q["e"], t * 4 + c + 1)
                        dve.wait_ge(q["l"], t * 4 + c + 3)
                        dve.sem_inc(s_gate_dve, 1)
                        v.link(dve.tensor_tensor_reduce(lm3[:, c % 2, :], l3[:, c % 2, :], nomask[:, c, :], 1.0, -3.0e38,
                                                        ALU.add, ALU.max, mx3[:, c:c + 1]))
                        dve.tensor_scalar(nm3[:, c:c + 1], mx3[:, c:c + 1], -1.0, None, ALU.mult).then_inc(q["nm"], 1)

                    def weigh(c):
                        dve.wait_ge(q["e"], t * 4 + c + 3)
                        dve.wait_ge(q["n"], t * 4 + c + 1)
                        dve.sem_inc(s_gate_dve, 1)
                        v.link(dve.tensor_tensor_reduce(pc3[:, c % 2, :], e3[:, c % 2, :], count[:, c, :], 1.0, 0.0,
                                                        ALU.mult, ALU.add, dn3[:, c:c + 1]))
                        v.link(dve.tensor_scalar(dn3[:, c:c + 1], dn3[:, c:c + 1], 1.0e-16, None, ALU.add))
                        v.link(dve.reciprocal(ri3[:, c:c + 1], dn3[:, c:c + 1]))
                        dve.sem_inc(q["c"], 1)

                    score(0)
                    score(1)
                    weigh(0)
                    score(2)
                    weigh(1)
                    score(3)
                    weigh(2)
                    weigh(3)
                    v.done()

            with nc.Block() as block:
                @block.sync
                def _(sp):
                    for j, (a, b) in enumerate(((asrc1, adst1), (asrc2, adst2))):
                        sp.dma_start(att_b[:, j, 0, :, :], a.partition_broadcast(P)).then_inc(s_att3, 16)
                        sp.dma_start(att_b[:, j, 1, :, :], b.partition_broadcast(P)).then_inc(s_att3, 16)
                    out_v = out.rearrange("(c p) d -> p c d", p=P)
                    sp.wait_ge(s_x3c, 1)
                    sp.dma_start(out_v, xs[:, :, :]).then_inc(s_out, 16)
                    sp.wait_ge(s_out, 16)

                @block.gpsimd
                def _(pool):
                    pool.sem_inc(q["n"], 2)
                    conv_pool(pool, 0)
                    conv_pool(pool, 1)

                @block.tensor
                def _(pe):
                    for k in range(KB):
                        if k >= 2:
                            pe.wait_ge(s_x3, k - 1)
                        for c in range(NB):
                            mm = pe.transpose(ps[k % 2][:, c * P:(c + 1) * P], xs[:, c, k * P:(k + 1) * P], ident[:, :])
                        mm.then_inc(s_loops, 1)
                    pe.wait_ge(s_b3, 48)
                    for j in range(2):
                        mm = pe.transpose(ps[3][:, j * K3:(j + 1) * K3], b3row[:, j, :], ident[0:K3, 0:K3])
                    mm.then_inc(s_b3p, 1)
                    pe.wait_ge(s_x3, KB)
                    for w in s_w3:
                        pe.wait_ge(w, 16)
                    conv_tensor(pe, 0, w31_sb, KB, xT)
                    pe.wait_ge(q["oc"], 2 * H3 + 2)
                    conv_tensor(pe, 1, w32_sb, K3, o3T[0])
                    pe.wait_ge(q["oc"], 4 * H3 + 2)
                    for c in range(NB):
                        for k in range(K3):
                            mm = pe.matmul(ps[c][:, :], o3T[1][:, k, c * P:(c + 1) * P], fcw_sb[:, k, :],
                                           start=(k == 0), stop=(k == K3 - 1))
                        mm.then_inc(s_y3, 1)

                @block.scalar
                def _(act):
                    for k in range(KB):
                        act.wait_ge(s_loops, k + 1)
                        act.activation(xT[:, k, :], ps[k % 2][:, :], ACT.Copy).then_inc(s_x3, 1)
                    act.wait_ge(s_b3p, 1)
                    act.activation(b3T[:, :, :].rearrange("p a b -> p (a b)"), ps[3][:, 0:2 * K3], ACT.Copy).then_inc(s_b3T, 1)
                    act.wait_ge(s_b3T, 1)
                    act.sem_inc(q["t"], 4)
                    act.sem_inc(q["pc"], 2)
                    act.sem_inc(q["oc"], 2)
                    act.sem_inc(q["e"], 2)
                    conv_scalar(act, 0, o3T[0])
                    conv_scalar(act, 1, o3T[1])
                    root(act, s_ln3, s_ln3r)

                @block.vector
                def _(dve):
                    s = Steps(dve, s_v3)
                    for c in range(NB):
                        d = count[:, c, c * P:(c + 1) * P]
                        s.mark(dve.tensor_tensor(d, d, ident[:, :], ALU.add))
                    s.wait()
                    for c in range(NB):
                        s.mark(dve.tensor_scalar(nomask[:, c, :], count[:, c, :], 0.0, NEG, ALU.is_equal, ALU.mult))
                    s.wait()
                    dve.wait_ge(s_att3, 64)
                    dve.sem_inc(q["l"], 2)
                    dve.sem_inc(q["c"], 2)
                    dve.sem_inc(q["p"], 4)
                    dve.sem_inc(q["g"], 2)
                    conv_vector(dve, 0)
                    conv_vector(dve, 1)
                    for c in range(NB):
                        dve.wait_ge(s_y3, c + 1)
                        s.mark(dve.tensor_tensor(y3[:, c, :], ps[c][:, :], fcb_b[:, :], ALU.add))
                    s.wait()
                    for c in range(NB):
                        s.mark(dve.tensor_tensor(y3[:, c, :], y3[:, c, :], xs[:, c, :], ALU.add))
                    s.wait()
                    layernorm(dve, s, s_ln3, s_ln3r, y3, xs)
                    dve.sem_inc(s_x3c, 1)
        lay3.close()
    return nc


_INS = ['x', 'src', 'dst', 'edge_attr_4', 'edge_attr_8', 'L0_gnn_W', 'L0_gnn_a', 'L1_gnn_Wq', 'L1_gnn_bq', 'L1_gnn_Wk',
        'L1_gnn_bk', 'L1_gnn_Wv', 'L1_gnn_bv', 'L1_gnn_Wskip', 'L1_gnn_bskip', 'L1_gnn_Wlin', 'L1_gnn_blin',
        'L1_gnn_gamma', 'L1_gnn_beta', 'L2_gnn_W_up0', 'L2_gnn_W_up1', 'L2_gnn_W_mlp1', 'L2_gnn_W_mlp2',
        'L2_gnn_W_mlp3', 'L2_gnn_W_mlp4', 'L2_gnn_W_out0', 'L2_gnn_W_out1', 'L3_gnn_W1', 'L3_gnn_att_src1',
        'L3_gnn_att_dst1', 'L3_gnn_b1', 'L3_gnn_W2', 'L3_gnn_att_src2', 'L3_gnn_att_dst2', 'L3_gnn_b2', 'L3_gnn_fcW',
        'L3_gnn_fcb']


def kernel(**inputs):
    import numpy as _np
    import concourse.bacc as _bacc
    from concourse import mybir as _mybir
    from concourse.bass_utils import run_bass_kernel_spmd as _run

    nc = _bacc.Bacc("TRN2", target_bir_lowering=False, num_devices=1)
    arrays, args = {}, []
    for name in _INS:
        a = _np.ascontiguousarray(inputs[name])
        arrays[f"in_{name}_dram"] = a
        args.append(nc.dram_tensor(f"in_{name}_dram", a.shape, _mybir.dt.from_np(a.dtype), kind="ExternalInput").ap())
    args.append(nc.dram_tensor("out_0_dram", (N, D), F32, kind="ExternalOutput").ap())
    graph_kernel(nc, *args)
    r = _run(nc, [arrays], core_ids=[0])
    return r.results[0]["out_0_dram"]
```

```python
from contextlib import ExitStack

import concourse.bass as bass
from concourse import mybir

F32 = mybir.dt.float32
F32R = mybir.dt.float32r
BF16 = mybir.dt.bfloat16
F16 = mybir.dt.float16
I32 = mybir.dt.int32
U32 = mybir.dt.uint32
ALU = mybir.AluOpType
ACT = mybir.ActivationFunctionType
AX = mybir.AxisListType

P = 128
N = 512
D = 512
E = 16384
NB = N // P
KB = D // P
ET = E // P
UNIT = 4 * P
NU = E // UNIT + NB - 1
REC = 16
NEG = -1.0e30
EPS = 1e-5
H0, F0 = 8, 64
H1 = 4
H3, F3 = 4, 256
W3 = H3 * F3
MUL = 128
HID = 64
SILU_2MOM = 1.679177
SPLIT_PASSES = ((0, 0), (0, 1), (1, 0))


class Steps:

    def __init__(self, eng, sem, turn=0, per_turn=0):
        self.eng, self.sem, self.base, self.n, self.per_turn = eng, sem, turn * per_turn, 0, per_turn

    def link(self, instruction):
        self.mark(instruction)
        self.wait()

    def mark(self, instruction):
        instruction.then_inc(self.sem, 1)
        self.n += 1

    def wait(self):
        self.eng.wait_ge(self.sem, self.base + self.n)

    def done(self):
        assert self.n == self.per_turn, self.n


def graph_kernel(nc, x, src, dst, ea, ef, w0, a0, wq, bq, wk, bk, wv, bv, wskip, bskip, wlin, blin, gamma, beta,
                 wup0, wup1, wm1, wm2, wm3, wm4, wout0, wout1, w31, asrc1, adst1, b31, w32, asrc2, adst2, b32,
                 fcw, fcb, out):
    ctx = ExitStack()
    with ctx:
        def sem(name):
            return ctx.enter_context(nc.semaphore(name))

        def sb(name, shape, dt=F32, where=ctx):
            return where.enter_context(nc.sbuf_tensor(name, shape, dt))

        ps = [ctx.enter_context(nc.psum_tensor(f"bank{b}", [P, 512], F32)) for b in range(8)]
        records = nc.dram_tensor("records", [(NU + 1) * UNIT, REC], F32)
        xup_dram = nc.dram_tensor("xup_dram", [N, 4 * MUL], F32)

        ident = sb("ident", [P, P])
        ones = sb("ones", [P, P])
        iota = sb("iota", [P, N])
        xs = sb("xs", [P, NB, D])
        xT = sb("xT", [P, KB, N])
        count = sb("count", [P, NB, N])
        nomask = sb("nomask", [P, NB, N])
        ln_stat = sb("ln_stat", [P, NB, 6])
        ln_mv = sb("ln_mv", [P, NB, 2])
        ln_std = sb("ln_std", [P, NB])
        ln_r = sb("ln_r", [P, NB])
        ubase = sb("ubase", [P, NU + 1], I32)
        s_stage = [sem(f"s_stage{b}") for b in range(2)]
        s_wh, s_split = sem("s_wh"), sem("s_split")
        s_b1 = sem("s_load_bias1")
        gamma_b = sb("gamma_b", [P, D])
        s_xbeta, s_xlast = sem("s_xbeta"), sem("s_xlast")
        s_gate_dve, s_gate_pool, s_gate_sp = sem("s_gate_dve"), sem("s_gate_pool"), sem("s_gate_sp")

        def psum4(b):
            return ps[b][:, :].rearrange("p (c n) -> p c n", c=4)

        def variances(dve, s, s_var, src_t):
            for c in range(NB):
                s.mark(dve.bn_stats(ln_stat[:, c, :], src_t[c]))
            s.wait()
            for c in range(NB):
                s.mark(dve.bn_aggr(ln_mv[:, c, :], ln_stat[:, c, :]))
            s.wait()
            dve.tensor_scalar(ln_std[:, :], ln_mv[:, :, 1], EPS, None, ALU.add).then_inc(s_var, 1)

        def root(act, s_var, s_std):
            act.wait_ge(s_var, 1)
            act.activation(ln_std[:, :], ln_std[:, :], ACT.Sqrt).then_inc(s_std, 1)

        def layernorm(dve, s, s_var, s_std, src_t, dst_t, s_done):
            variances(dve, s, s_var, [src_t[:, c, :] for c in range(NB)])
            dve.wait_ge(s_std, 1)
            s.link(dve.reciprocal(ln_r[:, :], ln_std[:, :]))
            for c in range(NB):
                dve.tensor_scalar(dst_t[:, c, :], src_t[:, c, :], ln_mv[:, c, 0:1], ln_r[:, c:c + 1],
                                  ALU.subtract, ALU.mult).then_inc(s_done, 1)

        lay1 = ExitStack()
        wA, wB, wC = ([sb(f"w{n}{part}", [P, KB, D], F32R, lay1) for part in ("_hi", "_lo")] for n in "ABC")
        stage = sb("stage", [P, 2, KB, D], F32, lay1)
        brow = sb("brow", [16, 3, P], F32, lay1)
        blin_row = sb("blin_row", [1, D], F32, lay1)
        beta_b = sb("beta_b", [P, D], F32, lay1)

        def stage_load(sp, i, job):
            h = (H1 - 1) - i
            sp.wait_ge(s_split, i * 5 + job + (5, 3, 4, 4, 4)[job])
            sp.sem_inc(s_gate_sp, 1)
            if job < 4:
                w = (wq, wk, wv, wskip)[job].rearrange("(k p) c -> p k c", p=P)[:, :, bass.ds(h * D, D)]
            else:
                w = wlin[bass.ds(h * D, D), :].rearrange("(k p) c -> p k c", p=P)
            sp.dma_start(stage[:, job % 2, :, :], w).then_inc(s_stage[job % 2], 16)

        def split_weights(pool, i, job):
            half, turn = job % 2, i * (3 - job % 2) + job // 2
            w = (wA, wB, wC, wA, wB)[job]
            pool.wait_ge(s_stage[half], turn * 16 + 16)
            pool.sem_inc(s_gate_pool, 1)
            pool.tensor_copy(w[0][:, :, :], stage[:, half, :, :]).then_inc(s_wh, 1)
            pool.wait_ge(s_wh, i * 5 + job + 1)
            pool.sem_inc(s_gate_pool, 1)
            pool.tensor_tensor(w[1][:, :, :], stage[:, half, :, :], w[0][:, :, :].bitcast(F32), ALU.subtract)\
                .then_inc(s_split, 1)

        with ExitStack() as c0:
            def t0(name, shape, dt=F32):
                return sb(name, shape, dt, c0)

            iota_i = t0("iota_i", [P, N], I32)
            iota_h = t0("iota_h", [P, N], F16)
            tri = t0("tri", [P, P])
            fill = t0("fill", [P, (NU + 1) * UNIT // P, REC])
            dst_i, src_i, tmp_i = (t0(n, [P, ET], I32) for n in ("dst_i", "src_i", "tmp_i"))
            dst_f, src_f, blk_f, loc_f, pos_f = (t0(n, [P, ET]) for n in ("dst_f", "src_f", "blk_f", "loc_f", "pos_f"))
            pos_i = t0("pos_i", [P, ET], I32)
            mask_g = t0("mask_g", [P, NB, ET])
            scan_g = t0("scan_g", [P, NB, ET])
            tot = t0("tot", [P, NB])
            sc = t0("sc", [P, 6, NB])
            sc_i = t0("sc_i", [P, 2, NB], I32)
            ub_f = t0("ub_f", [P, NU + 1])
            ef_sb = t0("ef_sb", [P, ET, 8])
            ea_sb = t0("ea_sb", [P, ET, 4])
            rec = t0("rec", [P, ET, REC])
            rbuf = t0("rbuf", [P, 2, 4, REC])
            ibuf = t0("ibuf", [P, 2, 4], I32)
            zero_b = t0("zero_b", [P, N], BF16)
            ohd = t0("ohd", [P, 4, N], BF16)
            ohs = t0("ohs", [P, 4, N], BF16)
            w0_sb = t0("w0_sb", [P, KB, D])
            w0T = t0("w0T", [P, KB, D])
            xh = t0("xh", [P, NB, H0 * F0])
            a_b = t0("a_b", [P, 2, H0, F0])
            prod = t0("prod", [P, 2, H0 * F0])
            sij = t0("sij", [P, 2, NB, H0])
            maskT = w0_sb
            diag = t0("diag", [P, NB, P])
            tsum = t0("tsum", [P, 2, N])
            esc = t0("esc", [P, 2, N])
            lsc = t0("lsc", [P, 2, N])
            emx = t0("emx", [P, 2])
            nmx = t0("nmx", [P, 4])
            ex = t0("ex", [P, 2, N])
            rsum = t0("rsum", [P, 4])
            rinv = t0("rinv", [P, 4])
            exT = t0("exT", [P, 2, NB, P])
            y0 = fill[:, :, :].rearrange("p r k -> p (r k)")[:, 0:NB * D].rearrange("p (c d) -> p c d", c=NB)

            s_idx, s_att, s_x, s_w0, s_a0, s_fill = (sem(n) for n in ("s_idx", "s_att", "s_x", "s_w0", "s_a0", "s_fill"))
            s_const, s_ident, s_iota, s_tot, s_off = (sem(n) for n in ("s_const", "s_ident", "s_iota", "s_tot", "s_off"))
            s_loc, s_pos, s_rec, s_cp = (sem(n) for n in ("s_loc", "s_pos", "s_rec", "s_cp"))
            s_sent = [sem(f"s_sent{b}") for b in range(2)]
            s_fillset, s_oh, s_ohfree, s_cnt, s_cs = (sem(n) for n in ("s_fillset", "s_oh", "s_ohfree", "s_cnt", "s_cs"))
            s_t0, s_t0c, s_xh, s_xhc, s_zero = (sem(n) for n in ("s_t0", "s_t0c", "s_xh", "s_xhc", "s_zero"))
            s_mT, s_mTc = sem("s_mT"), sem("s_mTc")
            s_v0, s_diag, s_sjb, s_ts, s_em, s_ex = (sem(n) for n in ("s_v0", "s_diag", "s_sjb", "s_ts", "s_em", "s_ex"))
            s_nm, s_xT, s_xTc, s_o, s_y, s_lm, s_ri = (sem(n) for n in ("s_nm", "s_xT", "s_xTc", "s_o", "s_y", "s_lm", "s_ri"))
            s_ln0, s_ln0r, s_lnx0, s_xT0, s_xT0c = (sem(n) for n in ("s_ln0", "s_ln0r", "s_lnx0", "s_xT0", "s_xT0c"))

            with nc.Block() as block:
                @block.sync
                def _(sp):
                    sp.dma_start(dst_i[:, :], dst.rearrange("(p t) -> p t", p=P)).then_inc(s_idx, 16)
                    sp.dma_start(src_i[:, :], src.rearrange("(p t) -> p t", p=P)).then_inc(s_idx, 16)
                    sp.dma_start(xs[:, :, :], x.rearrange("(c p) d -> p c d", p=P)).then_inc(s_x, 16)
                    sp.dma_start(w0_sb[:, :, :], w0.rearrange("h o i -> (h o) i").rearrange("(c p) i -> p c i", p=P))\
                        .then_inc(s_w0, 16)
                    for j in range(2):
                        sp.dma_start(a_b[:, j, :, :], a0[:, j * F0:(j + 1) * F0].partition_broadcast(P))\
                            .then_inc(s_a0, 16)
                    sp.dma_start(ef_sb[:, :, :], ef.rearrange("(p t) k -> p t k", p=P)).then_inc(s_att, 16)
                    sp.dma_start(ea_sb[:, :, :], ea.rearrange("(p t) k -> p t k", p=P)).then_inc(s_att, 16)
                    sp.wait_ge(s_fillset, 2)
                    sp.dma_start(records.ap().rearrange("(p r) k -> p r k", p=P), fill[:, :, :]).then_inc(s_fill, 16)
                    sp.sem_inc(s_split, 5)
                    for job in range(2):
                        stage_load(sp, 0, job)
                    for j, b in enumerate((bq, bk, bskip)):
                        sp.dma_start(brow[:, j, :], b.rearrange("(c p) -> c p", p=P)).then_inc(s_b1, 16)
                    sp.dma_start(blin_row[:, :], blin.rearrange("(a c) -> a c", a=1)).then_inc(s_b1, 16)
                    sp.dma_start(gamma_b[:, :], gamma.partition_broadcast(P)).then_inc(s_b1, 16)
                    sp.dma_start(beta_b[:, :], beta.partition_broadcast(P)).then_inc(s_b1, 16)
                    stage_load(sp, 0, 2)

                @block.gpsimd
                def _(pool):
                    pool.iota(iota_i[:, :], pattern=[[1, N]], base=0, channel_multiplier=0).then_inc(s_iota, 1)
                    pool.memset(ones[:, :], 1.0).then_inc(s_const, 1)
                    pool.memset(ident[:, :], 0.0).then_inc(s_const, 1)
                    pool.wait_ge(s_const, 2)
                    pool.affine_select(out=ident[:, :], in_=ident[:, :], compare_op=ALU.not_equal, fill=1.0, base=0,
                                       pattern=[[-1, P]], channel_multiplier=1).then_inc(s_ident, 1)
                    pool.affine_select(out=tri[:, :], in_=ones[:, :], compare_op=ALU.is_gt, fill=0.0, base=0,
                                       pattern=[[1, P]], channel_multiplier=-1).then_inc(s_ident, 1)
                    pool.memset(fill[:, :, :], 0.0).then_inc(s_fillset, 1)
                    pool.wait_ge(s_fillset, 1)
                    pool.memset(fill[:, :, 13:14], -1.0).then_inc(s_fillset, 1)
                    pool.memset(rec[:, :, 14:16], 0.0).then_inc(s_rec, 1)
                    pool.wait_ge(s_idx, 32)
                    pool.tensor_copy(rec[:, :, 12].bitcast(I32), src_i[:, :]).then_inc(s_rec, 1)
                    pool.wait_ge(s_att, 32)
                    pool.tensor_copy(rec[:, :, 0:8], ef_sb[:, :, :]).then_inc(s_rec, 1)
                    pool.tensor_copy(rec[:, :, 8:12], ea_sb[:, :, :]).then_inc(s_rec, 1)
                    pool.wait_ge(s_loc, 1)
                    pool.tensor_copy(rec[:, :, 13], loc_f[:, :]).then_inc(s_rec, 1)
                    pool.wait_ge(s_rec, 5)
                    pool.wait_ge(s_pos, 1)
                    pool.wait_ge(s_fill, 16)

                    def send(i, first):
                        for b in range(2):
                            if not first:
                                pool.wait_ge(s_sent[b], i * 64)
                            pool.tensor_copy(rbuf[:, b, :, :], rec[:, bass.ds(i * 8 + b * 4, 4), :]).then_inc(s_cp, 1)
                            pool.tensor_copy(ibuf[:, b, :], pos_i[:, bass.ds(i * 8 + b * 4, 4)]).then_inc(s_cp, 1)
                            pool.wait_ge(s_cp, i * 4 + b * 2 + 2)
                            pool.sem_inc(s_gate_pool, 1)
                            for k in range(4):
                                pool.indirect_dma_start(
                                    records.ap()[:, :],
                                    bass.IndirectOffsetOnAxis(ap=ibuf[:, b, k:k + 1], axis=0),
                                    rbuf[:, b, k, :], None).then_inc(s_sent[b], 16)

                    send(0, True)
                    with pool.Fori(1, ET // 8) as i:
                        send(i, False)
                    for b in range(2):
                        pool.wait_ge(s_sent[b], 64 * (ET // 8))
                    for job in range(3):
                        split_weights(pool, 0, job)

                @block.tensor
                def _(pe):
                    pe.wait_ge(s_ident, 1)
                    pe.wait_ge(s_x, 16)
                    pe.wait_ge(s_w0, 16)
                    n = 0
                    for t in (xs, w0_sb):
                        for k in range(KB):
                            if n >= 2:
                                pe.wait_ge(s_t0c, n - 1)
                            for c in range(NB):
                                mm = pe.transpose(ps[n % 2][:, c * P:(c + 1) * P], t[:, c, k * P:(k + 1) * P], ident[:, :])
                            mm.then_inc(s_t0, 1)
                            n += 1
                    pe.wait_ge(s_t0c, n)
                    for c in range(NB):
                        if c >= 2:
                            pe.wait_ge(s_xhc, c - 1)
                        for k in range(KB):
                            mm = pe.matmul(ps[c % 2][:, :], xT[:, k, c * P:(c + 1) * P], w0T[:, k, :],
                                           start=(k == 0), stop=(k == KB - 1))
                        mm.then_inc(s_xh, 1)
                    pe.wait_ge(s_ident, 2)
                    pe.wait_ge(s_tot, 1)
                    pe.matmul(ps[2][:, 0:NB], tri[:, :], tot[:, :], start=True, stop=True)
                    pe.matmul(ps[2][:, NB:2 * NB], ones[:, :], tot[:, :], start=True, stop=True).then_inc(s_off, 1)
                    pe.wait_ge(s_zero, 1)
                    for c in range(NB):
                        pe.matmul(ps[4 + c][:, :], zero_b[:, 0:P], zero_b[:, :], start=True, stop=False,
                                  skip_group_check=True)
                    pe.sem_inc(s_ohfree, 4)
                    pe.sem_inc(s_o, 2)
                    with pe.Fori(0, ET // 4) as i:
                        for k in range(4):
                            pe.wait_ge(s_oh, i * 4 + k + 1)
                            for c in range(NB):
                                mm = pe.matmul(ps[4 + c][:, :], ohd[:, k, c * P:(c + 1) * P], ohs[:, k, :],
                                               start=False, stop=False, skip_group_check=True)
                            mm.then_inc(s_ohfree, 1)
                    for c in range(NB):
                        mm = pe.matmul(ps[4 + c][:, :], zero_b[:, 0:P], zero_b[:, :], start=False, stop=True,
                                       skip_group_check=True)
                    mm.then_inc(s_cnt, 1)
                    pe.wait_ge(s_cs, 1)
                    for c in range(NB):
                        if c >= 2:
                            pe.wait_ge(s_mTc, c - 1)
                        for g in range(NB):
                            mm = pe.transpose(ps[c % 2][:, g * P:(g + 1) * P], count[:, g, c * P:(c + 1) * P], ident[:, :])
                        mm.then_inc(s_mT, 1)
                    def broadcast(h):
                        pe.wait_ge(s_diag, h + 1)
                        pe.wait_ge(s_ts, h * 4 + 4)
                        pe.matmul(ps[0][:, :], ones[:, :], diag[:, :, :].rearrange("p c n -> p (c n)"),
                                  start=True, stop=True).then_inc(s_sjb, 1)

                    def turn(h, c):
                        pe.wait_ge(s_ex, h * 4 + c + 3)
                        pe.wait_ge(s_xTc, h * 4 + c + 1)
                        for g in range(NB):
                            mm = pe.transpose(ps[2 + c % 2][:, g * P:(g + 1) * P], ex[:, c % 2, g * P:(g + 1) * P],
                                              ident[:, :])
                        mm.then_inc(s_xT, 1)

                    def neighbours(h, c):
                        pe.wait_ge(s_xTc, h * 4 + c + 3)
                        pe.wait_ge(s_y, h * 4 + c + 1)
                        for g in range(NB):
                            mm = pe.matmul(ps[4 + c % 2][:, 0:F0], exT[:, c % 2, g, :], xh[:, g, bass.ds(h * F0, F0)],
                                           start=(g == 0), stop=(g == NB - 1))
                        mm.then_inc(s_o, 1)

                    def head(h, first=False, last=False):
                        for c in range(NB):
                            turn(h, c)
                            if c:
                                neighbours(h, c - 1)
                            elif not first:
                                neighbours(h - 1, NB - 1)
                            if c == 1 and not last:
                                broadcast(h + 1)

                    broadcast(0)
                    head(0, first=True)
                    with pe.Fori(1, H0 - 1) as h:
                        head(h)
                    head(H0 - 1, last=True)
                    neighbours(H0 - 1, NB - 1)
                    pe.wait_ge(s_lnx0, NB)
                    for k in range(KB):
                        if k >= 2:
                            pe.wait_ge(s_xT0c, k - 1)
                        for c in range(NB):
                            mm = pe.transpose(ps[k % 2][:, c * P:(c + 1) * P], xs[:, c, k * P:(k + 1) * P], ident[:, :])
                        mm.then_inc(s_xT0, 1)

                @block.scalar
                def _(act):
                    act.sem_inc(s_ts, 4)
                    act.sem_inc(s_xTc, 2)
                    act.sem_inc(s_ex, 2)
                    for n in range(2 * KB):
                        act.wait_ge(s_t0, n + 1)
                        t = xT if n < KB else w0T
                        act.activation(t[:, n % KB, :], ps[n % 2][:, :], ACT.Copy).then_inc(s_t0c, 1)
                    for c in range(NB):
                        act.wait_ge(s_xh, c + 1)
                        act.activation(xh[:, c, :], ps[c % 2][:, :], ACT.Copy).then_inc(s_xhc, 1)

                    def tsum_step(h, c):
                        act.wait_ge(s_sjb, h + 1)
                        act.wait_ge(s_em, h * 4 + c + 1)
                        act.activation(tsum[:, c % 2, :], ps[0][:, :], ACT.Identity,
                                       bias=sij[:, 1, c, bass.ds(h, 1)]).then_inc(s_ts, 1)

                    def exp_step(h, c):
                        act.wait_ge(s_nm, h * 4 + c + 1)
                        act.activation(ex[:, c % 2, :], lsc[:, c % 2, :], ACT.Exp, bias=nmx[:, c:c + 1],
                                       accum_out=rsum[:, c:c + 1]).then_inc(s_ex, 1)

                    def evac_step(h, c):
                        act.wait_ge(s_xT, h * 4 + c + 1)
                        act.wait_ge(s_o, h * 4 + c + 1)
                        act.activation(exT[:, c % 2, :, :].rearrange("p g n -> p (g n)"), ps[2 + c % 2][:, :],
                                       ACT.Copy).then_inc(s_xTc, 1)

                    def head(h, first=False, last=False):
                        for c in range(NB):
                            exp_step(h, c)
                            if c:
                                evac_step(h, c - 1)
                            elif not first:
                                evac_step(h - 1, NB - 1)
                            if c < 2:
                                tsum_step(h, c + 2)
                            elif not last:
                                tsum_step(h + 1, c - 2)

                    tsum_step(0, 0)
                    tsum_step(0, 1)
                    head(0, first=True)
                    with act.Fori(1, H0 - 1) as h:
                        head(h)
                    head(H0 - 1, last=True)
                    evac_step(H0 - 1, NB - 1)
                    root(act, s_ln0, s_ln0r)
                    for k in range(KB):
                        act.wait_ge(s_xT0, k + 1)
                        act.activation(xT[:, k, :], ps[k % 2][:, :], ACT.Copy).then_inc(s_xT0c, 1)

                @block.vector
                def _(dve):
                    s = Steps(dve, s_v0)
                    dve.memset(zero_b[:, :], 0.0).then_inc(s_zero, 1)
                    dve.wait_ge(s_iota, 1)
                    s.mark(dve.tensor_copy(iota[:, :], iota_i[:, :]))
                    s.mark(dve.tensor_copy(iota_h[:, :], iota_i[:, :]))
                    dve.wait_ge(s_idx, 32)
                    s.mark(dve.tensor_copy(dst_f[:, :], dst_i[:, :]))
                    s.mark(dve.tensor_copy(src_f[:, :], src_i[:, :]))
                    s.link(dve.tensor_scalar(tmp_i[:, :], dst_i[:, :], P - 1, None, ALU.bitwise_and))
                    dve.tensor_copy(loc_f[:, :], tmp_i[:, :]).then_inc(s_loc, 1)
                    dve.wait_ge(s_loc, 1)
                    s.link(dve.tensor_scalar(tmp_i[:, :], dst_i[:, :], 7, None, ALU.logical_shift_right))
                    s.link(dve.tensor_copy(blk_f[:, :], tmp_i[:, :]))
                    dve.wait_ge(s_const, 2)
                    for g in range(NB):
                        s.mark(dve.tensor_scalar(mask_g[:, g, :], blk_f[:, :], float(g), None, ALU.is_equal))
                    s.wait()
                    for g in range(NB):
                        s.mark(dve.tensor_tensor_scan(scan_g[:, g, :], ones[:, :], mask_g[:, g, :], 0.0,
                                                      ALU.mult, ALU.add))
                    s.wait()
                    dve.tensor_copy(tot[:, :], scan_g[:, :, ET - 1]).then_inc(s_tot, 1)
                    dve.wait_ge(s_off, 1)
                    s.link(dve.tensor_scalar(sc_i[:, 0, :], ps[2][:, NB:2 * NB], float(UNIT - 1), None, ALU.add))
                    s.link(dve.tensor_scalar(sc_i[:, 1, :], sc_i[:, 0, :], 9, None, ALU.logical_shift_right))
                    s.link(dve.tensor_copy(sc[:, 0, :], sc_i[:, 1, :]))
                    s.link(dve.tensor_tensor_scan(sc[:, 1, :], ones[:, 0:NB], sc[:, 0, :], 0.0, ALU.mult, ALU.add))
                    s.link(dve.tensor_tensor(sc[:, 2, :], sc[:, 1, :], sc[:, 0, :], ALU.subtract))
                    s.link(dve.tensor_scalar(sc[:, 3, :], sc[:, 2, :], float(UNIT), -1.0, ALU.mult, ALU.add))
                    s.link(dve.tensor_tensor(sc[:, 4, :], ps[2][:, 0:NB], sc[:, 3, :], ALU.add))
                    for g in range(NB):
                        s.mark(dve.scalar_tensor_tensor(scan_g[:, g, :], scan_g[:, g, :], sc[:, 4, g:g + 1],
                                                        mask_g[:, g, :], ALU.add, ALU.mult))
                    s.wait()
                    s.link(dve.tensor_tensor(pos_f[:, :], scan_g[:, 0, :], scan_g[:, 1, :], ALU.add))
                    s.link(dve.tensor_tensor(pos_f[:, :], pos_f[:, :], scan_g[:, 2, :], ALU.add))
                    s.link(dve.tensor_tensor(pos_f[:, :], pos_f[:, :], scan_g[:, 3, :], ALU.add))
                    dve.tensor_copy(pos_i[:, :], pos_f[:, :]).then_inc(s_pos, 1)
                    s.link(dve.tensor_scalar(ub_f[:, :], iota[:, 0:NU + 1], sc[:, 2, 1:2], None, ALU.is_ge))
                    for g in (2, 3):
                        s.link(dve.scalar_tensor_tensor(ub_f[:, :], iota[:, 0:NU + 1], sc[:, 2, g:g + 1], ub_f[:, :],
                                                        ALU.is_ge, ALU.add))
                    s.link(dve.tensor_scalar(ubase[:, :], ub_f[:, :], 1024.0, None, ALU.mult))

                    with dve.Fori(0, ET // 4) as i:
                        for k in range(4):
                            dve.wait_ge(s_ohfree, i * 4 + k + 1)
                            dve.tensor_scalar(ohd[:, k, :], iota_h[:, :], dst_f[:, bass.ds(i * 4 + k, 1)], None,
                                              ALU.is_equal)
                            dve.tensor_scalar(ohs[:, k, :], iota_h[:, :], src_f[:, bass.ds(i * 4 + k, 1)], None,
                                              ALU.is_equal).then_inc(s_oh, 1)
                    dve.wait_ge(s_xhc, NB)
                    dve.wait_ge(s_a0, 32)
                    for c in range(NB):
                        for j in range(2):
                            s.mark(dve.tensor_tensor(prod[:, j, :], xh[:, c, :], a_b[:, j, :, :].rearrange("p h f -> p (h f)"), ALU.mult))
                        s.wait()
                        for j in range(2):
                            s.mark(dve.tensor_reduce(sij[:, j, c, :], prod[:, j, :].rearrange("p (h f) -> p h f", h=H0),
                                                     AX.X, ALU.add))
                        s.wait()
                    dve.wait_ge(s_cnt, 1)
                    for c in range(NB):
                        s.mark(dve.tensor_copy(count[:, c, :], ps[4 + c][:, :]))
                    s.wait()
                    for c in range(NB):
                        ins = dve.tensor_scalar(nomask[:, c, :], count[:, c, :], 0.0, NEG, ALU.is_equal, ALU.mult)
                    ins.then_inc(s_cs, 1)
                    for c in range(NB):
                        dve.wait_ge(s_mT, c + 1)
                        dve.tensor_scalar(maskT[:, c, :], ps[c % 2][:, :], 1.0, None, ALU.min).then_inc(s_mTc, 1)
                    dve.wait_ge(s_mTc, NB)
                    dve.wait_ge(s_fill, 16)
                    dve.sem_inc(s_em, 2)
                    dve.sem_inc(s_y, 2)

                    def diagonal(h):
                        dve.wait_ge(s_ts, h * 4 + 1)
                        dve.tensor_tensor(diag[:, :, :], ident[:, None, :].to_broadcast([P, NB, P]),
                                          sij[:, 0, :, bass.ds(h, 1)].to_broadcast([P, NB, P]), ALU.mult).then_inc(s_diag, 1)

                    def score(h, c):
                        dve.wait_ge(s_ts, h * 4 + c + 5)
                        dve.sem_inc(s_gate_dve, 1)
                        dve.tensor_tensor_reduce(esc[:, c % 2, :], tsum[:, c % 2, :], maskT[:, c, :], 1.0, -3.0e38,
                                                 ALU.mult, ALU.max, emx[:, c % 2:c % 2 + 1]).then_inc(s_em, 1)

                    def leaky(h, c):
                        dve.wait_ge(s_em, h * 4 + c + 3)
                        dve.wait_ge(s_ex, h * 4 + c + 1)
                        dve.scalar_tensor_tensor(nmx[:, c:c + 1], emx[:, c % 2:c % 2 + 1], 0.2,
                                                 emx[:, c % 2:c % 2 + 1], ALU.mult, ALU.max).then_inc(s_lm, 1)
                        dve.scalar_tensor_tensor(lsc[:, c % 2, :], esc[:, c % 2, :], 0.2, esc[:, c % 2, :],
                                                 ALU.mult, ALU.max)
                        dve.wait_ge(s_lm, h * 4 + c + 1)
                        dve.tensor_scalar(nmx[:, c:c + 1], nmx[:, c:c + 1], -1.0, None, ALU.mult).then_inc(s_nm, 1)

                    def result(h, c, part):
                        if part == 0:
                            dve.wait_ge(s_ex, h * 4 + c + 3)
                            dve.reciprocal(rinv[:, c:c + 1], rsum[:, c:c + 1]).then_inc(s_ri, 1)
                        else:
                            dve.wait_ge(s_ri, h * 4 + c + 1)
                            dve.wait_ge(s_o, h * 4 + c + 3)
                            dve.scalar_tensor_tensor(y0[:, c, bass.ds(h * F0, F0)], ps[4 + c % 2][:, 0:F0],
                                                     rinv[:, c:c + 1], xs[:, c, bass.ds(h * F0, F0)],
                                                     ALU.mult, ALU.add).then_inc(s_y, 1)

                    def head(h, first=False, last=False):
                        for c in range(NB):
                            ahead = (h, c + 1) if c < NB - 1 else (h + 1, 0)
                            behind = (h, c - 2) if c >= 2 else (h - 1, c + 2)
                            if not (last and c == NB - 1):
                                score(*ahead)
                            if not (first and c < 2):
                                result(*behind, 0)
                            if not (last and c == NB - 1):
                                leaky(*ahead)
                            if not (first and c < 2):
                                result(*behind, 1)
                            if c == 0 and not last:
                                diagonal(h + 1)

                    diagonal(0)
                    score(0, 0)
                    leaky(0, 0)
                    head(0, first=True)
                    with dve.Fori(1, H0 - 1) as h:
                        head(h)
                    head(H0 - 1, last=True)
                    for c in (2, 3):
                        for part in range(2):
                            result(H0 - 1, c, part)
                    dve.wait_ge(s_y, 4 * H0 + 2)
                    layernorm(dve, s, s_ln0, s_ln0r, y0, xs, s_lnx0)
        with ExitStack() as c1:
            def t1(name, shape, dt=F32):
                return sb(name, shape, dt, c1)

            SCALE1 = float(D) ** -0.5
            bvb = t1("bvb", [P, H1, D])
            bT = t1("bT", [P, 3, H1 * KB])
            xT_s, k_or_p, q_or_v, xa_s = ([t1(f"{n}{part}", [P, KB, N], F32R) for part in ("_hi", "_lo")]
                                          for n in ("xT", "k_or_p", "q_or_v", "xaT"))
            ident_r = t1("ident_r", [P, P], F32R)
            vt1 = t1("vt1", [P, 2, D])
            sm1 = t1("sm1", [P, 2, N])
            pr1 = t1("pr1", [P, 2, N])
            pc1 = t1("pc1", [P, 2, N])
            pn1 = t1("pn1", [P, NB, N])
            mx1 = t1("mx1", [P, 4])
            nm1 = t1("nm1", [P, 4])
            dn1 = t1("dn1", [P, 4])
            ri1 = t1("ri1", [P, 4])

            s_bv, s_bTp, s_bT, s_xs1 = (sem(n) for n in ("s_bv", "s_bTp", "s_bT", "s_xs1"))
            s_full, s_free, s_hi, s_nm1, s_e1, s_c1, s_n1 = (sem(n) for n in ("s_full", "s_free", "s_hi", "s_nm1", "s_e1", "s_c1", "s_n1"))
            s_vt, s_vlo, s_xl, s_d1 = (sem(n) for n in ("s_vt", "s_vlo", "s_xl", "s_d1"))

            GROUPS = 24
            GQ, GK, GS, GV, GT, GA = range(0, GROUPS, 4)
            HQ, HK, HV, HT, HA = range(0, 20, 4)

            with nc.Block() as block:
                @block.sync
                def _(sp):
                    sp.dma_start(bvb[:, :, :], bv.rearrange("(h c) -> h c", h=H1).partition_broadcast(P)).then_inc(s_bv, 16)
                    stage_load(sp, 0, 3)
                    stage_load(sp, 0, 4)
                    with sp.Fori(1, H1) as i:
                        for job in range(5):
                            stage_load(sp, i, job)

                @block.gpsimd
                def _(pool):
                    def split_next(i, job):
                        if job == 0:
                            pool.wait_ge(s_full, i * GROUPS + 1)
                        if job == 1:
                            pool.wait_ge(s_xl, i + 1)
                        if job == 3:
                            pool.wait_ge(s_full, i * GROUPS + GQ + 3 + 2)
                        if job == 4:
                            pool.wait_ge(s_full, i * GROUPS + GK + 3 + 2)
                        split_weights(pool, i, job)

                    split_next(0, 3)
                    split_next(0, 4)
                    pool.wait_ge(s_b1, 96)
                    pool.tensor_tensor(xs[:, :, :], xs[:, :, :], beta_b[:, None, :].to_broadcast([P, NB, D]), ALU.add)\
                        .then_inc(s_xbeta, 1)
                    with pool.Fori(1, H1) as i:
                        for job in range(5):
                            split_next(i, job)

                @block.tensor
                def _(pe):
                    pe.sem_inc(s_full, 1)
                    pe.sem_inc(s_xl, 1)
                    pe.wait_ge(s_b1, 96)
                    for j in range(3):
                        mm = pe.transpose(ps[4][:, j * 16:(j + 1) * 16], brow[:, j, :], ident[0:16, 0:16])
                    mm.then_inc(s_bTp, 1)
                    for c in range(NB):
                        pe.matmul(ps[c][:, :], ones[0:1, :], blin_row[:, :], start=True, stop=False, skip_group_check=True)
                    pe.wait_ge(s_bT, 2)
                    pe.wait_ge(s_xs1, 2)

                    def product(bank, left, lcols, right, start=True, stop=True, wait_last=None):
                        for k in range(KB):
                            if k == KB - 1 and wait_last:
                                wait_last()
                            for n, (a, b) in enumerate(SPLIT_PASSES):
                                mm = pe.matmul(bank, left[a][:, k, lcols], right[b][:, k, :],
                                               start=(start and k == 0 and n == 0),
                                               stop=(stop and k == KB - 1 and n == len(SPLIT_PASSES) - 1),
                                               skip_group_check=True)
                        return mm

                    with pe.Fori(0, H1) as i:
                        def bank_free(group):
                            pe.wait_ge(s_free, i * GROUPS + group + 1)

                        def taken(group):
                            pe.wait_ge(s_free, i * GROUPS + group + 1 + 4)

                        for job, w, base in ((0, wA, GQ), (1, wB, GK)):
                            pe.wait_ge(s_split, i * 5 + job + 6)
                            for c in range(KB):
                                bank_free(base + c)
                                product(ps[4 + c][:, :], w, slice(c * P, (c + 1) * P), xT_s).then_inc(s_full, 1)
                        for c in range(NB):
                            bank_free(GS + c)
                            if c == 0:
                                taken(GK + 2)
                            product(ps[4 + c][:, :], q_or_v, slice(c * P, (c + 1) * P), k_or_p,
                                    wait_last=(lambda: taken(GK + 3)) if c == 0 else None).then_inc(s_full, 1)
                        pe.wait_ge(s_split, i * 5 + 2 + 6)
                        for c in range(NB):
                            bank_free(GV + c)
                            product(ps[4 + c][:, :], xT_s, slice(c * P, (c + 1) * P), wC).then_inc(s_full, 1)
                        for c in range(NB):
                            pe.wait_ge(s_n1, i * 4 + c + 3)
                            bank_free(GT + c)
                            for g in range(NB):
                                mm = pe.transpose(ps[4 + c][:, g * P:(g + 1) * P], pn1[:, c, g * P:(g + 1) * P],
                                                  ident[:, :])
                            mm.then_inc(s_full, 1)
                        pe.wait_ge(s_split, i * 5 + 3 + 6)
                        for c in range(KB):
                            bank_free(GA + c)
                            product(ps[4 + c][:, :], wA, slice(c * P, (c + 1) * P), xT_s, stop=False)
                            if c == 1:
                                taken(GT + 3)
                                pe.wait_ge(s_vlo, i * 4 + 4)
                            for a in ((), (0, 1), (2,), (3,))[c]:
                                product(ps[4 + a][:, :], q_or_v, slice(a * P, (a + 1) * P), k_or_p, start=False)\
                                    .then_inc(s_full, 1)
                        pe.wait_ge(s_split, i * 5 + 4 + 6)
                        taken(GA + 2)
                        for c in range(NB):
                            mm = product(ps[c][:, :], xa_s, slice(c * P, (c + 1) * P), wB, start=False, stop=False,
                                         wait_last=(lambda: taken(GA + 3)) if c == 0 else None)
                        mm.then_inc(s_xl, 1)
                    for c in range(NB):
                        for k in range(KB):
                            for part in range(2):
                                mm = pe.matmul(ps[c][:, k * P:(k + 1) * P], xa_s[part][:, k, c * P:(c + 1) * P], ident_r[:, :],
                                               start=False, stop=(k == KB - 1 and part == 1), skip_group_check=True)
                    mm.then_inc(s_xlast, 1)

                @block.scalar
                def _(act):
                    act.activation(xT_s[0][:, :, :], xT[:, :, :], ACT.Copy).then_inc(s_xs1, 1)
                    act.activation(ident_r[:, :], ident[:, :], ACT.Copy).then_inc(s_bT, 1)
                    act.wait_ge(s_bTp, 1)
                    act.activation(bT[:, :, :].rearrange("p a b -> p (a b)"), ps[4][:, 0:48], ACT.Copy).then_inc(s_bT, 1)
                    act.wait_ge(s_bT, 2)
                    with act.Fori(0, H1) as i:
                        h = act.snap((H1 - 1) - i)
                        for j, (t, base) in enumerate(((q_or_v, GQ), (k_or_p, GK))):
                            for c in range(KB):
                                act.wait_ge(s_full, i * GROUPS + base + c + 2)
                                act.activation(t[0][:, c, :], ps[4 + c][:, :], ACT.Identity,
                                               bias=bT[:, j, bass.ds(h * KB + c, 1)]).then_inc(s_hi, 1)

                        def scaled(c):
                            act.wait_ge(s_c1, i * 4 + c + 3)
                            act.activation(pn1[:, c, :], pc1[:, c % 2, :], ACT.Copy, scale=ri1[:, c:c + 1])\
                               .then_inc(s_n1, 1)

                        for c in range(NB):
                            act.wait_ge(s_nm1, i * 4 + c + 1)
                            act.wait_ge(s_c1, i * 4 + c + 1)
                            act.activation(pr1[:, c % 2, :], sm1[:, c % 2, :], ACT.Exp, bias=nm1[:, c:c + 1],
                                           scale=SCALE1).then_inc(s_e1, 1)
                            if c >= 1:
                                scaled(c - 1)
                        scaled(NB - 1)
                        for c in range(NB):
                            act.wait_ge(s_vt, i * 4 + c + 1)
                            act.activation(q_or_v[0][:, c, :], vt1[:, c % 2, :], ACT.Copy).then_inc(s_hi, 1)
                        for c in range(NB):
                            act.wait_ge(s_full, i * GROUPS + GT + c + 2)
                            act.activation(k_or_p[0][:, :, c * P:(c + 1) * P], psum4(4 + c), ACT.Copy).then_inc(s_hi, 1)
                        for c in range(KB):
                            act.wait_ge(s_full, i * GROUPS + GA + c + 2)
                            act.activation(xa_s[0][:, c, :], ps[4 + c][:, :], ACT.Identity,
                                           bias=bT[:, 2, bass.ds(h * KB + c, 1)]).then_inc(s_hi, 1)

                @block.vector
                def _(dve):
                    dve.sem_inc(s_free, 4)
                    dve.sem_inc(s_c1, 2)
                    dve.sem_inc(s_e1, 2)
                    dve.sem_inc(s_n1, 2)
                    dve.wait_ge(s_xs1, 1)
                    dve.tensor_tensor(xT_s[1][:, :, :], xT[:, :, :], xT_s[0][:, :, :].bitcast(F32), ALU.subtract)\
                       .then_inc(s_xs1, 1)
                    dve.wait_ge(s_bT, 2)
                    with dve.Fori(0, H1) as i:
                        h = dve.snap((H1 - 1) - i)
                        v = Steps(dve, s_d1, i, 12)

                        def low(t, base, hi_base, bias):
                            for c in range(KB):
                                dve.wait_ge(s_hi, i * 20 + hi_base + c + 1)
                                dve.sem_inc(s_gate_dve, 1)
                                dve.scalar_tensor_tensor(t[1][:, c, :], ps[4 + c][:, :], bT[:, bias, bass.ds(h * KB + c, 1)],
                                                         t[0][:, c, :].bitcast(F32), ALU.add, ALU.subtract).then_inc(s_free, 1)

                        low(q_or_v, GQ, HQ, 0)
                        low(k_or_p, GK, HK, 1)

                        def score(c):
                            dve.wait_ge(s_full, i * GROUPS + GS + c + 2)
                            dve.wait_ge(s_e1, i * 4 + c + 1)
                            dve.sem_inc(s_gate_dve, 1)
                            dve.tensor_tensor_reduce(sm1[:, c % 2, :], ps[4 + c][:, :], nomask[:, c, :], 1.0, -3.0e38,
                                                     ALU.add, ALU.max, mx1[:, c:c + 1]).then_inc(s_free, 1)
                            dve.wait_ge(s_free, i * GROUPS + GS + c + 5)
                            dve.tensor_scalar(nm1[:, c:c + 1], mx1[:, c:c + 1], -SCALE1, None, ALU.mult).then_inc(s_nm1, 1)

                        def weigh(c):
                            dve.wait_ge(s_e1, i * 4 + c + 3)
                            dve.wait_ge(s_n1, i * 4 + c + 1)
                            dve.sem_inc(s_gate_dve, 1)
                            v.link(dve.tensor_tensor_reduce(pc1[:, c % 2, :], pr1[:, c % 2, :], count[:, c, :], 1.0, 0.0,
                                                            ALU.mult, ALU.add, dn1[:, c:c + 1]))
                            v.link(dve.tensor_scalar(dn1[:, c:c + 1], dn1[:, c:c + 1], 1.0e-30, None, ALU.max))
                            v.link(dve.reciprocal(ri1[:, c:c + 1], dn1[:, c:c + 1]))
                            dve.sem_inc(s_c1, 1)

                        score(0)
                        score(1)
                        weigh(0)
                        score(2)
                        weigh(1)
                        score(3)
                        weigh(2)
                        weigh(3)
                        v.done()
                        dve.wait_ge(s_bv, 16)

                        def v_low(c):
                            dve.wait_ge(s_hi, i * 20 + HV + c + 1)
                            dve.tensor_tensor(q_or_v[1][:, c, :], vt1[:, c % 2, :], q_or_v[0][:, c, :].bitcast(F32),
                                              ALU.subtract).then_inc(s_vlo, 1)

                        for c in range(NB):
                            if c >= 2:
                                v_low(c - 2)
                                dve.wait_ge(s_vlo, i * 4 + c - 1)
                            dve.wait_ge(s_full, i * GROUPS + GV + c + 2)
                            dve.sem_inc(s_gate_dve, 1)
                            dve.tensor_tensor(vt1[:, c % 2, :], ps[4 + c][:, :], bvb[:, bass.ds(h, 1), :].rearrange("p a c -> p (a c)"),
                                              ALU.add).then_inc(s_vt, 1)
                            dve.wait_ge(s_vt, i * 4 + c + 1)
                            dve.sem_inc(s_free, 1)
                        v_low(2)
                        v_low(3)
                        for c in range(NB):
                            dve.wait_ge(s_hi, i * 20 + HT + c + 1)
                            dve.tensor_tensor(k_or_p[1][:, :, c * P:(c + 1) * P], psum4(4 + c),
                                              k_or_p[0][:, :, c * P:(c + 1) * P].bitcast(F32), ALU.subtract).then_inc(s_free, 1)
                        low(xa_s, GA, HA, 2)
        lay1.close()

        lay3 = ExitStack()
        w31_sb = sb("w31_sb", [P, KB, W3], F32, lay3)
        w32_sb = sb("w32_sb", [P, W3 // P, W3], F32, lay3)
        fcw_sb = sb("fcw_sb", [P, W3 // P, D], F32, lay3)
        fcb_b = sb("fcb_b", [P, D], F32, lay3)
        b3row = sb("b3row", [W3 // P, 2, P], F32, lay3)
        s_w3 = [sem(f"s_w3_{n}") for n in range(3)]
        s_b3 = sem("s_b3")

        with ExitStack() as c2:
            def t2(name, shape, dt=F32):
                return sb(name, shape, dt, c2)

            wup = t2("wup", [P, 2, MUL])
            wmA = t2("wmA", [8, HID])
            wmB = t2("wmB", [HID, HID])
            wmC = t2("wmC", [HID, 2, HID])
            wm4_sb = t2("wm4_sb", [P, 4 * MUL])
            wm4_s = [t2(f"wm4{part}", [P, 4 * MUL], F32R) for part in ("_hi", "_lo")]
            wout = t2("wout", [P, 2, 2, MUL])
            uT = t2("uT", [P, 4, N])
            xup = t2("xup", [P, NB, 4 * MUL])
            rb = t2("rb", [P, 2, 4, REC])
            ra = t2("ra", [P, 2, 4, REC])
            sg = t2("sg", [P, 2, 4, 4 * MUL])
            efT = t2("efT", [8, UNIT])
            hA = t2("hA", [HID, UNIT])
            hB = t2("hB", [HID, UNIT])
            hC = t2("hC", [P, UNIT])
            upper = t2("upper", [P, 1])
            h3 = t2("h3", [P, 2, UNIT], F32R)
            oh = t2("oh", [P, 2, P])
            ohy = t2("ohy", [P, 2, 4, P])
            msg = t2("msg", [P, 2, 6, MUL])
            part4 = t2("part4", [P, 2, 3, MUL])
            dot = t2("dot", [P, 4, MUL])
            acc = t2("acc", [P, NB * 8 * MUL])
            mT = sg[:, :, :, :].rearrange("p b k d -> p (b k) d")
            y2 = uT

            s_w2, s_uT, s_uTc, s_up, s_upc, s_xup = (sem(n) for n in ("s_w2", "s_uT", "s_uTc", "s_up", "s_upc", "s_xup"))
            s_rl = [sem(f"s_rl{b}") for b in range(2)]
            s_ra = [sem(f"s_ra{b}") for b in range(2)]
            s_sg = [[sem(f"s_sg{b}{k}") for k in range(4)] for b in range(2)]
            s_h3, s_part4, s_dot, s_dotp, s_rows2 = (sem(n) for n in ("s_h3", "s_part4", "s_dot", "s_dotp", "s_rows2"))
            s_m, s_mc, s_w, s_msg, s_sc, s_fl, s_d2 = (sem(n) for n in ("s_m", "s_mc", "s_w", "s_msg", "s_sc", "s_fl", "s_d2"))
            s_mT2, s_mT2c, s_o2, s_o2c = (sem(n) for n in ("s_mT2", "s_mT2c", "s_o2", "s_o2c"))
            s_h1v, s_x2, s_x3in, s_wm, s_acc, s_upd, s_upper = (
                sem(n) for n in ("s_h1v", "s_x2", "s_x3in", "s_wm", "s_acc", "s_upd", "s_upper"))
            s_ln1a, s_ln1ar, s_ln1b, s_ln1br, s_ln2, s_ln2r = (
                sem(n) for n in ("s_ln1a", "s_ln1ar", "s_ln1b", "s_ln1br", "s_ln2", "s_ln2r"))
            s_w4, s_gate_pe = (sem(n) for n in ("s_w4", "s_gate_pe"))
            LOOPS = (NU - 1) // 2
            assert NU == 2 * LOOPS + 1

            with nc.Block() as block:
                @block.sync
                def _(sp):
                    def load(u, b, to, ready):
                        sp.dma_start(to[:, b, :, :], records.ap()[bass.ds(u * UNIT, UNIT), :].rearrange("(p t) k -> p t k", p=P))\
                            .then_inc(ready[b], 16)

                    load(0, 0, ra, s_ra)
                    sp.dma_start(wmA[:, :], wm1).then_inc(s_wm, 16)
                    sp.dma_start(wmB[:, :], wm2).then_inc(s_wm, 16)
                    for half in range(2):
                        sp.dma_start(wmC[:, half, :], wm3).then_inc(s_wm, 16)
                    load(1, 1, ra, s_ra)
                    sp.dma_start(wup[:, 0, :], wup0).then_inc(s_w2, 16)
                    sp.dma_start(wup[:, 1, :], wup1).then_inc(s_w2, 16)
                    for half in range(2):
                        sp.dma_start(wm4_sb[half * HID:(half + 1) * HID, :], wm4).then_inc(s_w2, 16)
                    for j, w in enumerate((wout0, wout1)):
                        sp.dma_start(wout[:, j, :, :], w.rearrange("(k p) v -> p k v", p=P)).then_inc(s_w2, 16)

                    def loads(u, b):
                        sp.wait_ge(s_m, u * 4 - 7)
                        sp.sem_inc(s_gate_sp, 1)
                        load(u, b, ra, s_ra)
                        sp.wait_ge(s_msg, u * 4 + 4)
                        sp.sem_inc(s_gate_sp, 1)
                        load(u, b, rb, s_rl)

                    for b in range(2):
                        load(b, b, rb, s_rl)
                    for c in range(NB):
                        sp.wait_ge(s_upd if c % 2 else s_upc, c // 2 + 1)
                        sp.dma_start(xup_dram.ap()[c * P:(c + 1) * P, :], xup[:, c, :]).then_inc(s_xup, 16)
                    sp.dma_start(fcb_b[:, :], fcb.partition_broadcast(P)).then_inc(s_b3, 16)
                    sp.dma_start(b3row[:, 0, :], b31.rearrange("(c p) -> c p", p=P)).then_inc(s_b3, 16)
                    sp.dma_start(b3row[:, 1, :], b32.rearrange("(c p) -> c p", p=P)).then_inc(s_b3, 16)

                    def weights3(w_sb, w, k, ready):
                        sp.dma_start(w_sb[:, bass.ds(k, 1), :].rearrange("p a c -> p (a c)"), w[bass.ds(k * P, P), :])\
                            .then_inc(ready, 16)

                    assert LOOPS - 1 >= W3 // P >= KB
                    with sp.Fori(0, KB) as j:
                        loads(j * 2 + 2, 0)
                        weights3(w31_sb, w31, j, s_w3[0])
                        loads(j * 2 + 3, 1)
                        weights3(w32_sb, w32, j, s_w3[1])
                        weights3(fcw_sb, fcw, j, s_w3[2])
                    with sp.Fori(KB, W3 // P) as j:
                        loads(j * 2 + 2, 0)
                        weights3(w32_sb, w32, j, s_w3[1])
                        loads(j * 2 + 3, 1)
                        weights3(fcw_sb, fcw, j, s_w3[2])
                    with sp.Fori(W3 // P, LOOPS - 1) as j:
                        loads(j * 2 + 2, 0)
                        loads(j * 2 + 3, 1)
                    loads(NU - 1, 0)

                @block.gpsimd
                def _(pool):
                    def gather(turn, b, k):
                        if k == 0:
                            pool.wait_ge(s_rl[b], turn * 16 + 16)
                            pool.sem_inc(s_gate_pool, 1)
                        pool.indirect_dma_start(sg[:, b, k, :], None, xup_dram.ap()[:, :],
                                                bass.IndirectOffsetOnAxis(ap=rb[:, b, k, 12:13].bitcast(I32), axis=0))\
                            .then_inc(s_sg[b][k], 16)

                    def dots(u, k):
                        p = part4[:, k % 2, :, :]
                        pool.wait_ge(s_part4, u * 4 + k + 1)
                        pool.tensor_tensor(p[:, 0, :], p[:, 0, :], p[:, 1, :], ALU.add).then_inc(s_dotp, 1)
                        pool.wait_ge(s_dotp, u * 4 + k + 1)
                        pool.wait_ge(s_msg, u * 4 + k + 5)
                        pool.tensor_tensor(dot[:, k, :], p[:, 0, :], p[:, 2, :], ALU.add).then_inc(s_dot, 1)

                    def low_h3(u, b):
                        pool.wait_ge(s_mc, u * 5 + 5)
                        pool.tensor_tensor(h3[:, b, :], hC[:, :], h3[:, b, :].bitcast(F32), ALU.subtract)\
                            .then_inc(s_h3, 1)

                    def finish(signal, value):
                        pool.wait_ge(signal, value)
                        pool.sem_inc(s_gate_pool, 1)

                    def unit(u, next_turn, b, more):
                        dots(u, 2)
                        if more:
                            finish(s_dot, u * 4 + 5)
                            gather(next_turn, 1 - b, 0)
                        dots(u, 3)
                        if more:
                            finish(s_dot, u * 4 + 6)
                            gather(next_turn, 1 - b, 1)
                            gather(next_turn, 1 - b, 2)
                            low_h3(u + 1, 1 - b)
                            dots(u + 1, 0)
                            finish(s_dot, u * 4 + 7)
                            gather(next_turn, 1 - b, 3)
                            dots(u + 1, 1)

                    pool.memset(acc[:, :], 0.0).then_inc(s_acc, 1)
                    low_h3(0, 0)
                    finish(s_h3, 2)
                    pool.wait_ge(s_xup, 16 * NB)
                    for k in range(4):
                        gather(0, 0, k)
                    dots(0, 0)
                    dots(0, 1)
                    unit(0, 0, 0, True)
                    with pool.Fori(0, LOOPS - 1) as j:
                        unit(j * 2 + 1, j + 1, 1, True)
                        unit(j * 2 + 2, j + 1, 0, True)
                    unit(NU - 2, LOOPS, 1, True)
                    unit(NU - 1, 0, 0, False)
                    for k in range(4):
                        pool.wait_ge(s_sg[0][k], 16 * (LOOPS + 1))
                        pool.wait_ge(s_sg[1][k], 16 * LOOPS)

                def up_features(pe):
                    for c in range(NB):
                        pe.wait_ge(s_x2, c + 1)
                        for m in range(4):
                            part = xs[:, c, 0:MUL] if m == 0 else xs[:, c, MUL + m - 1:D:3]
                            mm = pe.transpose(ps[m][:, c * P:(c + 1) * P], part, ident[:, :])
                    mm.then_inc(s_uT, 1)
                    pe.wait_ge(s_w2, 16 * 6)
                    pe.wait_ge(s_uTc, 4)
                    for c in range(NB):
                        for m in range(4):
                            mm = pe.matmul(ps[c][:, m * MUL:(m + 1) * MUL], uT[:, m, c * P:(c + 1) * P],
                                           wup[:, min(m, 1), :], start=True, stop=True)
                        mm.then_inc(s_up, 1)
                    pe.wait_ge(s_upc, 2)
                    pe.wait_ge(s_upd, 2)

                @block.tensor
                def _(pe):
                    def edge_mlp(u, turn, b, step):
                        if step == 0:
                            pe.wait_ge(s_ra[b], turn * 16 + 16)
                            if not isinstance(turn, int) or u > 0:
                                pe.wait_ge(s_mc, u * 5 - 1)
                            for k in range(4):
                                mm = pe.transpose(ps[6][0:8, k * P:(k + 1) * P], ra[:, b, k, 0:8], ident[:, :])
                        else:
                            pe.wait_ge(s_mc, u * 5 + step)
                            pe.sem_inc(s_gate_pe, 1)
                            w, t = ((wmA[:, :], efT), (wmB[:, :], hA), (wmC[:, :, :].rearrange("p a c -> p (a c)"), hB))[step - 1]
                            mm = pe.matmul(ps[6 + step % 2][0:w.shape[1], :], w, t[:, :], start=True, stop=True)
                        mm.then_inc(s_m, 1)

                    def weights(u, b, k):
                        if k == 0:
                            pe.wait_ge(s_h3, u + 2)
                        pe.wait_ge(s_msg, u * 4 + k + 7)
                        for part in range(2):
                            mm = pe.matmul(ps[4 + k % 2][:, :], h3[:, b, k * P:(k + 1) * P], wm4_s[part][:, :],
                                           start=(part == 0), stop=(part == 1))
                        mm.then_inc(s_w, 1)

                    def scatter(u, b, k):
                        if k == 0:
                            pe.wait_ge(s_fl, u + 1)
                        pe.wait_ge(s_msg, u * 4 + k + 9)
                        pe.matmul(ps[2 * b][:, :], ohy[:, k % 2, 0, :], msg[:, k % 2, 0:4, :].rearrange("p a v -> p (a v)"),
                                  start=(k == 0), stop=(k == 3))
                        for m in range(4):
                            rows = oh[:, k % 2, :] if m == 0 else ohy[:, k % 2, m, :]
                            mm = pe.matmul(ps[2 * b + 1][:, m * MUL:(m + 1) * MUL], rows, msg[:, k % 2, 4 if m else 5, :],
                                           start=(k == 0 and m == 0), stop=(k == 3 and m == 3), skip_group_check=True)
                        mm.then_inc(s_sc, 1)

                    def unit(u, turn, b, more=True, more2=True):
                        for k in range(4):
                            if k < 3:
                                weights(u, b, k + 1)
                            elif more:
                                weights(u + 1, 1 - b, 0)
                            if k < 2 and more:
                                edge_mlp(u + 1, 0, 1 - b, k + 2)
                            if k >= 2 and more2:
                                edge_mlp(u + 2, turn + 1, b, k - 2)
                            scatter(u, b, k)

                    pe.wait_ge(s_wm, 16 * 4)
                    for step in range(4):
                        edge_mlp(0, 0, 0, step)
                    up_features(pe)
                    pe.wait_ge(s_w4, 1)
                    edge_mlp(1, 0, 1, 0)
                    edge_mlp(1, 0, 1, 1)
                    weights(0, 0, 0)
                    unit(0, 0, 0)
                    with pe.Fori(0, LOOPS - 1) as j:
                        unit(j * 2 + 1, j, 1)
                        unit(j * 2 + 2, j + 1, 0)
                    unit(NU - 2, 0, 1, more2=False)
                    unit(NU - 1, 0, 0, more=False, more2=False)
                    pe.wait_ge(s_fl, NU + 2)
                    for m in range(8):
                        if m >= 2:
                            pe.wait_ge(s_mT2c, m - 1)
                        for g in range(NB):
                            col = (g * 8 + m) * MUL
                            mm = pe.transpose(ps[4 + m % 2][:, g * P:(g + 1) * P], acc[:, col:col + MUL], ident[:, :])
                        mm.then_inc(s_mT2, 1)
                    pe.wait_ge(s_mT2c, 8)
                    for c in range(NB):
                        if c >= 2:
                            pe.wait_ge(s_o2c, c - 1)
                        for m in range(4):
                            a, b = (3, 4) if m == 0 else (4 + m, m - 1)
                            for half, blk in enumerate((a, b)):
                                mm = pe.matmul(ps[c % 2][:, m * MUL:(m + 1) * MUL], mT[:, blk, c * P:(c + 1) * P],
                                               wout[:, min(m, 1), half, :], start=(half == 0), stop=(half == 1))
                        mm.then_inc(s_o2, 1)

                @block.scalar
                def _(act):
                    act.sem_inc(s_msg, 8)
                    act.sem_inc(s_sc, 2)
                    act.sem_inc(s_fl, 2)
                    act.sem_inc(s_h3, 1)
                    act.sem_inc(s_dot, 2)
                    def edge_mlp(u, b, step):
                        act.wait_ge(s_m, u * 4 + step + 1)
                        src_ps = ps[6 + step % 2]
                        if step == 0:
                            act.activation(efT[:, :], src_ps[0:8, :], ACT.Copy).then_inc(s_mc, 1)
                        elif step < 3:
                            act.activation((hA, hB)[step - 1][:, :], src_ps[0:HID, :], ACT.Silu,
                                           scale=(8 ** -0.5, SILU_2MOM * HID ** -0.5)[step - 1]).then_inc(s_mc, 1)
                        else:
                            act.wait_ge(s_h3, u + 1)
                            act.activation(hC[:, :], src_ps[:, :], ACT.Silu, scale=SILU_2MOM * HID ** -0.5).then_inc(s_mc, 1)
                            act.wait_ge(s_mc, u * 5 + 4)
                            act.activation(h3[:, b, :], hC[:, :], ACT.Copy, scale=upper[:, :]).then_inc(s_mc, 1)

                    def products(u, turn, b, k):
                        act.wait_ge(s_rl[b], turn * 16 + 16)
                        act.wait_ge(s_sg[b][k], turn * 16 + 16)
                        act.wait_ge(s_dot, u * 4 + k + 1)
                        for m in range(3):
                            ins = act.activation(part4[:, k % 2, m, :], sg[:, b, k, (1 + m) * MUL:(2 + m) * MUL], ACT.Copy,
                                                 scale=rb[:, b, k, 9 + m:10 + m])
                        ins.then_inc(s_part4, 1)

                    def unit(u, turn, next_turn, b, more=True, more2=True):
                        for k in range(4):
                            if k < 2:
                                products(u, turn, b, k + 2)
                                if more:
                                    edge_mlp(u + 1, 1 - b, k + 2)
                            elif more:
                                products(u + 1, next_turn, 1 - b, k - 2)
                                if more2:
                                    edge_mlp(u + 2, b, k - 2)

                    root(act, s_ln1a, s_ln1ar)
                    act.wait_ge(s_upper, 2)
                    for step in range(4):
                        edge_mlp(0, 0, step)
                    root(act, s_ln1b, s_ln1br)
                    act.wait_ge(s_uT, 1)
                    for m in (0, 1):
                        act.activation(uT[:, m, :], ps[m][:, :], ACT.Copy).then_inc(s_uTc, 1)
                    for c in (0, 2):
                        act.wait_ge(s_up, c + 1)
                        act.activation(xup[:, c, :], ps[c][:, :], ACT.Copy, scale=MUL ** -0.5).then_inc(s_upc, 1)
                    edge_mlp(1, 1, 0)
                    edge_mlp(1, 1, 1)
                    products(0, 0, 0, 0)
                    products(0, 0, 0, 1)
                    unit(0, 0, 0, 0)
                    with act.Fori(0, LOOPS - 1) as j:
                        unit(j * 2 + 1, j, j + 1, 1)
                        unit(j * 2 + 2, j + 1, j + 1, 0)
                    unit(NU - 2, LOOPS - 1, LOOPS, 1, more2=False)
                    unit(NU - 1, LOOPS, 0, 0, more=False, more2=False)
                    for m in range(8):
                        act.wait_ge(s_mT2, m + 1)
                        act.activation(mT[:, m, :], ps[4 + m % 2][:, :], ACT.Copy).then_inc(s_mT2c, 1)
                    root(act, s_ln2, s_ln2r)

                @block.vector
                def _(dve):
                    dve.memset(upper[0:HID, :], 0.0).then_inc(s_upper, 1)
                    dve.memset(upper[HID:P, :], 1.0).then_inc(s_upper, 1)
                    h1 = uT
                    s = Steps(dve, s_h1v)
                    dve.wait_ge(s_xlast, 1)
                    variances(dve, s, s_ln1a, [ps[c][:, :] for c in range(NB)])
                    for c in range(NB):
                        s.mark(dve.scalar_tensor_tensor(h1[:, c, :], ps[c][:, :], ln_mv[:, c, 0:1], gamma_b[:, :],
                                                        ALU.subtract, ALU.mult))
                    dve.wait_ge(s_ln1ar, 1)
                    s.link(dve.reciprocal(ln_r[:, :], ln_std[:, :]))
                    dve.wait_ge(s_xbeta, 1)
                    for c in range(NB):
                        s.mark(dve.scalar_tensor_tensor(h1[:, c, :], h1[:, c, :], ln_r[:, c:c + 1], xs[:, c, :],
                                                        ALU.mult, ALU.add))
                    s.wait()
                    layernorm(dve, s, s_ln1b, s_ln1br, h1, xs, s_x2)
                    s = Steps(dve, s_d2)
                    dve.wait_ge(s_w2, 16 * 6)
                    c4 = SILU_2MOM * HID ** -0.5
                    s.mark(dve.tensor_scalar(wm4_sb[:, 0:3 * MUL], wm4_sb[:, 0:3 * MUL], c4, None, ALU.mult))
                    s.link(dve.tensor_scalar(wm4_sb[:, 3 * MUL:], wm4_sb[:, 3 * MUL:], c4 * 3.0 ** -0.5, None, ALU.mult))
                    s.link(dve.tensor_copy(wm4_s[0][:, :], wm4_sb[:, :]))
                    dve.tensor_tensor(wm4_s[1][:, :], wm4_sb[:, :], wm4_s[0][:, :].bitcast(F32), ALU.subtract).then_inc(s_w4, 1)
                    dve.wait_ge(s_uT, 1)
                    for m in (2, 3):
                        dve.tensor_copy(uT[:, m, :], ps[m][:, :]).then_inc(s_uTc, 1)
                    for c in (1, 3):
                        dve.wait_ge(s_up, c + 1)
                        dve.tensor_scalar(xup[:, c, :], ps[c][:, :], MUL ** -0.5, None, ALU.mult).then_inc(s_upd, 1)
                    dve.wait_ge(s_acc, 1)

                    def messages(u, turn, b, k):
                        feat, w, out_ = sg[:, b, k, :], ps[4 + k % 2], msg[:, k % 2, :, :]
                        if k == 0:
                            dve.wait_ge(s_rl[b], turn * 16 + 16)
                        dve.wait_ge(s_sc, u * 4 + k + 1)
                        dve.tensor_scalar(oh[:, k % 2, :], iota[:, 0:P], rb[:, b, k, 13:14], None, ALU.is_equal).then_inc(s_rows2, 1)
                        dve.wait_ge(s_sg[b][k], turn * 16 + 16)
                        dve.wait_ge(s_w, u * 4 + k + 1)
                        dve.tensor_tensor(out_[:, 0:3, :], w[:, None, 2 * MUL:3 * MUL].to_broadcast([P, 3, MUL]),
                                          feat[:, MUL:].rearrange("p (m v) -> p m v", m=3), ALU.mult)
                        dve.tensor_tensor(out_[:, 3:5, :], w[:, 0:2 * MUL].rearrange("p (a v) -> p a v", a=2),
                                          feat[:, None, 0:MUL].to_broadcast([P, 2, MUL]), ALU.mult)
                        dve.wait_ge(s_rows2, u * 4 + k + 1)
                        dve.tensor_tensor(ohy[:, k % 2, :, :], oh[:, k % 2, None, :].to_broadcast([P, 4, P]),
                                          rb[:, b, k, 8:12, None].to_broadcast([P, 4, P]), ALU.mult)
                        dve.wait_ge(s_dot, u * 4 + k + 3)
                        dve.tensor_tensor(out_[:, 5, :], w[:, 3 * MUL:4 * MUL], dot[:, k, :], ALU.mult).then_inc(s_msg, 1)

                    def flush(u, b):
                        base = dve.value_load(ubase[0:1, bass.ds(u, 1)], min_val=0, max_val=(NB - 1) * 8 * MUL)
                        dve.wait_ge(s_sc, u * 4 + 4 + 2)
                        for half in range(2):
                            t = acc[:, bass.ds(base + half * 512, 512)]
                            ins = dve.tensor_tensor(t, ps[2 * b + half][:, :], t, ALU.add)
                        ins.then_inc(s_fl, 1)

                    for k in range(4):
                        messages(0, 0, 0, k)
                    with dve.Fori(0, LOOPS) as j:
                        for b, u, turn in ((1, j * 2 + 1, j), (0, j * 2 + 2, j + 1)):
                            for k in range(4):
                                messages(u, turn, b, k)
                                if k == 0:
                                    flush(u - 1, 1 - b)
                    flush(NU - 1, 0)
                    for c in range(NB):
                        dve.wait_ge(s_o2, c + 1)
                        sc2 = 1.0 / (16.0 * 10.0)
                        s.mark(dve.scalar_tensor_tensor(y2[:, c, 0:MUL], ps[c % 2][:, 0:MUL], sc2, xs[:, c, 0:MUL], ALU.mult, ALU.add))
                        dve.scalar_tensor_tensor(y2[:, c, MUL:].rearrange("p (v m) -> p m v", m=3),
                                                 ps[c % 2][:, MUL:].rearrange("p (m v) -> p m v", m=3), sc2,
                                                 xs[:, c, MUL:].rearrange("p (v m) -> p m v", m=3),
                                                 ALU.mult, ALU.add).then_inc(s_o2c, 1)
                    s.wait()
                    dve.wait_ge(s_o2c, NB)
                    layernorm(dve, s, s_ln2, s_ln2r, y2, xs, s_x3in)
                    dve.wait_ge(s_x3in, NB)

        with ExitStack() as c3:
            def t3(name, shape, dt=F32):
                return sb(name, shape, dt, c3)

            K3 = W3 // P
            FB = F3 // P
            att_b = t3("att_b", [P, 2, 2, H3, F3])
            b3T = t3("b3T", [P, 2, K3])
            hs3 = t3("hs3", [P, NB, W3])
            o3T = [t3("o3T0", [P, K3, N]), w31_sb[:, :, :].rearrange("p k (a n) -> p (k a) n", n=N)]
            sd3 = t3("sd3", [P, 2, NB, H3])
            diag3 = t3("diag3", [P, NB, P])
            ts3, l3, lm3, e3, pc3 = (t3(n, [P, 2, N]) for n in ("ts3", "l3", "lm3", "e3", "pc3"))
            pn3 = t3("pn3", [P, NB, N])
            junk3 = pn3[:, :, :].rearrange("p c (a f) -> p (c a) f", f=F3)
            pT3 = t3("pT3", [P, 2, NB, P])
            mx3, nm3, dn3, ri3 = (t3(n, [P, 4]) for n in ("mx3", "nm3", "dn3", "ri3"))
            y3 = hs3[:, :, 0:D]
            s_att3, s_b3p, s_b3T, s_loops, s_y3, s_out = (sem(n) for n in ("s_att3", "s_b3p", "s_b3T", "s_loops", "s_y3", "s_out"))
            s_ln3, s_ln3r, s_x3, s_x3c, s_v3 = (sem(n) for n in ("s_ln3", "s_ln3r", "s_x3", "s_x3c", "s_v3"))
            q = {n: sem(f"s3_{n}") for n in ("hp", "hc", "dg", "bc", "t", "l", "e", "nm", "c", "n", "p", "pc", "g", "oc",
                                             "v", "m", "d")}
            NH = 2 * NB

            def conv_tensor(pe, j, w_sb, kc, in_T):
                for c in range(NB):
                    for half in range(2):
                        n = 2 * c + half
                        if n >= 2 or j:
                            pe.wait_ge(q["hc"], j * NH + n - 1)
                        for k in range(kc):
                            mm = pe.matmul(ps[n % 2][:, :], in_T[:, k, c * P:(c + 1) * P],
                                           w_sb[:, k, half * 512:(half + 1) * 512], start=(k == 0), stop=(k == kc - 1))
                        mm.then_inc(q["hp"], 1)

                def broadcast(t, c):
                    if c == 0:
                        pe.wait_ge(q["t"], t * 4 + 4)
                        pe.wait_ge(q["dg"], t + 1)
                        pe.matmul(ps[2][:, :], ones[:, :], diag3[:, :, :].rearrange("p c n -> p (c n)"),
                                  start=True, stop=True).then_inc(q["bc"], 1)

                def turn(t, c):
                    pe.wait_ge(q["n"], t * 4 + c + 3)
                    pe.wait_ge(q["pc"], t * 4 + c + 1)
                    for g in range(NB):
                        mm = pe.transpose(ps[4 + c % 2][:, g * P:(g + 1) * P], pn3[:, c, g * P:(g + 1) * P], ident[:, :])
                    mm.then_inc(q["p"], 1)

                def gather(t, c):
                    pe.wait_ge(q["pc"], t * 4 + c + 3)
                    pe.wait_ge(q["oc"], t * 4 + c + 1)
                    for f in range(FB):
                        col = (t - j * H3) * F3 + f * P
                        for g in range(NB):
                            mm = pe.matmul(ps[6 + c % 2][:, f * P:(f + 1) * P], hs3[:, g, col:col + P], pT3[:, c % 2, g, :],
                                           start=(g == 0), stop=(g == NB - 1))
                    mm.then_inc(q["g"], 1)

                for i in range(H3):
                    pipelined(j * H3 + i, ((gather, 3), (turn, 1), (broadcast, -3)), first=(i == 0), last=(i == H3 - 1))

            def pipelined(t, steps, first=False, last=False):
                lead = min(lag for _, lag in steps) if first else 0
                tail = max(lag for _, lag in steps) if last else 0
                for n in range(min(lead, 0), NB + max(tail, 0)):
                    for step, lag in steps:
                        m = n - lag
                        if not (first and m < 0) and not (last and m >= NB):
                            step(t + m // NB, m % NB)

            def heads(eng, j, steps):
                pipelined(j * H3, steps, first=True)
                with eng.Fori(j * H3 + 1, (j + 1) * H3 - 1) as t:
                    pipelined(t, steps)
                pipelined((j + 1) * H3 - 1, steps, last=True)

            def conv_scalar(act, j, out_T):
                for n in range(2 * NB):
                    act.wait_ge(q["hp"], j * NH + n + 1)
                    act.activation(hs3[:, n // 2, (n % 2) * 512:(n % 2 + 1) * 512], ps[n % 2][:, :], ACT.Copy)\
                        .then_inc(q["hc"], 1)

                def plus(t, c):
                    act.wait_ge(q["bc"], t + 1)
                    act.wait_ge(q["l"], t * 4 + c + 1)
                    act.activation(ts3[:, c % 2, :], ps[2][:, :], ACT.Identity, bias=sd3[:, 1, c, bass.ds(t - j * H3, 1)])\
                        .then_inc(q["t"], 1)

                def exp(t, c):
                    act.wait_ge(q["nm"], t * 4 + c + 1)
                    act.wait_ge(q["c"], t * 4 + c + 1)
                    act.activation(e3[:, c % 2, :], lm3[:, c % 2, :], ACT.Exp, bias=nm3[:, c:c + 1]).then_inc(q["e"], 1)

                def turned(t, c):
                    act.wait_ge(q["p"], t * 4 + c + 5)
                    act.wait_ge(q["g"], t * 4 + c + 1)
                    act.activation(pT3[:, c % 2, :, :], psum4(4 + c % 2), ACT.Copy).then_inc(q["pc"], 1)

                def output(t, c):
                    act.wait_ge(q["g"], t * 4 + c + 3)
                    for f in range(FB):
                        row = (t - j * H3) * FB + f
                        ins = act.activation(out_T[:, bass.ds(row, 1), c * P:(c + 1) * P].rearrange("p a n -> p (a n)"),
                                             ps[6 + c % 2][:, f * P:(f + 1) * P], ACT.Relu, bias=b3T[:, j, bass.ds(row, 1)])
                    ins.then_inc(q["oc"], 1)

                heads(act, j, ((exp, 0), (turned, 2), (output, 4), (plus, -2)))

            def conv_pool(pool, j):
                def normalize(t, c):
                    pool.wait_ge(q["c"], t * 4 + c + 3)
                    pool.wait_ge(q["p"], t * 4 + c + 1)
                    pool.sem_inc(s_gate_pool, 1)
                    pool.tensor_scalar(pn3[:, c, :], pc3[:, c % 2, :], ri3[:, c:c + 1], 1.0, ALU.mult, ALU.mult)\
                        .then_inc(q["n"], 1)

                heads(pool, j, ((normalize, 0),))

            def conv_vector(dve, j):
                s = Steps(dve, q["v"], j, NB * 2 * H3)
                for c in range(NB):
                    dve.wait_ge(q["hc"], j * NH + 2 * c + 2)
                    if c == 0 and j:
                        dve.wait_ge(q["p"], j * NB * H3 + 4)
                    for h in range(H3):
                        for e in range(2):
                            s.mark(dve.tensor_tensor_reduce(junk3[:, 2 * h + e, :], hs3[:, c, h * F3:(h + 1) * F3],
                                                            att_b[:, j, e, h, :], 1.0, 0.0, ALU.mult, ALU.add,
                                                            sd3[:, e, c, h:h + 1]))
                    s.wait()

                def diagonal(t, c):
                    if c == 0:
                        dve.wait_ge(q["t"], t * 4 + 1)
                        dve.tensor_tensor(diag3[:, :, :], ident[:, None, :].to_broadcast([P, NB, P]),
                                          sd3[:, 0, :, bass.ds(t - j * H3, 1)].to_broadcast([P, NB, P]), ALU.mult)\
                            .then_inc(q["dg"], 1)

                def leaky(t, c):
                    dve.wait_ge(q["t"], t * 4 + c + 5)
                    dve.scalar_tensor_tensor(l3[:, c % 2, :], ts3[:, c % 2, :], 0.2, ts3[:, c % 2, :],
                                             ALU.mult, ALU.max).then_inc(q["l"], 1)

                def masked(t, c):
                    dve.wait_ge(q["e"], t * 4 + c + 1)
                    dve.wait_ge(q["l"], t * 4 + c + 3)
                    dve.sem_inc(s_gate_dve, 1)
                    dve.tensor_tensor_reduce(lm3[:, c % 2, :], l3[:, c % 2, :], nomask[:, c, :], 1.0, -3.0e38,
                                             ALU.add, ALU.max, mx3[:, c:c + 1]).then_inc(q["m"], 1)

                def negated(t, c):
                    dve.wait_ge(q["m"], t * 4 + c + 1)
                    dve.tensor_scalar(nm3[:, c:c + 1], mx3[:, c:c + 1], -1.0, None, ALU.mult).then_inc(q["nm"], 1)

                def weigh(t, c):
                    dve.wait_ge(q["e"], t * 4 + c + 3)
                    dve.wait_ge(q["n"], t * 4 + c + 1)
                    dve.sem_inc(s_gate_dve, 1)
                    dve.tensor_tensor_reduce(pc3[:, c % 2, :], e3[:, c % 2, :], count[:, c, :], 1.0, 1.0e-16,
                                             ALU.mult, ALU.add, dn3[:, c:c + 1]).then_inc(q["d"], 1)

                def inverted(t, c):
                    dve.wait_ge(q["d"], t * 4 + c + 1)
                    dve.reciprocal(ri3[:, c:c + 1], dn3[:, c:c + 1]).then_inc(q["c"], 1)

                heads(dve, j, ((leaky, -1), (weigh, 1), (masked, -1), (inverted, 1), (negated, -1), (diagonal, -4)))

            with nc.Block() as block:
                @block.sync
                def _(sp):
                    for j, (a, b) in enumerate(((asrc1, adst1), (asrc2, adst2))):
                        sp.dma_start(att_b[:, j, 0, :, :], a.partition_broadcast(P)).then_inc(s_att3, 16)
                        sp.dma_start(att_b[:, j, 1, :, :], b.partition_broadcast(P)).then_inc(s_att3, 16)
                    for c in range(NB):
                        sp.wait_ge(s_x3c, c + 1)
                        sp.dma_start(out[c * P:(c + 1) * P, :], xs[:, c, :]).then_inc(s_out, 16)
                    sp.wait_ge(s_out, 16 * NB)

                @block.gpsimd
                def _(pool):
                    pool.sem_inc(q["n"], 2)
                    for j in range(2):
                        conv_pool(pool, j)

                @block.tensor
                def _(pe):
                    for k in range(KB):
                        if k >= 2:
                            pe.wait_ge(s_x3, k - 1)
                        for c in range(NB):
                            mm = pe.transpose(ps[k % 2][:, c * P:(c + 1) * P], xs[:, c, k * P:(k + 1) * P], ident[:, :])
                        mm.then_inc(s_loops, 1)
                    pe.wait_ge(s_b3, 48)
                    for j in range(2):
                        mm = pe.transpose(ps[3][:, j * K3:(j + 1) * K3], b3row[:, j, :], ident[0:K3, 0:K3])
                    mm.then_inc(s_b3p, 1)
                    pe.wait_ge(s_x3, KB)
                    for w, blocks in zip(s_w3, (KB, K3, K3)):
                        pe.wait_ge(w, 16 * blocks)
                    conv_tensor(pe, 0, w31_sb, KB, xT)
                    pe.wait_ge(q["oc"], NB * H3 + 2)
                    conv_tensor(pe, 1, w32_sb, K3, o3T[0])
                    pe.wait_ge(q["oc"], 2 * NB * H3 + 2)
                    for c in range(NB):
                        for k in range(K3):
                            mm = pe.matmul(ps[c][:, :], o3T[1][:, k, c * P:(c + 1) * P], fcw_sb[:, k, :],
                                           start=(k == 0), stop=(k == K3 - 1))
                        mm.then_inc(s_y3, 1)

                @block.scalar
                def _(act):
                    for k in range(KB):
                        act.wait_ge(s_loops, k + 1)
                        act.activation(xT[:, k, :], ps[k % 2][:, :], ACT.Copy).then_inc(s_x3, 1)
                    act.wait_ge(s_b3p, 1)
                    act.activation(b3T[:, :, :].rearrange("p a b -> p (a b)"), ps[3][:, 0:2 * K3], ACT.Copy).then_inc(s_b3T, 1)
                    act.wait_ge(s_b3T, 1)
                    act.sem_inc(q["t"], 4)
                    act.sem_inc(q["pc"], 2)
                    act.sem_inc(q["oc"], 2)
                    act.sem_inc(q["e"], 2)
                    conv_scalar(act, 0, o3T[0])
                    conv_scalar(act, 1, o3T[1])
                    root(act, s_ln3, s_ln3r)

                @block.vector
                def _(dve):
                    s = Steps(dve, s_v3)
                    for c in range(NB):
                        d = count[:, c, c * P:(c + 1) * P]
                        s.mark(dve.tensor_tensor(d, d, ident[:, :], ALU.add))
                    s.wait()
                    for c in range(NB):
                        s.mark(dve.tensor_scalar(nomask[:, c, :], count[:, c, :], 0.0, NEG, ALU.is_equal, ALU.mult))
                    s.wait()
                    dve.wait_ge(s_att3, 64)
                    dve.sem_inc(q["l"], 2)
                    dve.sem_inc(q["c"], 2)
                    dve.sem_inc(q["p"], 4)
                    dve.sem_inc(q["g"], 2)
                    conv_vector(dve, 0)
                    conv_vector(dve, 1)
                    for c in range(NB):
                        dve.wait_ge(s_y3, c + 1)
                        s.mark(dve.tensor_tensor(y3[:, c, :], ps[c][:, :], fcb_b[:, :], ALU.add))
                    s.wait()
                    for c in range(NB):
                        s.mark(dve.tensor_tensor(y3[:, c, :], y3[:, c, :], xs[:, c, :], ALU.add))
                    s.wait()
                    layernorm(dve, s, s_ln3, s_ln3r, y3, xs, s_x3c)
        lay3.close()
    return nc


_INS = ['x', 'src', 'dst', 'edge_attr_4', 'edge_attr_8', 'L0_gnn_W', 'L0_gnn_a', 'L1_gnn_Wq', 'L1_gnn_bq', 'L1_gnn_Wk',
        'L1_gnn_bk', 'L1_gnn_Wv', 'L1_gnn_bv', 'L1_gnn_Wskip', 'L1_gnn_bskip', 'L1_gnn_Wlin', 'L1_gnn_blin',
        'L1_gnn_gamma', 'L1_gnn_beta', 'L2_gnn_W_up0', 'L2_gnn_W_up1', 'L2_gnn_W_mlp1', 'L2_gnn_W_mlp2',
        'L2_gnn_W_mlp3', 'L2_gnn_W_mlp4', 'L2_gnn_W_out0', 'L2_gnn_W_out1', 'L3_gnn_W1', 'L3_gnn_att_src1',
        'L3_gnn_att_dst1', 'L3_gnn_b1', 'L3_gnn_W2', 'L3_gnn_att_src2', 'L3_gnn_att_dst2', 'L3_gnn_b2', 'L3_gnn_fcW',
        'L3_gnn_fcb']


def kernel(**inputs):
    import numpy as _np
    import concourse.bacc as _bacc
    from concourse import mybir as _mybir
    from concourse.bass_utils import run_bass_kernel_spmd as _run

    nc = _bacc.Bacc("TRN2", target_bir_lowering=False, num_devices=1)
    arrays, args = {}, []
    for name in _INS:
        a = _np.ascontiguousarray(inputs[name])
        arrays[f"in_{name}_dram"] = a
        args.append(nc.dram_tensor(f"in_{name}_dram", a.shape, _mybir.dt.from_np(a.dtype), kind="ExternalInput").ap())
    args.append(nc.dram_tensor("out_0_dram", (N, D), F32, kind="ExternalOutput").ap())
    graph_kernel(nc, *args)
    r = _run(nc, [arrays], core_ids=[0])
    return r.results[0]["out_0_dram"]
```

```python
from contextlib import ExitStack

import concourse.bass as bass
from concourse import mybir

F32 = mybir.dt.float32
F32R = mybir.dt.float32r
BF16 = mybir.dt.bfloat16
F16 = mybir.dt.float16
I32 = mybir.dt.int32
U32 = mybir.dt.uint32
ALU = mybir.AluOpType
ACT = mybir.ActivationFunctionType
AX = mybir.AxisListType

P = 128
N = 512
D = 512
E = 16384
NB = N // P
KB = D // P
ET = E // P
UNIT = 4 * P
NU = E // UNIT + NB - 1
R_EF, R_LO, R_Y, R_SRC, R_DST, REC = 0, 8, 16, 20, 21, 24
NEG = -1.0e30
EPS = 1e-5
H0, F0 = 8, 64
H1 = 4
H3, F3 = 4, 256
W3 = H3 * F3
MUL = 128
HID = 64
SILU_2MOM = 1.679177
SPLIT_PASSES = ((0, 0), (0, 1), (1, 0))


class Steps:

    def __init__(self, eng, sem, turn=0, per_turn=0):
        self.eng, self.sem, self.base, self.n, self.per_turn = eng, sem, turn * per_turn, 0, per_turn

    def link(self, instruction):
        self.mark(instruction)
        self.wait()

    def mark(self, instruction):
        instruction.then_inc(self.sem, 1)
        self.n += 1

    def wait(self):
        self.eng.wait_ge(self.sem, self.base + self.n)

    def done(self):
        assert self.n == self.per_turn, self.n


def graph_kernel(nc, x, src, dst, ea, ef, w0, a0, wq, bq, wk, bk, wv, bv, wskip, bskip, wlin, blin, gamma, beta,
                 wup0, wup1, wm1, wm2, wm3, wm4, wout0, wout1, w31, asrc1, adst1, b31, w32, asrc2, adst2, b32,
                 fcw, fcb, out):
    ctx = ExitStack()
    with ctx:
        def sem(name):
            return ctx.enter_context(nc.semaphore(name))

        def sb(name, shape, dt=F32, where=ctx):
            return where.enter_context(nc.sbuf_tensor(name, shape, dt))

        ps = [ctx.enter_context(nc.psum_tensor(f"bank{b}", [P, 512], F32)) for b in range(8)]
        records = nc.dram_tensor("records", [(NU + 1) * UNIT, REC], F32)
        xup_dram = nc.dram_tensor("xup_dram", [N, 4 * MUL], F32)

        ident = sb("ident", [P, P])
        ones = sb("ones", [P, P])
        iota = sb("iota", [P, N])
        xs = sb("xs", [P, NB, D])
        xT = sb("xT", [P, KB, N])
        count = sb("count", [P, NB, N])
        nomask = sb("nomask", [P, NB, N])
        ln_stat = sb("ln_stat", [P, NB, 6])
        ln_mv = sb("ln_mv", [P, NB, 2])
        ln_std = sb("ln_std", [P, NB])
        ln_r = sb("ln_r", [P, NB])
        ubase = sb("ubase", [P, NU + 1], I32)
        s_stage = [sem(f"s_stage{b}") for b in range(2)]
        s_wh, s_split = sem("s_wh"), sem("s_split")
        s_b1 = sem("s_load_bias1")
        gamma_b = sb("gamma_b", [P, D])
        s_xbeta, s_xlast, s_h1v = sem("s_xbeta"), sem("s_xlast"), sem("s_h1v")
        s_gate_dve, s_gate_pool, s_gate_sp = sem("s_gate_dve"), sem("s_gate_pool"), sem("s_gate_sp")

        def psum4(b):
            return ps[b][:, :].rearrange("p (c n) -> p c n", c=4)

        def variances(dve, s, s_var):
            s.wait()
            for c in range(NB):
                s.mark(dve.bn_aggr(ln_mv[:, c, :], ln_stat[:, c, :]))
            s.wait()
            dve.tensor_scalar(ln_std[:, :], ln_mv[:, :, 1], EPS, None, ALU.add).then_inc(s_var, 1)

        def root(act, s_var, s_std):
            act.wait_ge(s_var, 1)
            act.activation(ln_std[:, :], ln_std[:, :], ACT.Sqrt).then_inc(s_std, 1)

        def sums(dve, s, src, c):
            s.mark(dve.bn_stats(ln_stat[:, c, :], src))

        def layernorm(dve, s, s_var, s_std, src_t, dst_t, s_done):
            variances(dve, s, s_var)
            dve.wait_ge(s_std, 1)
            s.link(dve.reciprocal(ln_r[:, :], ln_std[:, :]))
            for c in range(NB):
                dve.tensor_scalar(dst_t[:, c, :], src_t[:, c, :], ln_mv[:, c, 0:1], ln_r[:, c:c + 1],
                                  ALU.subtract, ALU.mult).then_inc(s_done, 1)

        lay1 = ExitStack()
        wA, wB, wC = ([sb(f"w{n}{part}", [P, KB, D], F32R, lay1) for part in ("_hi", "_lo")] for n in "ABC")
        stage = sb("stage", [P, 2, KB, D], F32, lay1)
        brow = sb("brow", [16, 3, P], F32, lay1)
        blin_row = sb("blin_row", [1, D], F32, lay1)
        bT = sb("bT", [P, 3, H1 * KB], F32, lay1)
        s_bTp, s_bT = sem("s_bTp"), sem("s_bT")
        beta_b = sb("beta_b", [P, D], F32, lay1)

        def stage_load(sp, i, job):
            h = (H1 - 1) - i
            sp.wait_ge(s_split, i * 5 + job + (5, 3, 4, 4, 4)[job])
            sp.sem_inc(s_gate_sp, 1)
            if job < 4:
                w = (wq, wk, wv, wskip)[job].rearrange("(k p) c -> p k c", p=P)[:, :, bass.ds(h * D, D)]
            else:
                w = wlin[bass.ds(h * D, D), :].rearrange("(k p) c -> p k c", p=P)
            sp.dma_start(stage[:, job % 2, :, :], w).then_inc(s_stage[job % 2], 16)

        def split_buffer(job):
            return (wA, wB, wC, wA, wB)[job]

        def split_weights(pool, i, job, high_done=False):
            half, turn = job % 2, i * (3 - job % 2) + job // 2
            w = split_buffer(job)
            pool.wait_ge(s_stage[half], turn * 16 + 16)
            pool.sem_inc(s_gate_pool, 1)
            if not high_done:
                pool.tensor_scalar(w[0][:, :, :], stage[:, half, :, :], 1.0, 1.0, ALU.mult, ALU.mult).then_inc(s_wh, 1)
            pool.wait_ge(s_wh, i * 5 + job + 1)
            pool.sem_inc(s_gate_pool, 1)
            pool.tensor_tensor(w[1][:, :, :], stage[:, half, :, :], w[0][:, :, :].bitcast(F32), ALU.subtract)\
                .then_inc(s_split, 1)

        with ExitStack() as c0:
            def t0(name, shape, dt=F32):
                return sb(name, shape, dt, c0)

            iota_i = t0("iota_i", [P, N], I32)
            iota_h = t0("iota_h", [P, N], F16)
            tri = t0("tri", [P, P])
            fill = t0("fill", [P, (NU + 1) * UNIT // P, REC])
            dst_i, src_i, tmp_i = (t0(n, [P, ET], I32) for n in ("dst_i", "src_i", "tmp_i"))
            dst_f, src_f, blk_f, loc_f, pos_f = (t0(n, [P, ET]) for n in ("dst_f", "src_f", "blk_f", "loc_f", "pos_f"))
            pos_i = t0("pos_i", [P, ET], I32)
            mask_g = t0("mask_g", [P, NB, ET])
            scan_g = t0("scan_g", [P, NB, ET])
            tot = t0("tot", [P, NB])
            sc = t0("sc", [P, 6, NB])
            sc_i = t0("sc_i", [P, 2, NB], I32)
            ub_f = t0("ub_f", [P, NU + 1])
            ef_sb = t0("ef_sb", [P, ET, 8])
            ea_sb = t0("ea_sb", [P, ET, 4])
            rec = t0("rec", [P, ET, REC])
            rbuf = t0("rbuf", [P, 2, 4, REC])
            ibuf = t0("ibuf", [P, 2, 4], I32)
            zero_b = t0("zero_b", [P, N], BF16)
            ohd = t0("ohd", [P, 4, N], BF16)
            ohs = t0("ohs", [P, 4, N], BF16)
            w0_sb = t0("w0_sb", [P, KB, D])
            w0T = t0("w0T", [P, KB, D])
            xh = t0("xh", [P, NB, H0 * F0])
            a_b = t0("a_b", [P, 2, H0, F0])
            prod = t0("prod", [P, 2, H0 * F0])
            sij = t0("sij", [P, 2, NB, H0])
            maskT = w0_sb
            diag = t0("diag", [P, NB, P])
            tsum = t0("tsum", [P, 2, N])
            esc = t0("esc", [P, 2, N])
            lsc = t0("lsc", [P, 2, N])
            emx = t0("emx", [P, 2])
            nmx = t0("nmx", [P, 4])
            ex = w0T[:, 0:2, :]
            rsum = t0("rsum", [P, 4])
            rinv = t0("rinv", [P, 4])
            exT = w0T[:, 2:4, :].rearrange("p b (g n) -> p b g n", g=NB)
            y0 = fill[:, :, :].rearrange("p r k -> p (r k)")[:, 0:NB * D].rearrange("p (c d) -> p c d", c=NB)

            s_idx, s_att, s_x, s_w0, s_a0, s_fill = (sem(n) for n in ("s_idx", "s_att", "s_x", "s_w0", "s_a0", "s_fill"))
            s_const, s_ident, s_iota, s_tot, s_off = (sem(n) for n in ("s_const", "s_ident", "s_iota", "s_tot", "s_off"))
            s_loc, s_pos, s_rec, s_cp = (sem(n) for n in ("s_loc", "s_pos", "s_rec", "s_cp"))
            s_sent = [sem(f"s_sent{b}") for b in range(2)]
            s_fillset, s_oh, s_ohfree, s_cnt, s_cs, s_sij, s_efhi = (
                sem(n) for n in ("s_fillset", "s_oh", "s_ohfree", "s_cnt", "s_cs", "s_sij", "s_efhi"))
            s_t0, s_t0c, s_xh, s_xhc, s_zero = (sem(n) for n in ("s_t0", "s_t0c", "s_xh", "s_xhc", "s_zero"))
            s_mT, s_mTc = sem("s_mT"), sem("s_mTc")
            s_v0, s_diag, s_sjb, s_ts, s_em, s_ex = (sem(n) for n in ("s_v0", "s_diag", "s_sjb", "s_ts", "s_em", "s_ex"))
            s_nm, s_xT, s_xTc, s_o, s_y, s_lm, s_ri = (sem(n) for n in ("s_nm", "s_xT", "s_xTc", "s_o", "s_y", "s_lm", "s_ri"))
            s_ln0, s_ln0r, s_lnx0, s_xT0, s_xT0c = (sem(n) for n in ("s_ln0", "s_ln0r", "s_lnx0", "s_xT0", "s_xT0c"))

            with nc.Block() as block:
                @block.sync
                def _(sp):
                    sp.dma_start(dst_i[:, :], dst.rearrange("(p t) -> p t", p=P)).then_inc(s_idx, 16)
                    sp.dma_start(src_i[:, :], src.rearrange("(p t) -> p t", p=P)).then_inc(s_idx, 16)
                    sp.dma_start(xs[:, :, :], x.rearrange("(c p) d -> p c d", p=P)).then_inc(s_x, 16)
                    sp.dma_start(w0_sb[:, :, :], w0.rearrange("h o i -> (h o) i").rearrange("(c p) i -> p c i", p=P))\
                        .then_inc(s_w0, 16)
                    for j in range(2):
                        sp.dma_start(a_b[:, j, :, :], a0[:, j * F0:(j + 1) * F0].partition_broadcast(P))\
                            .then_inc(s_a0, 16)
                    sp.dma_start(ef_sb[:, :, :], ef.rearrange("(p t) k -> p t k", p=P)).then_inc(s_att, 16)
                    sp.dma_start(ea_sb[:, :, :], ea.rearrange("(p t) k -> p t k", p=P)).then_inc(s_att, 16)
                    sp.wait_ge(s_fillset, 2)
                    sp.dma_start(records.ap().rearrange("(p r) k -> p r k", p=P), fill[:, :, :]).then_inc(s_fill, 16)
                    sp.sem_inc(s_split, 5)
                    for job in range(2):
                        stage_load(sp, 0, job)
                    for j, b in enumerate((bq, bk, bskip)):
                        sp.dma_start(brow[:, j, :], b.rearrange("(c p) -> c p", p=P)).then_inc(s_b1, 16)
                    sp.dma_start(blin_row[:, :], blin.rearrange("(a c) -> a c", a=1)).then_inc(s_b1, 16)
                    sp.dma_start(gamma_b[:, :], gamma.partition_broadcast(P)).then_inc(s_b1, 16)
                    sp.dma_start(beta_b[:, :], beta.partition_broadcast(P)).then_inc(s_b1, 16)
                    stage_load(sp, 0, 2)

                @block.gpsimd
                def _(pool):
                    pool.iota(iota_i[:, :], pattern=[[1, N]], base=0, channel_multiplier=0).then_inc(s_iota, 1)
                    pool.memset(ones[:, :], 1.0).then_inc(s_const, 1)
                    pool.memset(ident[:, :], 0.0).then_inc(s_const, 1)
                    pool.wait_ge(s_const, 2)
                    pool.affine_select(out=ident[:, :], in_=ident[:, :], compare_op=ALU.not_equal, fill=1.0, base=0,
                                       pattern=[[-1, P]], channel_multiplier=1).then_inc(s_ident, 1)
                    pool.affine_select(out=tri[:, :], in_=ones[:, :], compare_op=ALU.is_gt, fill=0.0, base=0,
                                       pattern=[[1, P]], channel_multiplier=-1).then_inc(s_ident, 1)
                    pool.memset(fill[:, :, :], 0.0).then_inc(s_fillset, 1)
                    pool.wait_ge(s_fillset, 1)
                    pool.memset(fill[:, :, R_DST:R_DST + 1], -1.0).then_inc(s_fillset, 1)
                    pool.memset(rec[:, :, R_DST + 1:], 0.0).then_inc(s_rec, 1)
                    pool.wait_ge(s_idx, 32)
                    pool.tensor_copy(rec[:, :, R_SRC].bitcast(I32), src_i[:, :]).then_inc(s_rec, 1)
                    pool.wait_ge(s_att, 32)
                    pool.tensor_copy(rec[:, :, R_Y:R_SRC], ea_sb[:, :, :]).then_inc(s_rec, 1)
                    pool.wait_ge(s_loc, 1)
                    pool.tensor_copy(rec[:, :, R_DST], loc_f[:, :]).then_inc(s_rec, 1)
                    pool.wait_ge(s_efhi, 1)
                    pool.tensor_tensor(rec[:, :, R_LO:R_Y], ef_sb[:, :, :], rec[:, :, R_EF:R_LO], ALU.subtract).then_inc(s_rec, 1)
                    pool.wait_ge(s_rec, 5)
                    pool.wait_ge(s_pos, 1)
                    pool.wait_ge(s_fill, 16)

                    def send(i, first):
                        for b in range(2):
                            if not first:
                                pool.wait_ge(s_sent[b], i * 64)
                            pool.tensor_copy(rbuf[:, b, :, :], rec[:, bass.ds(i * 8 + b * 4, 4), :]).then_inc(s_cp, 1)
                            pool.tensor_copy(ibuf[:, b, :], pos_i[:, bass.ds(i * 8 + b * 4, 4)]).then_inc(s_cp, 1)
                            pool.wait_ge(s_cp, i * 4 + b * 2 + 2)
                            pool.sem_inc(s_gate_pool, 1)
                            for k in range(4):
                                pool.indirect_dma_start(
                                    records.ap()[:, :],
                                    bass.IndirectOffsetOnAxis(ap=ibuf[:, b, k:k + 1], axis=0),
                                    rbuf[:, b, k, :], None).then_inc(s_sent[b], 16)

                    send(0, True)
                    with pool.Fori(1, ET // 8) as i:
                        send(i, False)
                    for b in range(2):
                        pool.wait_ge(s_sent[b], 64 * (ET // 8))
                    for job in range(3):
                        split_weights(pool, 0, job, high_done=(job < 2))

                @block.tensor
                def _(pe):
                    pe.wait_ge(s_ident, 2)
                    pe.wait_ge(s_tot, 1)
                    pe.matmul(ps[2][:, 0:NB], tri[:, :], tot[:, :], start=True, stop=True)
                    pe.matmul(ps[2][:, NB:2 * NB], ones[:, :], tot[:, :], start=True, stop=True).then_inc(s_off, 1)
                    pe.wait_ge(s_x, 16)
                    pe.wait_ge(s_w0, 16)
                    n = 0
                    for t in (xs, w0_sb):
                        for k in range(KB):
                            if n >= 2:
                                pe.wait_ge(s_t0c, n - 1)
                            for c in range(NB):
                                mm = pe.transpose(ps[n % 2][:, c * P:(c + 1) * P], t[:, c, k * P:(k + 1) * P], ident[:, :])
                            mm.then_inc(s_t0, 1)
                            n += 1
                    pe.wait_ge(s_zero, 1)
                    for c in range(NB):
                        pe.matmul(ps[4 + c][:, :], zero_b[:, 0:P], zero_b[:, :], start=True, stop=False,
                                  skip_group_check=True)
                    pe.sem_inc(s_ohfree, 4)
                    pe.sem_inc(s_o, 2)

                    def counts(first, last):
                        with pe.Fori(first, last) as i:
                            for k in range(4):
                                pe.wait_ge(s_oh, i * 4 + k + 1)
                                for c in range(NB):
                                    mm = pe.matmul(ps[4 + c][:, :], ohd[:, k, c * P:(c + 1) * P], ohs[:, k, :],
                                                   start=False, stop=False, skip_group_check=True)
                                mm.then_inc(s_ohfree, 1)

                    counts(0, ET // 16)
                    pe.wait_ge(s_t0c, n)
                    for c in range(NB):
                        if c >= 2:
                            pe.wait_ge(s_xhc, c - 1)
                        for k in range(KB):
                            mm = pe.matmul(ps[c % 2][:, :], xT[:, k, c * P:(c + 1) * P], w0T[:, k, :],
                                           start=(k == 0), stop=(k == KB - 1))
                        mm.then_inc(s_xh, 1)
                    counts(ET // 16, ET // 4)
                    for c in range(NB):
                        mm = pe.matmul(ps[4 + c][:, :], zero_b[:, 0:P], zero_b[:, :], start=False, stop=True,
                                       skip_group_check=True)
                    mm.then_inc(s_cnt, 1)
                    def broadcast(h):
                        pe.wait_ge(s_diag, h + 1)
                        pe.wait_ge(s_ts, h * 4 + 4)
                        pe.matmul(ps[0][:, :], ones[:, :], diag[:, :, :].rearrange("p c n -> p (c n)"),
                                  start=True, stop=True).then_inc(s_sjb, 1)

                    def turn(h, c):
                        pe.wait_ge(s_ex, h * 4 + c + 3)
                        pe.wait_ge(s_xTc, h * 4 + c + 1)
                        for g in range(NB):
                            mm = pe.transpose(ps[2 + c % 2][:, g * P:(g + 1) * P], ex[:, c % 2, g * P:(g + 1) * P],
                                              ident[:, :])
                        mm.then_inc(s_xT, 1)

                    def neighbours(h, c):
                        pe.wait_ge(s_xTc, h * 4 + c + 3)
                        pe.wait_ge(s_y, h * 4 + c + 1)
                        for g in range(NB):
                            mm = pe.matmul(ps[4 + c % 2][:, 0:F0], exT[:, c % 2, g, :], xh[:, g, bass.ds(h * F0, F0)],
                                           start=(g == 0), stop=(g == NB - 1))
                        mm.then_inc(s_o, 1)

                    def head(h, first=False, last=False):
                        for c in range(NB):
                            turn(h, c)
                            if c:
                                neighbours(h, c - 1)
                            elif not first:
                                neighbours(h - 1, NB - 1)
                            if c == 1 and not last:
                                broadcast(h + 1)

                    broadcast(0)
                    pe.wait_ge(s_cs, NB)
                    for c in range(NB):
                        if c >= 2:
                            pe.wait_ge(s_mTc, c - 1)
                        for g in range(NB):
                            mm = pe.transpose(ps[2 + c % 2][:, g * P:(g + 1) * P], count[:, g, c * P:(c + 1) * P], ident[:, :])
                        mm.then_inc(s_mT, 1)
                    pe.wait_ge(s_mTc, NB)
                    head(0, first=True)
                    with pe.Fori(1, H0 - 1) as h:
                        head(h)
                    head(H0 - 1, last=True)
                    neighbours(H0 - 1, NB - 1)
                    pe.wait_ge(s_b1, 96)
                    for j in range(3):
                        mm = pe.transpose(ps[6][:, j * 16:(j + 1) * 16], brow[:, j, :], ident[0:16, 0:16])
                    mm.then_inc(s_bTp, 1)
                    pe.wait_ge(s_xTc, 4 * H0 + 2)
                    for c in range(NB):
                        pe.matmul(ps[c][:, :], ones[0:1, :], blin_row[:, :], start=True, stop=False, skip_group_check=True)

                @block.scalar
                def _(act):
                    act.sem_inc(s_ts, 4)
                    act.sem_inc(s_xTc, 2)
                    act.sem_inc(s_ex, 2)
                    for n in range(2 * KB):
                        act.wait_ge(s_t0, n + 1)
                        t = xT if n < KB else w0T
                        act.activation(t[:, n % KB, :], ps[n % 2][:, :], ACT.Copy).then_inc(s_t0c, 1)
                        if n == KB:
                            act.wait_ge(s_att, 32)
                            act.activation(rec[:, :, R_EF:R_LO].bitcast(F32R), ef_sb[:, :, :], ACT.Copy).then_inc(s_efhi, 1)
                    for c in range(NB):
                        act.wait_ge(s_xh, c + 1)
                        act.activation(xh[:, c, :], ps[c % 2][:, :], ACT.Copy).then_inc(s_xhc, 1)
                    for job in range(2):
                        act.wait_ge(s_stage[job], 16)
                        act.activation(split_buffer(job)[0][:, :, :], stage[:, job, :, :], ACT.Copy).then_inc(s_wh, 1)
                    act.wait_ge(s_cnt, 1)
                    for c in range(2):
                        act.activation(count[:, c, :], ps[4 + c][:, :], ACT.Copy).then_inc(s_cs, 1)

                    def tsum_step(h, c):
                        act.wait_ge(s_sjb, h + 1)
                        act.wait_ge(s_em, h * 4 + c + 1)
                        act.activation(tsum[:, c % 2, :], ps[0][:, :], ACT.Identity,
                                       bias=sij[:, 1, c, bass.ds(h, 1)]).then_inc(s_ts, 1)

                    def exp_step(h, c):
                        act.wait_ge(s_nm, h * 4 + c + 1)
                        act.activation(ex[:, c % 2, :], lsc[:, c % 2, :], ACT.Exp, bias=nmx[:, c:c + 1],
                                       accum_out=rsum[:, c:c + 1]).then_inc(s_ex, 1)

                    def evac_step(h, c):
                        act.wait_ge(s_xT, h * 4 + c + 1)
                        act.wait_ge(s_o, h * 4 + c + 1)
                        act.activation(exT[:, c % 2, :, :].rearrange("p g n -> p (g n)"), ps[2 + c % 2][:, :],
                                       ACT.Copy).then_inc(s_xTc, 1)

                    def head(h, first=False, last=False):
                        for c in range(NB):
                            exp_step(h, c)
                            if c:
                                evac_step(h, c - 1)
                            elif not first:
                                evac_step(h - 1, NB - 1)
                            if c < 2:
                                tsum_step(h, c + 2)
                            elif not last:
                                tsum_step(h + 1, c - 2)

                    tsum_step(0, 0)
                    tsum_step(0, 1)
                    head(0, first=True)
                    with act.Fori(1, H0 - 1) as h:
                        head(h)
                    head(H0 - 1, last=True)
                    evac_step(H0 - 1, NB - 1)
                    act.wait_ge(s_bTp, 1)
                    act.activation(bT[:, :, :].rearrange("p a b -> p (a b)"), ps[6][:, 0:48], ACT.Copy).then_inc(s_bT, 1)
                    root(act, s_ln0, s_ln0r)

                @block.vector
                def _(dve):
                    s = Steps(dve, s_v0)
                    dve.memset(zero_b[:, :], 0.0).then_inc(s_zero, 1)
                    dve.wait_ge(s_iota, 1)
                    s.mark(dve.tensor_copy(iota[:, :], iota_i[:, :]))
                    s.mark(dve.tensor_copy(iota_h[:, :], iota_i[:, :]))
                    dve.wait_ge(s_idx, 32)
                    s.mark(dve.tensor_copy(dst_f[:, :], dst_i[:, :]))
                    s.mark(dve.tensor_copy(src_f[:, :], src_i[:, :]))
                    s.link(dve.tensor_scalar(tmp_i[:, :], dst_i[:, :], P - 1, None, ALU.bitwise_and))
                    dve.tensor_copy(loc_f[:, :], tmp_i[:, :]).then_inc(s_loc, 1)
                    dve.wait_ge(s_loc, 1)
                    s.link(dve.tensor_scalar(tmp_i[:, :], dst_i[:, :], 7, None, ALU.logical_shift_right))
                    s.link(dve.tensor_copy(blk_f[:, :], tmp_i[:, :]))
                    dve.wait_ge(s_const, 2)
                    for g in range(NB):
                        s.mark(dve.tensor_scalar(mask_g[:, g, :], blk_f[:, :], float(g), None, ALU.is_equal))
                    s.wait()
                    for g in range(NB):
                        s.mark(dve.tensor_tensor_scan(scan_g[:, g, :], ones[:, :], mask_g[:, g, :], 0.0,
                                                      ALU.mult, ALU.add))
                    s.wait()
                    dve.tensor_copy(tot[:, :], scan_g[:, :, ET - 1]).then_inc(s_tot, 1)
                    dve.wait_ge(s_off, 1)
                    s.link(dve.tensor_scalar(sc_i[:, 0, :], ps[2][:, NB:2 * NB], float(UNIT - 1), None, ALU.add))
                    s.link(dve.tensor_scalar(sc_i[:, 1, :], sc_i[:, 0, :], 9, None, ALU.logical_shift_right))
                    s.link(dve.tensor_copy(sc[:, 0, :], sc_i[:, 1, :]))
                    s.link(dve.tensor_tensor_scan(sc[:, 1, :], ones[:, 0:NB], sc[:, 0, :], 0.0, ALU.mult, ALU.add))
                    s.link(dve.tensor_tensor(sc[:, 2, :], sc[:, 1, :], sc[:, 0, :], ALU.subtract))
                    s.link(dve.tensor_scalar(sc[:, 3, :], sc[:, 2, :], float(UNIT), -1.0, ALU.mult, ALU.add))
                    s.link(dve.tensor_tensor(sc[:, 4, :], ps[2][:, 0:NB], sc[:, 3, :], ALU.add))
                    for g in range(NB):
                        s.mark(dve.scalar_tensor_tensor(scan_g[:, g, :], scan_g[:, g, :], sc[:, 4, g:g + 1],
                                                        mask_g[:, g, :], ALU.add, ALU.mult))
                    s.wait()
                    s.link(dve.tensor_tensor(pos_f[:, :], scan_g[:, 0, :], scan_g[:, 1, :], ALU.add))
                    s.link(dve.tensor_tensor(pos_f[:, :], pos_f[:, :], scan_g[:, 2, :], ALU.add))
                    s.link(dve.tensor_tensor(pos_f[:, :], pos_f[:, :], scan_g[:, 3, :], ALU.add))
                    dve.tensor_copy(pos_i[:, :], pos_f[:, :]).then_inc(s_pos, 1)
                    s.link(dve.tensor_scalar(ub_f[:, :], iota[:, 0:NU + 1], sc[:, 2, 1:2], None, ALU.is_ge))
                    for g in (2, 3):
                        s.link(dve.scalar_tensor_tensor(ub_f[:, :], iota[:, 0:NU + 1], sc[:, 2, g:g + 1], ub_f[:, :],
                                                        ALU.is_ge, ALU.add))
                    s.link(dve.tensor_scalar(ubase[:, :], ub_f[:, :], 1024.0, None, ALU.mult))

                    def one_hots(tile, k):
                        dve.wait_ge(s_ohfree, tile + 1)
                        dve.tensor_scalar(ohd[:, k, :], iota_h[:, :], dst_f[:, bass.ds(tile, 1)], None, ALU.is_equal)
                        dve.tensor_scalar(ohs[:, k, :], iota_h[:, :], src_f[:, bass.ds(tile, 1)], None,
                                          ALU.is_equal).then_inc(s_oh, 1)

                    with dve.Fori(0, ET // 8) as i:
                        for k in range(4):
                            one_hots(i * 4 + k, k)
                    dve.wait_ge(s_xhc, NB)
                    dve.wait_ge(s_a0, 32)
                    dve.sem_inc(s_sij, 1)
                    with dve.Fori(0, NB) as c:
                        for k in range(ET // 8):
                            one_hots(c * (ET // 8) + (ET // 2 + k), k % 4)
                            if k % 4 == 3:
                                step = k // 4
                                j = step % 2
                                if step < 2:
                                    if step == 0:
                                        dve.wait_ge(s_sij, c * 4 + 1)
                                    dve.tensor_tensor(prod[:, j, :], xh[:, bass.ds(c, 1), :].rearrange("p a d -> p (a d)"),
                                                      a_b[:, j, :, :].rearrange("p h f -> p (h f)"), ALU.mult)\
                                        .then_inc(s_sij, 1)
                                else:
                                    dve.wait_ge(s_sij, c * 4 + 2 + j)
                                    dve.sem_inc(s_gate_dve, 1)
                                    dve.tensor_reduce(sij[:, j, bass.ds(c, 1), :].rearrange("p a h -> p (a h)"),
                                                      prod[:, j, :].rearrange("p (h f) -> p h f", h=H0), AX.X, ALU.add)\
                                        .then_inc(s_sij, 1)
                    dve.wait_ge(s_sij, 4 * NB + 1)
                    dve.tensor_tensor(diag[:, :, :], ident[:, None, :].to_broadcast([P, NB, P]),
                                      sij[:, 0, :, 0:1].to_broadcast([P, NB, P]), ALU.mult).then_inc(s_diag, 1)
                    dve.wait_ge(s_cnt, 1)
                    for c in range(2, NB):
                        dve.tensor_copy(count[:, c, :], ps[4 + c][:, :]).then_inc(s_cs, 1)
                    for c in range(NB):
                        dve.wait_ge(s_mT, c + 1)
                        dve.tensor_scalar(maskT[:, c, :], ps[2 + c % 2][:, :], 1.0, None, ALU.min).then_inc(s_mTc, 1)
                    dve.wait_ge(s_mTc, NB)
                    dve.wait_ge(s_fill, 16)
                    dve.sem_inc(s_em, 2)
                    dve.sem_inc(s_y, 2)

                    def diagonal(h):
                        dve.wait_ge(s_ts, h * 4 + 1)
                        dve.tensor_tensor(diag[:, :, :], ident[:, None, :].to_broadcast([P, NB, P]),
                                          sij[:, 0, :, bass.ds(h, 1)].to_broadcast([P, NB, P]), ALU.mult).then_inc(s_diag, 1)

                    def score(h, c):
                        dve.wait_ge(s_ts, h * 4 + c + 5)
                        dve.sem_inc(s_gate_dve, 1)
                        dve.tensor_tensor_reduce(esc[:, c % 2, :], tsum[:, c % 2, :], maskT[:, c, :], 1.0, -3.0e38,
                                                 ALU.mult, ALU.max, emx[:, c % 2:c % 2 + 1]).then_inc(s_em, 1)

                    def leaky(h, c):
                        dve.wait_ge(s_em, h * 4 + c + 3)
                        dve.wait_ge(s_ex, h * 4 + c + 1)
                        dve.scalar_tensor_tensor(nmx[:, c:c + 1], emx[:, c % 2:c % 2 + 1], 0.2,
                                                 emx[:, c % 2:c % 2 + 1], ALU.mult, ALU.max).then_inc(s_lm, 1)
                        dve.scalar_tensor_tensor(lsc[:, c % 2, :], esc[:, c % 2, :], 0.2, esc[:, c % 2, :],
                                                 ALU.mult, ALU.max)
                        dve.wait_ge(s_lm, h * 4 + c + 1)
                        dve.tensor_scalar(nmx[:, c:c + 1], nmx[:, c:c + 1], -1.0, None, ALU.mult).then_inc(s_nm, 1)

                    def result(h, c, part):
                        if part == 0:
                            dve.wait_ge(s_ex, h * 4 + c + 3)
                            dve.reciprocal(rinv[:, c:c + 1], rsum[:, c:c + 1]).then_inc(s_ri, 1)
                        else:
                            dve.wait_ge(s_ri, h * 4 + c + 1)
                            dve.wait_ge(s_o, h * 4 + c + 3)
                            dve.scalar_tensor_tensor(y0[:, c, bass.ds(h * F0, F0)], ps[4 + c % 2][:, 0:F0],
                                                     rinv[:, c:c + 1], xs[:, c, bass.ds(h * F0, F0)],
                                                     ALU.mult, ALU.add).then_inc(s_y, 1)

                    def head(h, first=False, last=False):
                        for c in range(NB):
                            ahead = (h, c + 1) if c < NB - 1 else (h + 1, 0)
                            behind = (h, c - 2) if c >= 2 else (h - 1, c + 2)
                            if not (last and c == NB - 1):
                                score(*ahead)
                            if not (first and c < 2):
                                result(*behind, 0)
                            if not (last and c == NB - 1):
                                leaky(*ahead)
                            if not (first and c < 2):
                                result(*behind, 1)
                            if c == 0 and not last:
                                diagonal(h + 1)

                    score(0, 0)
                    leaky(0, 0)
                    head(0, first=True)
                    with dve.Fori(1, H0 - 1) as h:
                        head(h)
                    head(H0 - 1, last=True)
                    for c in (2, 3):
                        for part in range(2):
                            result(H0 - 1, c, part)
                    dve.wait_ge(s_y, 4 * H0 + 2)
                    for c in range(NB):
                        sums(dve, s, y0[:, c, :], c)
                    layernorm(dve, s, s_ln0, s_ln0r, y0, xs, s_lnx0)
        with ExitStack() as c1:
            def t1(name, shape, dt=F32):
                return sb(name, shape, dt, c1)

            SCALE1 = float(D) ** -0.5
            bvb = t1("bvb", [P, H1, D])
            xT_s, k_or_p, q_or_v, xa_s = ([t1(f"{n}{part}", [P, KB, N], F32R) for part in ("_hi", "_lo")]
                                          for n in ("xT", "k_or_p", "q_or_v", "xaT"))
            ident_r = t1("ident_r", [P, P], F32R)
            vt1 = t1("vt1", [P, 2, D])
            sm1 = t1("sm1", [P, 2, N])
            pr1 = t1("pr1", [P, 2, N])
            pc1 = t1("pc1", [P, 2, N])
            pn1 = t1("pn1", [P, NB, N])
            mx1 = t1("mx1", [P, 4])
            nm1 = t1("nm1", [P, 4])
            dn1 = t1("dn1", [P, 4])
            ri1 = t1("ri1", [P, 4])

            s_bv = sem("s_bv")
            s_full, s_free, s_hi, s_nm1, s_e1, s_c1, s_n1 = (sem(n) for n in ("s_full", "s_free", "s_hi", "s_nm1", "s_e1", "s_c1", "s_n1"))
            s_vt, s_vlo, s_xl, s_d1, s_nomask = (sem(n) for n in ("s_vt", "s_vlo", "s_xl", "s_d1", "s_nomask"))

            GROUPS = 24
            GQ, GK, GS, GV, GT, GA = range(0, GROUPS, 4)
            HQ, HK, HV, HT, HA = range(0, 20, 4)

            with nc.Block() as block:
                @block.sync
                def _(sp):
                    sp.dma_start(bvb[:, :, :], bv.rearrange("(h c) -> h c", h=H1).partition_broadcast(P)).then_inc(s_bv, 16)
                    stage_load(sp, 0, 3)
                    stage_load(sp, 0, 4)
                    with sp.Fori(1, H1) as i:
                        for job in range(5):
                            stage_load(sp, i, job)

                @block.gpsimd
                def _(pool):
                    def split_next(i, job):
                        if job == 0:
                            pool.wait_ge(s_full, i * GROUPS + 1)
                        if job == 1:
                            pool.wait_ge(s_xl, i + 1)
                        if job == 3:
                            pool.wait_ge(s_full, i * GROUPS + GQ + 3 + 2)
                        if job == 4:
                            pool.wait_ge(s_full, i * GROUPS + GK + 3 + 2)
                        split_weights(pool, i, job)

                    split_next(0, 3)
                    split_next(0, 4)
                    pool.wait_ge(s_b1, 96)
                    pool.tensor_tensor(xs[:, :, :], xs[:, :, :], beta_b[:, None, :].to_broadcast([P, NB, D]), ALU.add)\
                        .then_inc(s_xbeta, 1)
                    with pool.Fori(1, H1) as i:
                        for job in range(5):
                            split_next(i, job)

                @block.tensor
                def _(pe):
                    pe.sem_inc(s_full, 1)
                    pe.sem_inc(s_xl, 1)
                    pe.wait_ge(s_lnx0, NB)
                    for k in range(KB):
                        for c in range(NB):
                            mm = pe.transpose(ps[4 + k][:, c * P:(c + 1) * P], xs[:, c, k * P:(k + 1) * P], ident[:, :])
                        mm.then_inc(s_xT0, 1)
                    pe.wait_ge(s_bT, 2)
                    pe.wait_ge(s_free, KB)

                    def product(bank, left, lcols, right, start=True, stop=True, wait_last=None):
                        for k in range(KB):
                            if k == KB - 1 and wait_last:
                                wait_last()
                            for n, (a, b) in enumerate(SPLIT_PASSES):
                                mm = pe.matmul(bank, left[a][:, k, lcols], right[b][:, k, :],
                                               start=(start and k == 0 and n == 0),
                                               stop=(stop and k == KB - 1 and n == len(SPLIT_PASSES) - 1),
                                               skip_group_check=True)
                        return mm

                    with pe.Fori(0, H1) as i:
                        def bank_free(group):
                            pe.wait_ge(s_free, i * GROUPS + group + 1)

                        def taken(group):
                            pe.wait_ge(s_free, i * GROUPS + group + 1 + 4)

                        for job, w, base in ((0, wA, GQ), (1, wB, GK)):
                            pe.wait_ge(s_split, i * 5 + job + 6)
                            for c in range(KB):
                                bank_free(base + c)
                                product(ps[4 + c][:, :], w, slice(c * P, (c + 1) * P), xT_s).then_inc(s_full, 1)
                        for c in range(NB):
                            bank_free(GS + c)
                            if c == 0:
                                taken(GK + 2)
                            product(ps[4 + c][:, :], q_or_v, slice(c * P, (c + 1) * P), k_or_p,
                                    wait_last=(lambda: taken(GK + 3)) if c == 0 else None).then_inc(s_full, 1)
                        pe.wait_ge(s_split, i * 5 + 2 + 6)
                        for c in range(NB):
                            bank_free(GV + c)
                            product(ps[4 + c][:, :], xT_s, slice(c * P, (c + 1) * P), wC).then_inc(s_full, 1)
                        for c in range(NB):
                            pe.wait_ge(s_n1, i * 4 + c + 3)
                            bank_free(GT + c)
                            for g in range(NB):
                                mm = pe.transpose(ps[4 + c][:, g * P:(g + 1) * P], pn1[:, c, g * P:(g + 1) * P],
                                                  ident[:, :])
                            mm.then_inc(s_full, 1)
                        pe.wait_ge(s_split, i * 5 + 3 + 6)
                        for c in range(KB):
                            bank_free(GA + c)
                            product(ps[4 + c][:, :], wA, slice(c * P, (c + 1) * P), xT_s, stop=False)
                            if c == 1:
                                taken(GT + 3)
                                pe.wait_ge(s_vlo, i * 4 + 4)
                            for a in ((), (0, 1), (2,), (3,))[c]:
                                product(ps[4 + a][:, :], q_or_v, slice(a * P, (a + 1) * P), k_or_p, start=False)\
                                    .then_inc(s_full, 1)
                        pe.wait_ge(s_split, i * 5 + 4 + 6)
                        taken(GA + 2)
                        for c in range(NB):
                            mm = product(ps[c][:, :], xa_s, slice(c * P, (c + 1) * P), wB, start=False, stop=False,
                                         wait_last=(lambda: taken(GA + 3)) if c == 0 else None)
                        mm.then_inc(s_xl, 1)
                    for c in range(NB):
                        for k in range(KB):
                            for part in range(2):
                                mm = pe.matmul(ps[c][:, k * P:(k + 1) * P], xa_s[part][:, k, c * P:(c + 1) * P], ident_r[:, :],
                                               start=False, stop=(k == KB - 1 and part == 1), skip_group_check=True)
                        mm.then_inc(s_xlast, 1)

                @block.scalar
                def _(act):
                    act.activation(ident_r[:, :], ident[:, :], ACT.Copy).then_inc(s_bT, 1)
                    for k in range(KB):
                        act.wait_ge(s_xT0, k + 1)
                        act.activation(xT_s[0][:, k, :], ps[4 + k][:, :], ACT.Copy).then_inc(s_xT0c, 1)
                    act.wait_ge(s_bT, 2)
                    with act.Fori(0, H1) as i:
                        h = act.snap((H1 - 1) - i)
                        for j, (t, base) in enumerate(((q_or_v, GQ), (k_or_p, GK))):
                            for c in range(KB):
                                act.wait_ge(s_full, i * GROUPS + base + c + 2)
                                act.activation(t[0][:, c, :], ps[4 + c][:, :], ACT.Identity,
                                               bias=bT[:, j, bass.ds(h * KB + c, 1)]).then_inc(s_hi, 1)

                        def scaled(c):
                            act.wait_ge(s_c1, i * 4 + c + 3)
                            act.activation(pn1[:, c, :], pc1[:, c % 2, :], ACT.Copy, scale=ri1[:, c:c + 1])\
                               .then_inc(s_n1, 1)

                        for c in range(NB):
                            act.wait_ge(s_nm1, i * 4 + c + 1)
                            act.wait_ge(s_c1, i * 4 + c + 1)
                            act.activation(pr1[:, c % 2, :], sm1[:, c % 2, :], ACT.Exp, bias=nm1[:, c:c + 1],
                                           scale=SCALE1).then_inc(s_e1, 1)
                            if c >= 1:
                                scaled(c - 1)
                        scaled(NB - 1)
                        for c in range(NB):
                            act.wait_ge(s_vt, i * 4 + c + 1)
                            act.activation(q_or_v[0][:, c, :], vt1[:, c % 2, :], ACT.Copy).then_inc(s_hi, 1)
                        for c in range(NB):
                            act.wait_ge(s_full, i * GROUPS + GT + c + 2)
                            act.activation(k_or_p[0][:, :, c * P:(c + 1) * P], psum4(4 + c), ACT.Copy).then_inc(s_hi, 1)
                        for c in range(KB):
                            act.wait_ge(s_full, i * GROUPS + GA + c + 2)
                            act.activation(xa_s[0][:, c, :], ps[4 + c][:, :], ACT.Identity,
                                           bias=bT[:, 2, bass.ds(h * KB + c, 1)]).then_inc(s_hi, 1)

                @block.vector
                def _(dve):
                    dve.sem_inc(s_c1, 2)
                    dve.sem_inc(s_e1, 2)
                    dve.sem_inc(s_n1, 2)
                    for k in range(KB):
                        dve.wait_ge(s_xT0c, k + 1)
                        dve.tensor_tensor(xT_s[1][:, k, :], ps[4 + k][:, :], xT_s[0][:, k, :].bitcast(F32), ALU.subtract)\
                            .then_inc(s_free, 1)
                    for c in range(NB):
                        dve.tensor_scalar(nomask[:, c, :], count[:, c, :], 0.0, NEG, ALU.is_equal, ALU.mult).then_inc(s_nomask, 1)
                    dve.wait_ge(s_nomask, NB)
                    dve.wait_ge(s_bT, 2)
                    with dve.Fori(0, H1) as i:
                        h = dve.snap((H1 - 1) - i)
                        v = Steps(dve, s_d1, i, 12)

                        def low(t, base, hi_base, bias):
                            for c in range(KB):
                                dve.wait_ge(s_hi, i * 20 + hi_base + c + 1)
                                dve.sem_inc(s_gate_dve, 1)
                                dve.scalar_tensor_tensor(t[1][:, c, :], ps[4 + c][:, :], bT[:, bias, bass.ds(h * KB + c, 1)],
                                                         t[0][:, c, :].bitcast(F32), ALU.add, ALU.subtract).then_inc(s_free, 1)

                        low(q_or_v, GQ, HQ, 0)
                        low(k_or_p, GK, HK, 1)

                        def score(c):
                            dve.wait_ge(s_full, i * GROUPS + GS + c + 2)
                            dve.wait_ge(s_e1, i * 4 + c + 1)
                            dve.sem_inc(s_gate_dve, 1)
                            dve.tensor_tensor_reduce(sm1[:, c % 2, :], ps[4 + c][:, :], nomask[:, c, :], 1.0, -3.0e38,
                                                     ALU.add, ALU.max, mx1[:, c:c + 1]).then_inc(s_free, 1)
                            dve.wait_ge(s_free, i * GROUPS + GS + c + 5)
                            dve.tensor_scalar(nm1[:, c:c + 1], mx1[:, c:c + 1], -SCALE1, None, ALU.mult).then_inc(s_nm1, 1)

                        def weigh(c):
                            dve.wait_ge(s_e1, i * 4 + c + 3)
                            dve.wait_ge(s_n1, i * 4 + c + 1)
                            dve.sem_inc(s_gate_dve, 1)
                            v.link(dve.tensor_tensor_reduce(pc1[:, c % 2, :], pr1[:, c % 2, :], count[:, c, :], 1.0, 0.0,
                                                            ALU.mult, ALU.add, dn1[:, c:c + 1]))
                            v.link(dve.tensor_scalar(dn1[:, c:c + 1], dn1[:, c:c + 1], 1.0e-30, None, ALU.max))
                            v.link(dve.reciprocal(ri1[:, c:c + 1], dn1[:, c:c + 1]))
                            dve.sem_inc(s_c1, 1)

                        score(0)
                        score(1)
                        weigh(0)
                        score(2)
                        weigh(1)
                        score(3)
                        weigh(2)
                        weigh(3)
                        v.done()
                        dve.wait_ge(s_bv, 16)

                        def v_low(c):
                            dve.wait_ge(s_hi, i * 20 + HV + c + 1)
                            dve.tensor_tensor(q_or_v[1][:, c, :], vt1[:, c % 2, :], q_or_v[0][:, c, :].bitcast(F32),
                                              ALU.subtract).then_inc(s_vlo, 1)

                        for c in range(NB):
                            if c >= 2:
                                v_low(c - 2)
                                dve.wait_ge(s_vlo, i * 4 + c - 1)
                            dve.wait_ge(s_full, i * GROUPS + GV + c + 2)
                            dve.sem_inc(s_gate_dve, 1)
                            dve.tensor_tensor(vt1[:, c % 2, :], ps[4 + c][:, :], bvb[:, bass.ds(h, 1), :].rearrange("p a c -> p (a c)"),
                                              ALU.add).then_inc(s_vt, 1)
                            dve.wait_ge(s_vt, i * 4 + c + 1)
                            dve.sem_inc(s_free, 1)
                        v_low(2)
                        v_low(3)
                        for c in range(NB):
                            dve.wait_ge(s_hi, i * 20 + HT + c + 1)
                            dve.tensor_tensor(k_or_p[1][:, :, c * P:(c + 1) * P], psum4(4 + c),
                                              k_or_p[0][:, :, c * P:(c + 1) * P].bitcast(F32), ALU.subtract).then_inc(s_free, 1)
                        low(xa_s, GA, HA, 2)
                    s1 = Steps(dve, s_h1v)
                    for c in range(NB):
                        dve.wait_ge(s_xlast, c + 1)
                        sums(dve, s1, ps[c][:, :], c)
                    s1.wait()
        lay1.close()

        lay3 = ExitStack()
        w31_sb = sb("w31_sb", [P, KB, W3], F32, lay3)
        w32_sb = sb("w32_sb", [P, W3 // P, W3], F32, lay3)
        fcw_sb = sb("fcw_sb", [P, W3 // P, D], F32, lay3)
        fcb_b = sb("fcb_b", [P, D], F32, lay3)
        b3row = sb("b3row", [W3 // P, 2, P], F32, lay3)
        s_w3 = [sem(f"s_w3_{n}") for n in range(3)]
        s_b3 = sem("s_b3")

        with ExitStack() as c2:
            def t2(name, shape, dt=F32):
                return sb(name, shape, dt, c2)

            wup = t2("wup", [P, 2, MUL])
            EFR = 2 * (R_Y - R_EF)
            wmA = t2("wmA", [EFR, HID])
            wmA_t = t2("wmA_t", [EFR, HID], F32R)
            wmA_s = t2("wmA_s", [EFR, HID], F32R)
            lows = t2("lows", [EFR, 1])
            wmB = t2("wmB", [HID, HID])
            wmC = t2("wmC", [HID, 2, HID])
            wm4_sb = t2("wm4_sb", [P, 4 * MUL])
            wm4_s = [t2(f"wm4{part}", [P, 4 * MUL], F32R) for part in ("_hi", "_lo")]
            wout = t2("wout", [P, 2, 2, MUL])
            uT = t2("uT", [P, 4, N])
            xup = t2("xup", [P, NB, 4 * MUL])
            rb = t2("rb", [P, 2, 4, REC])
            ra = t2("ra", [P, 2, 4, 2, R_Y - R_EF])
            sg = t2("sg", [P, 2, 4, 4 * MUL])
            efT = t2("efT", [EFR, UNIT], F32R)
            hA = t2("hA", [HID, UNIT])
            hB = t2("hB", [HID, UNIT])
            hC = t2("hC", [P, UNIT])
            upper = t2("upper", [P, 1])
            h3 = t2("h3", [P, 2, UNIT], F32R)
            oh = t2("oh", [P, 2, P])
            ohy = t2("ohy", [P, 2, 4, P])
            msg = t2("msg", [P, 2, 6, MUL])
            part4 = t2("part4", [P, 2, 3, MUL])
            dot = t2("dot", [P, 4, MUL])
            acc = t2("acc", [P, NB * 8 * MUL])
            mT = sg[:, :, :, :].rearrange("p b k d -> p (b k) d")
            y2 = uT

            s_w2, s_uT, s_uTc, s_up, s_upc, s_xup = (sem(n) for n in ("s_w2", "s_uT", "s_uTc", "s_up", "s_upc", "s_xup"))
            s_rl = [sem(f"s_rl{b}") for b in range(2)]
            s_ra = [sem(f"s_ra{b}") for b in range(2)]
            s_sg = [[sem(f"s_sg{b}{k}") for k in range(4)] for b in range(2)]
            s_h3, s_part4, s_dot, s_dotp, s_rows2 = (sem(n) for n in ("s_h3", "s_part4", "s_dot", "s_dotp", "s_rows2"))
            s_m, s_mc, s_w, s_msg, s_sc, s_fl, s_d2 = (sem(n) for n in ("s_m", "s_mc", "s_w", "s_msg", "s_sc", "s_fl", "s_d2"))
            s_mT2, s_mT2c, s_o2, s_o2c = (sem(n) for n in ("s_mT2", "s_mT2c", "s_o2", "s_o2c"))
            s_x2, s_x3in, s_wm, s_upd, s_upper, s_lows = (
                sem(n) for n in ("s_x2", "s_x3in", "s_wm", "s_upd", "s_upper", "s_lows"))
            s_ln1a, s_ln1ar, s_ln1b, s_ln1br, s_ln2, s_ln2r = (
                sem(n) for n in ("s_ln1a", "s_ln1ar", "s_ln1b", "s_ln1br", "s_ln2", "s_ln2r"))
            s_w4, s_gate_pe = (sem(n) for n in ("s_w4", "s_gate_pe"))
            LOOPS = (NU - 1) // 2
            assert NU == 2 * LOOPS + 1

            with nc.Block() as block:
                @block.sync
                def _(sp):
                    def edges(u):
                        return records.ap()[bass.ds(u * UNIT, UNIT), :].rearrange("(p t) k -> p t k", p=P)

                    def load_input(u, b):
                        for copy in range(2):
                            sp.dma_start(ra[:, b, :, copy, :], edges(u)[:, :, R_EF:R_Y]).then_inc(s_ra[b], 16)

                    load_input(0, 0)
                    for group in range(4):
                        sp.dma_start(wmA[group * 8:(group + 1) * 8, :], wm1).then_inc(s_wm, 16)
                    sp.dma_start(wmB[:, :], wm2).then_inc(s_wm, 16)
                    for half in range(2):
                        sp.dma_start(wmC[:, half, :], wm3).then_inc(s_wm, 16)
                    load_input(1, 1)
                    sp.dma_start(wup[:, 0, :], wup0).then_inc(s_w2, 16)
                    sp.dma_start(wup[:, 1, :], wup1).then_inc(s_w2, 16)
                    for half in range(2):
                        sp.dma_start(wm4_sb[half * HID:(half + 1) * HID, :], wm4).then_inc(s_w2, 16)
                    for j, w in enumerate((wout0, wout1)):
                        sp.dma_start(wout[:, j, :, :], w.rearrange("(k p) v -> p k v", p=P)).then_inc(s_w2, 16)

                    def loads(u, b):
                        sp.wait_ge(s_m, u * 4 - 7)
                        sp.sem_inc(s_gate_sp, 1)
                        load_input(u, b)
                        sp.wait_ge(s_msg, u * 4 + 4)
                        sp.sem_inc(s_gate_sp, 1)
                        sp.dma_start(rb[:, b, :, :], edges(u)).then_inc(s_rl[b], 16)

                    for b in range(2):
                        sp.dma_start(rb[:, b, :, :], edges(b)).then_inc(s_rl[b], 16)
                    for c in range(NB):
                        sp.wait_ge(s_upd if c % 2 else s_upc, c // 2 + 1)
                        sp.dma_start(xup_dram.ap()[c * P:(c + 1) * P, :], xup[:, c, :]).then_inc(s_xup, 16)
                    sp.dma_start(fcb_b[:, :], fcb.partition_broadcast(P)).then_inc(s_b3, 16)
                    sp.dma_start(b3row[:, 0, :], b31.rearrange("(c p) -> c p", p=P)).then_inc(s_b3, 16)
                    sp.dma_start(b3row[:, 1, :], b32.rearrange("(c p) -> c p", p=P)).then_inc(s_b3, 16)

                    def weights3(w_sb, w, k, ready):
                        sp.dma_start(w_sb[:, bass.ds(k, 1), :].rearrange("p a c -> p (a c)"), w[bass.ds(k * P, P), :])\
                            .then_inc(ready, 16)

                    assert LOOPS - 1 >= W3 // P >= KB
                    with sp.Fori(0, KB) as j:
                        loads(j * 2 + 2, 0)
                        weights3(w31_sb, w31, j, s_w3[0])
                        loads(j * 2 + 3, 1)
                        weights3(w32_sb, w32, j, s_w3[1])
                        weights3(fcw_sb, fcw, j, s_w3[2])
                    with sp.Fori(KB, W3 // P) as j:
                        loads(j * 2 + 2, 0)
                        weights3(w32_sb, w32, j, s_w3[1])
                        loads(j * 2 + 3, 1)
                        weights3(fcw_sb, fcw, j, s_w3[2])
                    with sp.Fori(W3 // P, LOOPS - 1) as j:
                        loads(j * 2 + 2, 0)
                        loads(j * 2 + 3, 1)
                    loads(NU - 1, 0)

                @block.gpsimd
                def _(pool):
                    def gather(turn, b, k):
                        if k == 0:
                            pool.wait_ge(s_rl[b], turn * 16 + 16)
                            pool.sem_inc(s_gate_pool, 1)
                        pool.indirect_dma_start(sg[:, b, k, :], None, xup_dram.ap()[:, :],
                                                bass.IndirectOffsetOnAxis(ap=rb[:, b, k, R_SRC:R_SRC + 1].bitcast(I32), axis=0))\
                            .then_inc(s_sg[b][k], 16)

                    def dots(u, k):
                        p = part4[:, k % 2, :, :]
                        pool.wait_ge(s_part4, u * 4 + k + 1)
                        pool.tensor_tensor(p[:, 0, :], p[:, 0, :], p[:, 1, :], ALU.add).then_inc(s_dotp, 1)
                        pool.wait_ge(s_dotp, u * 4 + k + 1)
                        pool.wait_ge(s_msg, u * 4 + k + 5)
                        pool.tensor_tensor(dot[:, k, :], p[:, 0, :], p[:, 2, :], ALU.add).then_inc(s_dot, 1)

                    def low_h3(u, b):
                        pool.wait_ge(s_mc, u * 5 + 5)
                        pool.tensor_tensor(h3[:, b, :], hC[:, :], h3[:, b, :].bitcast(F32), ALU.subtract)\
                            .then_inc(s_h3, 1)

                    def finish(signal, value):
                        pool.wait_ge(signal, value)
                        pool.sem_inc(s_gate_pool, 1)

                    def unit(u, next_turn, b, more):
                        dots(u, 2)
                        if more:
                            finish(s_dot, u * 4 + 5)
                            gather(next_turn, 1 - b, 0)
                        dots(u, 3)
                        if more:
                            finish(s_dot, u * 4 + 6)
                            gather(next_turn, 1 - b, 1)
                            gather(next_turn, 1 - b, 2)
                            low_h3(u + 1, 1 - b)
                            dots(u + 1, 0)
                            finish(s_dot, u * 4 + 7)
                            gather(next_turn, 1 - b, 3)
                            dots(u + 1, 1)

                    pool.memset(lows[:, :], 1.0).then_inc(s_lows, 1)
                    pool.wait_ge(s_lows, 1)
                    pool.affine_select(out=lows[:, :], in_=lows[:, :], compare_op=ALU.is_ge, fill=0.0, base=-(EFR // 2),
                                       pattern=[[0, 1]], channel_multiplier=1).then_inc(s_lows, 1)
                    pool.wait_ge(s_lows, 2)
                    pool.wait_ge(s_wm, 16 * 7)
                    pool.tensor_scalar(wmA_t[:, :], wmA[:, :], lows[:, :], 1.0, ALU.mult, ALU.mult).then_inc(s_lows, 1)
                    pool.wait_ge(s_lows, 3)
                    pool.tensor_tensor(wmA_s[:, :], wmA[:, :], wmA_t[:, :].bitcast(F32), ALU.subtract).then_inc(s_lows, 1)
                    pool.memset(acc[:, :], 0.0).then_inc(s_lows, 1)
                    low_h3(0, 0)
                    finish(s_h3, 2)
                    pool.wait_ge(s_xup, 16 * NB)
                    for k in range(4):
                        gather(0, 0, k)
                    dots(0, 0)
                    dots(0, 1)
                    unit(0, 0, 0, True)
                    with pool.Fori(0, LOOPS - 1) as j:
                        unit(j * 2 + 1, j + 1, 1, True)
                        unit(j * 2 + 2, j + 1, 0, True)
                    unit(NU - 2, LOOPS, 1, True)
                    unit(NU - 1, 0, 0, False)
                    for k in range(4):
                        pool.wait_ge(s_sg[0][k], 16 * (LOOPS + 1))
                        pool.wait_ge(s_sg[1][k], 16 * LOOPS)

                def turn_features(pe):
                    for c in range(NB):
                        pe.wait_ge(s_x2, c + 1)
                        for m in range(4):
                            part = xs[:, c, 0:MUL] if m == 0 else xs[:, c, MUL + m - 1:D:3]
                            mm = pe.transpose(ps[m][:, c * P:(c + 1) * P], part, ident[:, :])
                    mm.then_inc(s_uT, 1)

                def up_features(pe):
                    pe.wait_ge(s_w2, 16 * 6)
                    pe.wait_ge(s_uTc, 4)
                    for c in range(NB):
                        for m in range(4):
                            mm = pe.matmul(ps[c][:, m * MUL:(m + 1) * MUL], uT[:, m, c * P:(c + 1) * P],
                                           wup[:, min(m, 1), :], start=True, stop=True)
                        mm.then_inc(s_up, 1)

                @block.tensor
                def _(pe):
                    def edge_mlp(u, turn, b, step):
                        if step == 0:
                            pe.wait_ge(s_ra[b], turn * 32 + 32)
                            if not isinstance(turn, int) or u > 0:
                                pe.wait_ge(s_mc, u * 5 - 1)
                            for k in range(4):
                                mm = pe.transpose(ps[6][0:EFR, k * P:(k + 1) * P],
                                                  ra[:, b, k, :, :].rearrange("p a k -> p (a k)"), ident[:, :])
                        else:
                            pe.wait_ge(s_mc, u * 5 + step)
                            pe.sem_inc(s_gate_pe, 1)
                            w, t = ((wmA_s[:, :], efT), (wmB[:, :], hA), (wmC[:, :, :].rearrange("p a c -> p (a c)"), hB))[step - 1]
                            mm = pe.matmul(ps[6 + step % 2][0:w.shape[1], :], w, t[:, :], start=True, stop=True)
                        mm.then_inc(s_m, 1)

                    def weights(u, b, k):
                        if k == 0:
                            pe.wait_ge(s_h3, u + 2)
                        pe.wait_ge(s_msg, u * 4 + k + 7)
                        for part in range(2):
                            mm = pe.matmul(ps[4 + k % 2][:, :], h3[:, b, k * P:(k + 1) * P], wm4_s[part][:, :],
                                           start=(part == 0), stop=(part == 1))
                        mm.then_inc(s_w, 1)

                    def scatter(u, b, k):
                        if k == 0:
                            pe.wait_ge(s_fl, u + 1)
                        pe.wait_ge(s_msg, u * 4 + k + 9)
                        pe.matmul(ps[2 * b][:, :], ohy[:, k % 2, 0, :], msg[:, k % 2, 0:4, :].rearrange("p a v -> p (a v)"),
                                  start=(k == 0), stop=(k == 3))
                        for m in range(4):
                            rows = oh[:, k % 2, :] if m == 0 else ohy[:, k % 2, m, :]
                            mm = pe.matmul(ps[2 * b + 1][:, m * MUL:(m + 1) * MUL], rows, msg[:, k % 2, 4 if m else 5, :],
                                           start=(k == 0 and m == 0), stop=(k == 3 and m == 3), skip_group_check=True)
                        mm.then_inc(s_sc, 1)

                    def unit(u, turn, b, more=True, more2=True):
                        for k in range(4):
                            if k < 3:
                                weights(u, b, k + 1)
                            elif more:
                                weights(u + 1, 1 - b, 0)
                            if k < 2 and more:
                                edge_mlp(u + 1, 0, 1 - b, k + 2)
                            if k >= 2 and more2:
                                edge_mlp(u + 2, turn + 1, b, k - 2)
                            scatter(u, b, k)

                    pe.wait_ge(s_wm, 16 * 7)
                    pe.wait_ge(s_lows, 4)
                    edge_mlp(0, 0, 0, 0)
                    edge_mlp(0, 0, 0, 1)
                    turn_features(pe)
                    edge_mlp(0, 0, 0, 2)
                    up_features(pe)
                    edge_mlp(0, 0, 0, 3)
                    pe.wait_ge(s_w4, 1)
                    edge_mlp(1, 0, 1, 0)
                    edge_mlp(1, 0, 1, 1)
                    weights(0, 0, 0)
                    pe.wait_ge(s_upc, 2)
                    pe.wait_ge(s_upd, 2)
                    unit(0, 0, 0)
                    with pe.Fori(0, LOOPS - 1) as j:
                        unit(j * 2 + 1, j, 1)
                        unit(j * 2 + 2, j + 1, 0)
                    unit(NU - 2, 0, 1, more2=False)
                    unit(NU - 1, 0, 0, more=False, more2=False)
                    pe.wait_ge(s_fl, NU + 2)
                    for m in range(8):
                        if m >= 2:
                            pe.wait_ge(s_mT2c, m - 1)
                        for g in range(NB):
                            col = (g * 8 + m) * MUL
                            mm = pe.transpose(ps[4 + m % 2][:, g * P:(g + 1) * P], acc[:, col:col + MUL], ident[:, :])
                        mm.then_inc(s_mT2, 1)
                    pe.wait_ge(s_mT2c, 8)
                    for c in range(NB):
                        if c >= 2:
                            pe.wait_ge(s_o2c, c - 1)
                        for m in range(4):
                            a, b = (3, 4) if m == 0 else (4 + m, m - 1)
                            for half, blk in enumerate((a, b)):
                                mm = pe.matmul(ps[c % 2][:, m * MUL:(m + 1) * MUL], mT[:, blk, c * P:(c + 1) * P],
                                               wout[:, min(m, 1), half, :], start=(half == 0), stop=(half == 1))
                        mm.then_inc(s_o2, 1)

                @block.scalar
                def _(act):
                    act.sem_inc(s_msg, 8)
                    act.sem_inc(s_sc, 2)
                    act.sem_inc(s_fl, 2)
                    act.sem_inc(s_h3, 1)
                    act.sem_inc(s_dot, 2)
                    def edge_mlp(u, b, step):
                        act.wait_ge(s_m, u * 4 + step + 1)
                        src_ps = ps[6 + step % 2]
                        if step == 0:
                            act.activation(efT[:, :], src_ps[0:EFR, :], ACT.Copy).then_inc(s_mc, 1)
                        elif step < 3:
                            act.activation((hA, hB)[step - 1][:, :], src_ps[0:HID, :], ACT.Silu,
                                           scale=(8 ** -0.5, SILU_2MOM * HID ** -0.5)[step - 1]).then_inc(s_mc, 1)
                        else:
                            act.wait_ge(s_h3, u + 1)
                            act.activation(hC[:, :], src_ps[:, :], ACT.Silu, scale=SILU_2MOM * HID ** -0.5).then_inc(s_mc, 1)
                            act.wait_ge(s_mc, u * 5 + 4)
                            act.activation(h3[:, b, :], hC[:, :], ACT.Copy, scale=upper[:, :]).then_inc(s_mc, 1)

                    def products(u, turn, b, k):
                        act.wait_ge(s_rl[b], turn * 16 + 16)
                        act.wait_ge(s_sg[b][k], turn * 16 + 16)
                        act.wait_ge(s_dot, u * 4 + k + 1)
                        for m in range(3):
                            ins = act.activation(part4[:, k % 2, m, :], sg[:, b, k, (1 + m) * MUL:(2 + m) * MUL], ACT.Copy,
                                                 scale=rb[:, b, k, R_Y + 1 + m:R_Y + 2 + m])
                        ins.then_inc(s_part4, 1)

                    def unit(u, turn, next_turn, b, more=True, more2=True):
                        for k in range(4):
                            if k < 2:
                                products(u, turn, b, k + 2)
                                if more:
                                    edge_mlp(u + 1, 1 - b, k + 2)
                            elif more:
                                products(u + 1, next_turn, 1 - b, k - 2)
                                if more2:
                                    edge_mlp(u + 2, b, k - 2)

                    root(act, s_ln1a, s_ln1ar)
                    act.wait_ge(s_upper, 2)
                    edge_mlp(0, 0, 0)
                    root(act, s_ln1b, s_ln1br)
                    edge_mlp(0, 0, 1)
                    act.wait_ge(s_uT, 1)
                    for m in (0, 1):
                        act.activation(uT[:, m, :], ps[m][:, :], ACT.Copy).then_inc(s_uTc, 1)
                    edge_mlp(0, 0, 2)
                    for c in (0, 2):
                        act.wait_ge(s_up, c + 1)
                        act.activation(xup[:, c, :], ps[c][:, :], ACT.Copy, scale=MUL ** -0.5).then_inc(s_upc, 1)
                    edge_mlp(0, 0, 3)
                    edge_mlp(1, 1, 0)
                    edge_mlp(1, 1, 1)
                    products(0, 0, 0, 0)
                    products(0, 0, 0, 1)
                    unit(0, 0, 0, 0)
                    with act.Fori(0, LOOPS - 1) as j:
                        unit(j * 2 + 1, j, j + 1, 1)
                        unit(j * 2 + 2, j + 1, j + 1, 0)
                    unit(NU - 2, LOOPS - 1, LOOPS, 1, more2=False)
                    unit(NU - 1, LOOPS, 0, 0, more=False, more2=False)
                    for m in range(8):
                        act.wait_ge(s_mT2, m + 1)
                        act.activation(mT[:, m, :], ps[4 + m % 2][:, :], ACT.Copy).then_inc(s_mT2c, 1)
                    root(act, s_ln2, s_ln2r)

                @block.vector
                def _(dve):
                    dve.memset(upper[0:HID, :], 0.0).then_inc(s_upper, 1)
                    dve.memset(upper[HID:P, :], 1.0).then_inc(s_upper, 1)
                    h1 = uT
                    s = Steps(dve, s_h1v, 1, NB)
                    variances(dve, s, s_ln1a)
                    for c in range(NB):
                        s.mark(dve.scalar_tensor_tensor(h1[:, c, :], ps[c][:, :], ln_mv[:, c, 0:1], gamma_b[:, :],
                                                        ALU.subtract, ALU.mult))
                    dve.wait_ge(s_ln1ar, 1)
                    s.link(dve.reciprocal(ln_r[:, :], ln_std[:, :]))
                    dve.wait_ge(s_xbeta, 1)
                    for c in range(NB):
                        s.mark(dve.scalar_tensor_tensor(h1[:, c, :], h1[:, c, :], ln_r[:, c:c + 1], xs[:, c, :],
                                                        ALU.mult, ALU.add))
                    for c in range(NB):
                        if c == 0:
                            s.wait()
                        sums(dve, s, h1[:, c, :], c)
                    layernorm(dve, s, s_ln1b, s_ln1br, h1, xs, s_x2)
                    s = Steps(dve, s_d2)
                    dve.wait_ge(s_w2, 16 * 6)
                    c4 = SILU_2MOM * HID ** -0.5
                    s.mark(dve.tensor_scalar(wm4_sb[:, 0:3 * MUL], wm4_sb[:, 0:3 * MUL], c4, None, ALU.mult))
                    s.link(dve.tensor_scalar(wm4_sb[:, 3 * MUL:], wm4_sb[:, 3 * MUL:], c4 * 3.0 ** -0.5, None, ALU.mult))
                    s.link(dve.tensor_copy(wm4_s[0][:, :], wm4_sb[:, :]))
                    dve.tensor_tensor(wm4_s[1][:, :], wm4_sb[:, :], wm4_s[0][:, :].bitcast(F32), ALU.subtract).then_inc(s_w4, 1)
                    dve.wait_ge(s_uT, 1)
                    for m in (2, 3):
                        dve.tensor_copy(uT[:, m, :], ps[m][:, :]).then_inc(s_uTc, 1)
                    for c in (1, 3):
                        dve.wait_ge(s_up, c + 1)
                        dve.tensor_scalar(xup[:, c, :], ps[c][:, :], MUL ** -0.5, None, ALU.mult).then_inc(s_upd, 1)
                    dve.wait_ge(s_lows, 5)

                    def messages(u, turn, b, k):
                        feat, w, out_ = sg[:, b, k, :], ps[4 + k % 2], msg[:, k % 2, :, :]
                        if k == 0:
                            dve.wait_ge(s_rl[b], turn * 16 + 16)
                        dve.wait_ge(s_sc, u * 4 + k + 1)
                        dve.tensor_scalar(oh[:, k % 2, :], iota[:, 0:P], rb[:, b, k, R_DST:R_DST + 1], None, ALU.is_equal).then_inc(s_rows2, 1)
                        dve.wait_ge(s_sg[b][k], turn * 16 + 16)
                        dve.wait_ge(s_w, u * 4 + k + 1)
                        dve.tensor_tensor(out_[:, 0:3, :], w[:, None, 2 * MUL:3 * MUL].to_broadcast([P, 3, MUL]),
                                          feat[:, MUL:].rearrange("p (m v) -> p m v", m=3), ALU.mult)
                        dve.tensor_tensor(out_[:, 3:5, :], w[:, 0:2 * MUL].rearrange("p (a v) -> p a v", a=2),
                                          feat[:, None, 0:MUL].to_broadcast([P, 2, MUL]), ALU.mult)
                        dve.wait_ge(s_rows2, u * 4 + k + 1)
                        dve.tensor_tensor(ohy[:, k % 2, :, :], oh[:, k % 2, None, :].to_broadcast([P, 4, P]),
                                          rb[:, b, k, R_Y:R_SRC, None].to_broadcast([P, 4, P]), ALU.mult)
                        dve.wait_ge(s_dot, u * 4 + k + 3)
                        dve.tensor_tensor(out_[:, 5, :], w[:, 3 * MUL:4 * MUL], dot[:, k, :], ALU.mult).then_inc(s_msg, 1)

                    def flush(u, b):
                        base = dve.value_load(ubase[0:1, bass.ds(u, 1)], min_val=0, max_val=(NB - 1) * 8 * MUL)
                        dve.wait_ge(s_sc, u * 4 + 4 + 2)
                        for half in range(2):
                            t = acc[:, bass.ds(base + half * 512, 512)]
                            ins = dve.tensor_tensor(t, ps[2 * b + half][:, :], t, ALU.add)
                        ins.then_inc(s_fl, 1)

                    for k in range(4):
                        messages(0, 0, 0, k)
                    with dve.Fori(0, LOOPS) as j:
                        for b, u, turn in ((1, j * 2 + 1, j), (0, j * 2 + 2, j + 1)):
                            for k in range(4):
                                messages(u, turn, b, k)
                                if k == 0:
                                    flush(u - 1, 1 - b)
                    flush(NU - 1, 0)
                    for c in range(NB):
                        dve.wait_ge(s_o2, c + 1)
                        sc2 = 1.0 / (16.0 * 10.0)
                        s.mark(dve.scalar_tensor_tensor(y2[:, c, 0:MUL], ps[c % 2][:, 0:MUL], sc2, xs[:, c, 0:MUL], ALU.mult, ALU.add))
                        dve.scalar_tensor_tensor(y2[:, c, MUL:].rearrange("p (v m) -> p m v", m=3),
                                                 ps[c % 2][:, MUL:].rearrange("p (m v) -> p m v", m=3), sc2,
                                                 xs[:, c, MUL:].rearrange("p (v m) -> p m v", m=3),
                                                 ALU.mult, ALU.add).then_inc(s_o2c, 1)
                        s.wait()
                        dve.wait_ge(s_o2c, c + 1)
                        sums(dve, s, y2[:, c, :], c)
                    layernorm(dve, s, s_ln2, s_ln2r, y2, xs, s_x3in)
                    dve.wait_ge(s_x3in, NB)

        with ExitStack() as c3:
            def t3(name, shape, dt=F32):
                return sb(name, shape, dt, c3)

            K3 = W3 // P
            FB = F3 // P
            att_b = t3("att_b", [P, 2, 2, H3, F3])
            b3T = t3("b3T", [P, 2, K3])
            hs3 = t3("hs3", [P, NB, W3])
            o3T = [t3("o3T0", [P, K3, N]), w31_sb[:, :, :].rearrange("p k (a n) -> p (k a) n", n=N)]
            sd3 = t3("sd3", [P, 2, NB, H3])
            diag3 = t3("diag3", [P, NB, P])
            ts3, l3, lm3, e3, pc3 = (t3(n, [P, 2, N]) for n in ("ts3", "l3", "lm3", "e3", "pc3"))
            pn3 = t3("pn3", [P, NB, N])
            junk3 = t3("junk3", [P, 4, F3])
            pT3 = t3("pT3", [P, 2, NB, P])
            mx3, nm3, dn3, ri3 = (t3(n, [P, 4]) for n in ("mx3", "nm3", "dn3", "ri3"))
            y3 = hs3[:, :, 0:D]
            s_att3, s_b3p, s_b3T, s_loops, s_y3, s_out = (sem(n) for n in ("s_att3", "s_b3p", "s_b3T", "s_loops", "s_y3", "s_out"))
            s_ln3, s_ln3r, s_x3, s_x3c, s_v3 = (sem(n) for n in ("s_ln3", "s_ln3r", "s_x3", "s_x3c", "s_v3"))
            q = {n: sem(f"s3_{n}") for n in ("hp", "hc", "dg", "bc", "t", "l", "e", "nm", "c", "n", "p", "pc", "g", "oc",
                                             "v", "m", "d")}
            NH = 2 * NB

            def conv_tensor(pe, j, w_sb, kc, in_T):
                def lay_out(t):
                    pe.wait_ge(q["t"], t * 4 + 4)
                    pe.wait_ge(q["dg"], t + 1)
                    pe.matmul(ps[2][:, :], ones[:, :], diag3[:, :, :].rearrange("p c n -> p (c n)"),
                              start=True, stop=True).then_inc(q["bc"], 1)

                for half in range(2):
                    for c in range(NB):
                        n = NB * half + c
                        if n >= 2 or j:
                            pe.wait_ge(q["hc"], j * NH + n - 1)
                        for k in range(kc):
                            mm = pe.matmul(ps[n % 2][:, :], in_T[:, k, c * P:(c + 1) * P],
                                           w_sb[:, k, half * 512:(half + 1) * 512], start=(k == 0), stop=(k == kc - 1))
                        mm.then_inc(q["hp"], 1)
                        if n == NB:
                            lay_out(j * H3)

                def broadcast(t, c):
                    if c == 0 and t != j * H3:
                        lay_out(t)

                def turn(t, c):
                    pe.wait_ge(q["n"], t * 4 + c + 3)
                    pe.wait_ge(q["pc"], t * 4 + c + 1)
                    for g in range(NB):
                        mm = pe.transpose(ps[4 + c % 2][:, g * P:(g + 1) * P], pn3[:, c, g * P:(g + 1) * P], ident[:, :])
                    mm.then_inc(q["p"], 1)

                def gather(t, c):
                    pe.wait_ge(q["pc"], t * 4 + c + 3)
                    pe.wait_ge(q["oc"], t * 4 + c + 1)
                    for f in range(FB):
                        col = (t - j * H3) * F3 + f * P
                        for g in range(NB):
                            mm = pe.matmul(ps[6 + c % 2][:, f * P:(f + 1) * P], hs3[:, g, col:col + P], pT3[:, c % 2, g, :],
                                           start=(g == 0), stop=(g == NB - 1))
                    mm.then_inc(q["g"], 1)

                for i in range(H3):
                    pipelined(j * H3 + i, ((gather, 3), (turn, 1), (broadcast, -3)), first=(i == 0), last=(i == H3 - 1))

            def pipelined(t, steps, first=False, last=False, before=None):
                lead = min(lag for _, lag in steps) if first else 0
                tail = max(lag for _, lag in steps) if last else 0
                for n in range(min(lead, 0), NB + max(tail, 0)):
                    if before and n in before:
                        before[n]()
                    for step, lag in steps:
                        m = n - lag
                        if not (first and m < 0) and not (last and m >= NB):
                            step(t + m // NB, m % NB)

            def heads(eng, j, steps, before=None):
                pipelined(j * H3, steps, first=True, before=before)
                with eng.Fori(j * H3 + 1, (j + 1) * H3 - 1) as t:
                    pipelined(t, steps)
                pipelined((j + 1) * H3 - 1, steps, last=True)

            def conv_scalar(act, j, out_T):
                def features(n):
                    half, c = divmod(n, NB)
                    act.wait_ge(q["hp"], j * NH + n + 1)
                    act.activation(hs3[:, c, half * 512:(half + 1) * 512], ps[n % 2][:, :], ACT.Copy).then_inc(q["hc"], 1)

                for n in range(NB):
                    features(n)

                def plus(t, c):
                    act.wait_ge(q["bc"], t + 1)
                    act.wait_ge(q["l"], t * 4 + c + 1)
                    act.activation(ts3[:, c % 2, :], ps[2][:, :], ACT.Identity, bias=sd3[:, 1, c, bass.ds(t - j * H3, 1)])\
                        .then_inc(q["t"], 1)

                def exp(t, c):
                    act.wait_ge(q["nm"], t * 4 + c + 1)
                    act.wait_ge(q["c"], t * 4 + c + 1)
                    act.activation(e3[:, c % 2, :], lm3[:, c % 2, :], ACT.Exp, bias=nm3[:, c:c + 1]).then_inc(q["e"], 1)

                def turned(t, c):
                    act.wait_ge(q["p"], t * 4 + c + 5)
                    act.wait_ge(q["g"], t * 4 + c + 1)
                    act.activation(pT3[:, c % 2, :, :], psum4(4 + c % 2), ACT.Copy).then_inc(q["pc"], 1)

                def output(t, c):
                    act.wait_ge(q["g"], t * 4 + c + 3)
                    for f in range(FB):
                        row = (t - j * H3) * FB + f
                        ins = act.activation(out_T[:, bass.ds(row, 1), c * P:(c + 1) * P].rearrange("p a n -> p (a n)"),
                                             ps[6 + c % 2][:, f * P:(f + 1) * P], ACT.Relu, bias=b3T[:, j, bass.ds(row, 1)])
                    ins.then_inc(q["oc"], 1)

                heads(act, j, ((exp, 0), (turned, 2), (output, 4), (plus, -2)),
                      before={-2: lambda: features(4), 0: lambda: features(5), 1: lambda: features(6),
                              2: lambda: features(7)})

            def conv_pool(pool, j):
                def normalize(t, c):
                    pool.wait_ge(q["c"], t * 4 + c + 3)
                    pool.wait_ge(q["p"], t * 4 + c + 1)
                    pool.sem_inc(s_gate_pool, 1)
                    pool.tensor_scalar(pn3[:, c, :], pc3[:, c % 2, :], ri3[:, c:c + 1], 1.0, ALU.mult, ALU.mult)\
                        .then_inc(q["n"], 1)

                heads(pool, j, ((normalize, 0),))

            def conv_vector(dve, j):
                s = Steps(dve, q["v"], j, NB * 2 * H3)

                def node_scores(half, c):
                    dve.wait_ge(q["hc"], j * NH + half * NB + c + 1)
                    if half or c:
                        s.wait()
                    for i in range(4):
                        h, e = half * 2 + i // 2, i % 2
                        s.mark(dve.tensor_tensor_reduce(junk3[:, i, :], hs3[:, c, h * F3:(h + 1) * F3], att_b[:, j, e, h, :],
                                                        1.0, 0.0, ALU.mult, ALU.add, sd3[:, e, c, h:h + 1]))

                for c in range(NB):
                    node_scores(0, c)
                s.wait()

                def diagonal(t, c):
                    if c == 0:
                        dve.wait_ge(q["t"], t * 4 + 1)
                        dve.tensor_tensor(diag3[:, :, :], ident[:, None, :].to_broadcast([P, NB, P]),
                                          sd3[:, 0, :, bass.ds(t - j * H3, 1)].to_broadcast([P, NB, P]), ALU.mult)\
                            .then_inc(q["dg"], 1)

                def leaky(t, c):
                    dve.wait_ge(q["t"], t * 4 + c + 5)
                    dve.scalar_tensor_tensor(l3[:, c % 2, :], ts3[:, c % 2, :], 0.2, ts3[:, c % 2, :],
                                             ALU.mult, ALU.max).then_inc(q["l"], 1)

                def masked(t, c):
                    dve.wait_ge(q["e"], t * 4 + c + 1)
                    dve.wait_ge(q["l"], t * 4 + c + 3)
                    dve.sem_inc(s_gate_dve, 1)
                    dve.tensor_tensor_reduce(lm3[:, c % 2, :], l3[:, c % 2, :], nomask[:, c, :], 1.0, -3.0e38,
                                             ALU.add, ALU.max, mx3[:, c:c + 1]).then_inc(q["m"], 1)

                def negated(t, c):
                    dve.wait_ge(q["m"], t * 4 + c + 1)
                    dve.tensor_scalar(nm3[:, c:c + 1], mx3[:, c:c + 1], -1.0, None, ALU.mult).then_inc(q["nm"], 1)

                def weigh(t, c):
                    dve.wait_ge(q["e"], t * 4 + c + 3)
                    dve.wait_ge(q["n"], t * 4 + c + 1)
                    dve.sem_inc(s_gate_dve, 1)
                    dve.tensor_tensor_reduce(pc3[:, c % 2, :], e3[:, c % 2, :], count[:, c, :], 1.0, 1.0e-16,
                                             ALU.mult, ALU.add, dn3[:, c:c + 1]).then_inc(q["d"], 1)

                def inverted(t, c):
                    dve.wait_ge(q["d"], t * 4 + c + 1)
                    dve.reciprocal(ri3[:, c:c + 1], dn3[:, c:c + 1]).then_inc(q["c"], 1)

                heads(dve, j, ((leaky, -1), (weigh, 1), (masked, -1), (inverted, 1), (negated, -1), (diagonal, -4)),
                      before={c: (lambda c=c: node_scores(1, c)) for c in range(NB)})
                s.wait()

            with nc.Block() as block:
                @block.sync
                def _(sp):
                    for j, (a, b) in enumerate(((asrc1, adst1), (asrc2, adst2))):
                        sp.dma_start(att_b[:, j, 0, :, :], a.partition_broadcast(P)).then_inc(s_att3, 16)
                        sp.dma_start(att_b[:, j, 1, :, :], b.partition_broadcast(P)).then_inc(s_att3, 16)
                    for c in range(NB):
                        sp.wait_ge(s_x3c, c + 1)
                        sp.dma_start(out[c * P:(c + 1) * P, :], xs[:, c, :]).then_inc(s_out, 16)
                    sp.wait_ge(s_out, 16 * NB)

                @block.gpsimd
                def _(pool):
                    pool.sem_inc(q["n"], 2)
                    for j in range(2):
                        conv_pool(pool, j)

                @block.tensor
                def _(pe):
                    for k in range(KB):
                        if k >= 2:
                            pe.wait_ge(s_x3, k - 1)
                        for c in range(NB):
                            mm = pe.transpose(ps[k % 2][:, c * P:(c + 1) * P], xs[:, c, k * P:(k + 1) * P], ident[:, :])
                        mm.then_inc(s_loops, 1)
                    pe.wait_ge(s_b3, 48)
                    for j in range(2):
                        mm = pe.transpose(ps[3][:, j * K3:(j + 1) * K3], b3row[:, j, :], ident[0:K3, 0:K3])
                    mm.then_inc(s_b3p, 1)
                    pe.wait_ge(s_x3, KB)
                    for w, blocks in zip(s_w3, (KB, K3, K3)):
                        pe.wait_ge(w, 16 * blocks)
                    conv_tensor(pe, 0, w31_sb, KB, xT)
                    pe.wait_ge(q["oc"], NB * H3 + 2)
                    conv_tensor(pe, 1, w32_sb, K3, o3T[0])
                    pe.wait_ge(q["oc"], 2 * NB * H3 + 2)
                    for c in range(NB):
                        for k in range(K3):
                            mm = pe.matmul(ps[c][:, :], o3T[1][:, k, c * P:(c + 1) * P], fcw_sb[:, k, :],
                                           start=(k == 0), stop=(k == K3 - 1))
                        mm.then_inc(s_y3, 1)

                @block.scalar
                def _(act):
                    for k in range(KB):
                        act.wait_ge(s_loops, k + 1)
                        act.activation(xT[:, k, :], ps[k % 2][:, :], ACT.Copy).then_inc(s_x3, 1)
                    act.wait_ge(s_b3p, 1)
                    act.activation(b3T[:, :, :].rearrange("p a b -> p (a b)"), ps[3][:, 0:2 * K3], ACT.Copy).then_inc(s_b3T, 1)
                    act.wait_ge(s_b3T, 1)
                    act.sem_inc(q["t"], 4)
                    act.sem_inc(q["pc"], 2)
                    act.sem_inc(q["oc"], 2)
                    act.sem_inc(q["e"], 2)
                    conv_scalar(act, 0, o3T[0])
                    conv_scalar(act, 1, o3T[1])
                    for c in range(NB):
                        act.wait_ge(s_ln3, c + 1)
                        act.activation(ln_std[:, c:c + 1], ln_std[:, c:c + 1], ACT.Sqrt).then_inc(s_ln3r, 1)

                @block.vector
                def _(dve):
                    s = Steps(dve, s_v3)
                    for c in range(NB):
                        d = count[:, c, c * P:(c + 1) * P]
                        s.mark(dve.tensor_tensor(d, d, ident[:, :], ALU.add))
                    s.wait()
                    for c in range(NB):
                        s.mark(dve.tensor_scalar(nomask[:, c, :], count[:, c, :], 0.0, NEG, ALU.is_equal, ALU.mult))
                    s.wait()
                    dve.wait_ge(s_att3, 64)
                    dve.sem_inc(q["l"], 2)
                    dve.sem_inc(q["c"], 2)
                    dve.sem_inc(q["p"], 4)
                    dve.sem_inc(q["g"], 2)
                    conv_vector(dve, 0)
                    conv_vector(dve, 1)
                    dve.wait_ge(s_b3, 48)
                    for c in range(NB):
                        s.mark(dve.tensor_tensor(xs[:, c, :], xs[:, c, :], fcb_b[:, :], ALU.add))
                    s.wait()
                    for c in range(NB):
                        dve.wait_ge(s_y3, c + 1)
                        s.link(dve.tensor_tensor(y3[:, c, :], ps[c][:, :], xs[:, c, :], ALU.add))
                        s.link(dve.bn_stats(ln_stat[:, c, :], y3[:, c, :]))
                        s.link(dve.bn_aggr(ln_mv[:, c, :], ln_stat[:, c, :]))
                        dve.tensor_scalar(ln_std[:, c:c + 1], ln_mv[:, c, 1:2], EPS, None, ALU.add).then_inc(s_ln3, 1)
                        dve.wait_ge(s_ln3r, c + 1)
                        s.link(dve.reciprocal(ln_r[:, c:c + 1], ln_std[:, c:c + 1]))
                        dve.tensor_scalar(xs[:, c, :], y3[:, c, :], ln_mv[:, c, 0:1], ln_r[:, c:c + 1],
                                          ALU.subtract, ALU.mult).then_inc(s_x3c, 1)
        lay3.close()
    return nc


_INS = ['x', 'src', 'dst', 'edge_attr_4', 'edge_attr_8', 'L0_gnn_W', 'L0_gnn_a', 'L1_gnn_Wq', 'L1_gnn_bq', 'L1_gnn_Wk',
        'L1_gnn_bk', 'L1_gnn_Wv', 'L1_gnn_bv', 'L1_gnn_Wskip', 'L1_gnn_bskip', 'L1_gnn_Wlin', 'L1_gnn_blin',
        'L1_gnn_gamma', 'L1_gnn_beta', 'L2_gnn_W_up0', 'L2_gnn_W_up1', 'L2_gnn_W_mlp1', 'L2_gnn_W_mlp2',
        'L2_gnn_W_mlp3', 'L2_gnn_W_mlp4', 'L2_gnn_W_out0', 'L2_gnn_W_out1', 'L3_gnn_W1', 'L3_gnn_att_src1',
        'L3_gnn_att_dst1', 'L3_gnn_b1', 'L3_gnn_W2', 'L3_gnn_att_src2', 'L3_gnn_att_dst2', 'L3_gnn_b2', 'L3_gnn_fcW',
        'L3_gnn_fcb']


def kernel(**inputs):
    import numpy as _np
    import concourse.bacc as _bacc
    from concourse import mybir as _mybir
    from concourse.bass_utils import run_bass_kernel_spmd as _run

    nc = _bacc.Bacc("TRN2", target_bir_lowering=False, num_devices=1)
    arrays, args = {}, []
    for name in _INS:
        a = _np.ascontiguousarray(inputs[name])
        arrays[f"in_{name}_dram"] = a
        args.append(nc.dram_tensor(f"in_{name}_dram", a.shape, _mybir.dt.from_np(a.dtype), kind="ExternalInput").ap())
    args.append(nc.dram_tensor("out_0_dram", (N, D), F32, kind="ExternalOutput").ap())
    graph_kernel(nc, *args)
    r = _run(nc, [arrays], core_ids=[0])
    return r.results[0]["out_0_dram"]
```
